# Optimizing a Trainium2 kernel written in Bass

```python
import numpy as np
import jax
import jax.numpy as jnp

def _softmax(x, axis=-1):
    return jax.nn.softmax(x, axis=axis)

def _gelu(x):
    return jax.nn.gelu(x, approximate=True)

def _silu(x):
    return jax.nn.silu(x)

def _sigmoid(x):
    return jax.nn.sigmoid(x)

def _layernorm(x, axis=-1, eps=1e-05):
    m = jnp.mean(x, axis=axis, keepdims=True)
    v = jnp.var(x, axis=axis, keepdims=True)
    return (x - m) / jnp.sqrt(v + eps)

def _scatter_add(tgt, idx, src, axis=0):
    return tgt.at[idx].add(src)

def _segment_sum(src, seg, n):
    return jax.ops.segment_sum(src, seg, n)
kernel_name = 'mk_gnn_resnorm_d4_gnn_r32_740c87'

def setup_inputs(seed: int=0):
    np.random.seed(seed)
    _w = jnp.asarray

    def _rec_inputs():
        import jax
        import jax.numpy as jnp
        _gk = jax.random.key(seed)
        x = -0.0002117 + 1 * jax.random.normal(jax.random.fold_in(_gk, 1), (3125, 256), jnp.float32)
        _s = jax.random.randint(jax.random.fold_in(_gk, 2), (25000,), 0, 3125, jnp.int32)
        _d = jax.random.randint(jax.random.fold_in(_gk, 3), (25000,), 0, 3125, jnp.int32)
        _loop = jnp.arange(3125, dtype=jnp.int32)
        src = jnp.concatenate([_s, _d, _loop])
        dst = jnp.concatenate([_d, _s, _loop])
        _o = jnp.argsort(dst, stable=True)
        src = src[_o]
        dst = dst[_o]
        edge_weight = jax.random.uniform(jax.random.fold_in(_gk, 13), (53125,), jnp.float32, 0.0, 1)
        return (x, src, dst, edge_weight)
    x, src, dst, edge_weight = _rec_inputs()

    def _L0_gnn_setup():
        import jax, jax.numpy as jnp
        import numpy as np
        N_NODES = 3125

        def sage_conv(x, edge_index, Wl, bl, Wr):
            src, dst = (edge_index[0], edge_index[1])
            msg = x[src]
            agg = jax.ops.segment_sum(msg, dst, num_segments=N_NODES)
            cnt = jax.ops.segment_sum(jnp.ones((edge_index.shape[1],), x.dtype), dst, num_segments=N_NODES)
            agg = agg / jnp.maximum(cnt, 1.0)[:, None]
            return agg @ Wl.T + bl + x @ Wr.T
        key = jax.random.key(seed)
        ks = jax.random.split(key, 8)
        d_in, d_hid, d_out, E = (256, 512, 256, 10000)
        s = lambda k, shape, fan: jax.random.normal(k, shape, jnp.float32) * (1.0 / np.sqrt(fan))
        return {'x': jax.random.normal(ks[0], (N_NODES, d_in), jnp.float32), 'edge_index': jax.random.randint(ks[1], (2, E), 0, N_NODES, dtype=jnp.int64), 'W1l': s(ks[2], (d_hid, d_in), d_in), 'b1l': jnp.zeros((d_hid,), jnp.float32), 'W1r': s(ks[3], (d_hid, d_in), d_in), 'W2l': s(ks[4], (d_out, d_hid), d_hid), 'b2l': jnp.zeros((d_out,), jnp.float32), 'W2r': s(ks[5], (d_out, d_hid), d_hid)}
    _L0_gnn_all = _L0_gnn_setup()
    _L0_gnn_in = {k: v for k, v in _L0_gnn_all.items() if k in ('W1l', 'b1l', 'W1r', 'W2l', 'b2l', 'W2r')}
    del _L0_gnn_all

    def _L1_gnn_setup():
        import jax, jax.numpy as jnp
        import numpy as np
        N_NODES = 3125
        NNZ = 100000
        DIM = 256
        HOPS = 3
        key = jax.random.key(seed)
        ks = jax.random.split(key, 8)
        m = jax.random.normal(ks[0], (N_NODES, DIM), dtype=jnp.float32)
        vals = jax.random.uniform(ks[1], (NNZ,), dtype=jnp.float32)
        scale = 1.0 / np.sqrt(DIM)
        Wn = jax.random.normal(ks[2], (HOPS, DIM, DIM), dtype=jnp.float32) * scale
        bn = jax.random.normal(ks[3], (HOPS, DIM), dtype=jnp.float32) * 0.01
        Ws = jax.random.normal(ks[4], (HOPS, DIM, DIM), dtype=jnp.float32) * scale
        bs = jax.random.normal(ks[5], (HOPS, DIM), dtype=jnp.float32) * 0.01
        rows = jax.random.randint(ks[6], (NNZ,), 0, N_NODES, dtype=jnp.int64)
        cols = jax.random.randint(ks[7], (NNZ,), 0, N_NODES, dtype=jnp.int64)
        return {'m': m, 'vals': vals, 'Wn': Wn, 'bn': bn, 'Ws': Ws, 'bs': bs, 'rows': rows, 'cols': cols}
    _L1_gnn_all = _L1_gnn_setup()
    _L1_gnn_in = {k: v for k, v in _L1_gnn_all.items() if k in ('Wn', 'bn', 'Ws', 'bs')}
    del _L1_gnn_all

    def _L2_gnn_setup():
        import jax, jax.numpy as jnp
        import numpy as np
        N_NODES = 25000
        N_EDGES = 12500
        D = 256
        key = jax.random.key(seed)
        k1, k2, k3, k4, k5 = jax.random.split(key, 5)
        feat = jax.random.normal(k1, (N_NODES, D), dtype=jnp.float32)
        src = jax.random.randint(k2, (N_EDGES,), 0, N_NODES, dtype=jnp.int32)
        dst = jax.random.randint(k3, (N_EDGES,), 0, N_NODES, dtype=jnp.int32)
        a = float(np.sqrt(6.0 / (D + D)))
        W1 = jax.random.uniform(k4, (D, D), minval=-a, maxval=a, dtype=jnp.float32)
        W2 = jax.random.uniform(k5, (D, D), minval=-a, maxval=a, dtype=jnp.float32)
        b = jnp.zeros((D,), dtype=jnp.float32)
        return {'feat': feat, 'W1': W1, 'W2': W2, 'b': b, 'src': src, 'dst': dst}
    _L2_gnn_all = _L2_gnn_setup()
    _L2_gnn_in = {k: v for k, v in _L2_gnn_all.items() if k in ('W1', 'W2', 'b')}
    del _L2_gnn_all

    def _L3_gnn_setup():
        import jax, jax.numpy as jnp
        import numpy as np
        N, E = (50000, 25000)
        IN_DIM, HEADS, OUT_DIM = (256, 8, 32)
        NEG_SLOPE = 0.2
        LN_EPS = 1e-05
        key = jax.random.key(seed)
        ks = jax.random.split(key, 8)
        HC = HEADS * OUT_DIM
        x = jax.random.normal(ks[0], (N, IN_DIM), dtype=jnp.float32)
        edge_index = jax.random.randint(ks[1], (2, E), 0, N, dtype=jnp.int32)
        W = jax.random.normal(ks[2], (IN_DIM, HC), dtype=jnp.float32) / np.sqrt(IN_DIM)
        att_src = jax.random.normal(ks[3], (HEADS, OUT_DIM), dtype=jnp.float32) / np.sqrt(OUT_DIM)
        att_dst = jax.random.normal(ks[4], (HEADS, OUT_DIM), dtype=jnp.float32) / np.sqrt(OUT_DIM)
        bias = jnp.zeros((HC,), dtype=jnp.float32)
        ln_gamma = jnp.ones((HC,), dtype=jnp.float32)
        ln_beta = jnp.zeros((HC,), dtype=jnp.float32)
        return {'x': x, 'edge_index': edge_index, 'W': W, 'att_src': att_src, 'att_dst': att_dst, 'bias': bias, 'ln_gamma': ln_gamma, 'ln_beta': ln_beta}
    _L3_gnn_all = _L3_gnn_setup()
    _L3_gnn_in = {k: v for k, v in _L3_gnn_all.items() if k in ('W', 'att_src', 'att_dst', 'bias', 'ln_gamma', 'ln_beta')}
    del _L3_gnn_all
    return {'x': x, 'src': src, 'dst': dst, 'edge_weight': edge_weight, 'L0_gnn_W1l': _L0_gnn_in['W1l'], 'L0_gnn_b1l': _L0_gnn_in['b1l'], 'L0_gnn_W1r': _L0_gnn_in['W1r'], 'L0_gnn_W2l': _L0_gnn_in['W2l'], 'L0_gnn_b2l': _L0_gnn_in['b2l'], 'L0_gnn_W2r': _L0_gnn_in['W2r'], 'L1_gnn_Wn': _L1_gnn_in['Wn'], 'L1_gnn_bn': _L1_gnn_in['bn'], 'L1_gnn_Ws': _L1_gnn_in['Ws'], 'L1_gnn_bs': _L1_gnn_in['bs'], 'L2_gnn_W1': _L2_gnn_in['W1'], 'L2_gnn_W2': _L2_gnn_in['W2'], 'L2_gnn_b': _L2_gnn_in['b'], 'L3_gnn_W': _L3_gnn_in['W'], 'L3_gnn_att_src': _L3_gnn_in['att_src'], 'L3_gnn_att_dst': _L3_gnn_in['att_dst'], 'L3_gnn_bias': _L3_gnn_in['bias'], 'L3_gnn_ln_gamma': _L3_gnn_in['ln_gamma'], 'L3_gnn_ln_beta': _L3_gnn_in['ln_beta']}

def reference(x, src, dst, edge_weight, L0_gnn_W1l, L0_gnn_b1l, L0_gnn_W1r, L0_gnn_W2l, L0_gnn_b2l, L0_gnn_W2r, L1_gnn_Wn, L1_gnn_bn, L1_gnn_Ws, L1_gnn_bs, L2_gnn_W1, L2_gnn_W2, L2_gnn_b, L3_gnn_W, L3_gnn_att_src, L3_gnn_att_dst, L3_gnn_bias, L3_gnn_ln_gamma, L3_gnn_ln_beta):
    import jax
    import jax.numpy as jnp

    def _L0_gnn_ref(x, edge_index, W1l, b1l, W1r, W2l, b2l, W2r):
        import jax, jax.numpy as jnp
        import numpy as np
        N_NODES = 3125

        def sage_conv(x, edge_index, Wl, bl, Wr):
            src, dst = (edge_index[0], edge_index[1])
            msg = x[src]
            agg = jax.ops.segment_sum(msg, dst, num_segments=N_NODES)
            cnt = jax.ops.segment_sum(jnp.ones((edge_index.shape[1],), x.dtype), dst, num_segments=N_NODES)
            agg = agg / jnp.maximum(cnt, 1.0)[:, None]
            return agg @ Wl.T + bl + x @ Wr.T
        h = sage_conv(x, edge_index, W1l, b1l, W1r)
        h = jax.nn.relu(h)
        out = sage_conv(h, edge_index, W2l, b2l, W2r)
        return out

    def _L1_gnn_ref(m, vals, Wn, bn, Ws, bs, rows, cols):
        import jax, jax.numpy as jnp
        import numpy as np
        N_NODES = 3125
        NNZ = 100000
        DIM = 256
        HOPS = 3
        N = m.shape[0]
        hop_num = Wn.shape[0]
        H = m
        for i in range(hop_num):
            msg = H[cols] * vals[:, None]
            Hn = jax.ops.segment_sum(msg, rows, num_segments=N)
            Hn = Hn @ Wn[i].T + bn[i]
            Hs = H @ Ws[i].T + bs[i]
            H = Hn + Hs
            if i != hop_num - 1:
                H = jax.nn.elu(H)
        return H

    def _L2_gnn_ref(feat, W1, W2, b, src, dst):
        import jax, jax.numpy as jnp
        import numpy as np
        N_NODES = 25000
        N_EDGES = 12500
        D = 256
        n = feat.shape[0]
        ones = jnp.ones(src.shape[0], dtype=feat.dtype)
        out_deg = jnp.maximum(jax.ops.segment_sum(ones, src, num_segments=n), 1.0)
        in_cnt = jax.ops.segment_sum(ones, dst, num_segments=n)
        t1 = feat @ W1
        msg = t1[src] + feat[src] * feat[dst] @ W2
        scale = jnp.sqrt(out_deg[src]) * jnp.sqrt(out_deg[dst])
        msg = msg / scale[:, None]
        agg = jax.ops.segment_sum(msg, dst, num_segments=n)
        embed = jnp.where(in_cnt[:, None] > 0, t1 + agg, jnp.zeros_like(t1))
        embed = embed + b
        embed = jax.nn.leaky_relu(embed, negative_slope=0.01)
        norm = jnp.linalg.norm(embed, axis=1, keepdims=True)
        embed = embed / jnp.maximum(norm, 1e-12)
        return embed

    def _L3_gnn_ref(x, edge_index, W, att_src, att_dst, bias, ln_gamma, ln_beta):
        import jax, jax.numpy as jnp
        import numpy as np
        N, E = (50000, 25000)
        IN_DIM, HEADS, OUT_DIM = (256, 8, 32)
        NEG_SLOPE = 0.2
        LN_EPS = 1e-05
        n = x.shape[0]
        loop = jnp.arange(n, dtype=edge_index.dtype)
        src = jnp.concatenate([edge_index[0], loop])
        dst = jnp.concatenate([edge_index[1], loop])
        h = (x @ W).reshape(n, HEADS, OUT_DIM)
        a_src = jnp.einsum('nhc,hc->nh', h, att_src)
        a_dst = jnp.einsum('nhc,hc->nh', h, att_dst)
        e = jax.nn.leaky_relu(a_src[src] + a_dst[dst], NEG_SLOPE)
        m = jax.ops.segment_max(e, dst, num_segments=n)
        e = jnp.exp(e - m[dst])
        denom = jax.ops.segment_sum(e, dst, num_segments=n)
        alpha = e / (denom[dst] + 1e-16)
        out = jax.ops.segment_sum(h[src] * alpha[:, :, None], dst, num_segments=n)
        out = out.reshape(n, HEADS * OUT_DIM) + bias
        mu = jnp.mean(out, axis=-1, keepdims=True)
        var = jnp.mean(jnp.square(out - mu), axis=-1, keepdims=True)
        return ln_gamma * (out - mu) * jax.lax.rsqrt(var + LN_EPS) + ln_beta
    edge_index = jnp.stack([src, dst])
    x = _layernorm(x + _L0_gnn_ref(x, edge_index, L0_gnn_W1l, L0_gnn_b1l, L0_gnn_W1r, L0_gnn_W2l, L0_gnn_b2l, L0_gnn_W2r), axis=-1)
    x = _layernorm(x + _L1_gnn_ref(x, edge_weight, L1_gnn_Wn, L1_gnn_bn, L1_gnn_Ws, L1_gnn_bs, src, dst), axis=-1)
    x = _layernorm(x + _L2_gnn_ref(x, L2_gnn_W1, L2_gnn_W2, L2_gnn_b, src, dst), axis=-1)
    x = _layernorm(x + _L3_gnn_ref(x, edge_index, L3_gnn_W, L3_gnn_att_src, L3_gnn_att_dst, L3_gnn_bias, L3_gnn_ln_gamma, L3_gnn_ln_beta), axis=-1)
    return x

_drawn_inputs = setup_inputs


def setup_inputs(seed=0):
    import zlib

    import numpy as np

    out = dict(_drawn_inputs(seed))
    spreads = {'L0_gnn_b1l': (0.0, 0.1),
     'L0_gnn_b2l': (0.0, 0.1),
     'L2_gnn_b': (0.0, 2.0),
     'L3_gnn_bias': (0.0, 0.1),
     'L3_gnn_ln_gamma': (1.0, 0.2),
     'L3_gnn_ln_beta': (0.0, 0.1)}
    factors = {'L0_gnn_W1l': 2.672,
     'L1_gnn_bn': 41.855,
     'L1_gnn_bs': 30.834,
     'L3_gnn_att_src': 64.0,
     'L3_gnn_att_dst': 64.0}
    for name, (base, spread) in spreads.items():
        noise = np.random.default_rng([zlib.crc32(name.encode()), seed]).standard_normal(out[name].shape)
        drawn = base * np.exp(spread * noise) if base else spread * noise
        out[name] = jnp.asarray(drawn.astype(out[name].dtype))
    for name, factor in factors.items():
        out[name] = (out[name] * factor).astype(out[name].dtype)
    return out
```

```python
from contextlib import ExitStack

import numpy as np
import concourse.bass as bass
from concourse import mybir

F32 = mybir.dt.float32
BF16 = mybir.dt.bfloat16
I32 = mybir.dt.int32
ALU = mybir.AluOpType
ACT = mybir.ActivationFunctionType
AX_X = mybir.AxisListType.X

P = 128
NODES = 3125
EDGES = 53125
DIM = 256
HIDDEN = 512
HOPS = 3
HEADS = 8
HEAD_DIM = DIM // HEADS
HEAD_ROW = HEAD_DIM + 1
ATT_ROW = HEADS * HEAD_ROW
NODE_TILES = -(-NODES // P)
PADDED_NODES = NODE_TILES * P
LAST_ROWS = NODES - (NODE_TILES - 1) * P
WINDOWED_NODES = PADDED_NODES + P
EDGE_TILES = 416
PADDED_EDGES = EDGE_TILES * P
UNROLL = 8
TURNS = EDGE_TILES // UNROLL
LAG = 2
PSUM_RING = 4
SCAN_ROWS = P // HEADS
SCAN_TILES = EDGE_TILES // SCAN_ROWS
SCAN_LEN = SCAN_TILES * P
PAD_NODE = PADDED_NODES - 1
RECORD = 4
BIG = 1.0e30
LN_EPS = 1e-5
K_IN = DIM // P
K_HID = HIDDEN // P


class Program:

    ENGINES = ("pe", "dve", "act", "pool", "sp")

    def __init__(self, nc, stack):
        self.nc, self.stack = nc, stack
        self.queue = {e: [] for e in self.ENGINES}
        self.done = {e: stack.enter_context(nc.semaphore(f"done_{e}")) for e in self.ENGINES}
        self.count = {}

    def sem(self, name):
        return self.stack.enter_context(self.nc.semaphore(name))

    def op(self, e, fn, *waits, sem=None, by=1):
        sem = self.done[e] if sem is None else sem
        self.count[sem.name] = self.count.get(sem.name, 0) + by
        waits = [w for w in waits if w is not None]

        def emit(eng):
            for s, v in waits:
                eng.wait_ge(s, v)
            fn(eng).then_inc(sem, by)

        self.queue[e].append(emit)
        return sem, self.count[sem.name]

    def dma(self, e, sem, out, in_, *waits):
        return self.op(e, lambda eng: eng.dma_start(out, in_), *waits, sem=sem, by=16)

    def last(self, e):
        return self.done[e], self.count.get(self.done[e].name, 0)

    def run(self, block):
        names = dict(pe=block.tensor, dve=block.vector, act=block.scalar, pool=block.gpsimd, sp=block.sync)
        for e, deco in names.items():
            def body(eng, e=e):
                for emit in self.queue[e]:
                    emit(eng)
            deco(body)


def residual_gnn(nc, a, out):
    with ExitStack() as stack:
        pr = Program(nc, stack)

        def sb(name, shape, dt=F32):
            return stack.enter_context(nc.sbuf_tensor(name, shape, dt))

        x = sb("x_nodes", [P, NODE_TILES, DIM])
        xT = sb("x_features", [P, K_IN, PADDED_NODES])
        agg = sb("aggregate", [P, 3, WINDOWED_NODES])
        own = sb("own_term", [P, NODE_TILES, ATT_ROW])
        rows = sb("gathered_rows", [P, UNROLL, ATT_ROW])
        onehot = sb("edge_to_window", [P, UNROLL, P])
        src_lo_hot = sb("src_lo_onehot", [P, UNROLL, P], BF16)
        src_hi_hot = sb("src_hi_onehot", [P, UNROLL, 32], BF16)
        w_a = sb("weights_a", [P, 2048])
        w_b = sb("weights_b", [P, K_HID, 2 * DIM])
        w_c = sb("weights_c", [P, HOPS, 2, K_IN, DIM])
        hidden = sb("hidden", [P, 2 * K_HID * 512])
        tmp = sb("tmp", [P, 4, ATT_ROW])
        stage = tmp
        src = sb("src", [P, EDGE_TILES], I32)
        src_i = hidden[:, 0:EDGE_TILES].bitcast(I32)
        src_lo = sb("src_lo", [P, EDGE_TILES])
        src_hi = sb("src_hi", [P, EDGE_TILES])
        dst = sb("dst", [P, EDGE_TILES], I32)
        base = sb("window_base", [P, EDGE_TILES], I32)
        local = sb("dst_in_window", [P, EDGE_TILES])
        weight = sb("edge_weight", [P, EDGE_TILES])
        iota_i = hidden[:, EDGE_TILES:EDGE_TILES + P].bitcast(I32)
        iota = sb("iota", [P, P])
        part_i = sb("partition_i", [P, 1], I32)
        part = sb("partition", [P, 1])
        ident = sb("identity", [P, P])
        ones = sb("ones", [P, P])
        zeros_b = sb("zeros_bf16", [P, P], BF16)
        b1 = sb("bias_hidden", [P, K_HID])
        brow = sb("bias_rows", [P, 8, DIM])
        B_HID2, B_HOP, B_L2, B_ATT, B_GAMMA, B_BETA = 0, 1, 4, 5, 6, 7
        att = sb("attention_vectors", [P, 2, DIM])
        stats = sb("ln_stats", [P, NODE_TILES, 6])
        mv = sb("ln_mean_var", [P, NODE_TILES, 2])
        rstd = sb("ln_rstd", [P, NODE_TILES])
        out_cnt = sb("out_count", [P, NODE_TILES])
        eps = sb("eps", [P, 1])
        in_cnt = sb("in_count", [P, NODE_TILES])
        rcnt = sb("inverse_count", [P, NODE_TILES])
        mask = sb("has_edges", [P, NODE_TILES])
        maskb = sb("no_edge_bias", [P, NODE_TILES])
        ends = sb("segment_end", [P, NODE_TILES])
        rdeg = sb("inverse_root_degree", [P, NODE_TILES])
        sq = sb("squares", [P, NODE_TILES])
        late, at = w_c[:, :, :, :, :].rearrange("p a b c d -> p (a b c d)"), [0]

        def part_of_late(n, pattern, **dims):
            lo = at[0]
            at[0] += n
            return late[:, lo:lo + n].rearrange(pattern, **dims)

        a_src, a_dst, p_self = (part_of_late(NODE_TILES * HEADS, "p (t h) -> p t h", h=HEADS) for _ in range(3))
        am = part_of_late((NODE_TILES + 1) * 2 * HEADS, "p (t h) -> p t h", h=2 * HEADS)
        small = part_of_late(4 * P, "p (a b) -> p a b", b=P)
        window = part_of_late(UNROLL * 2 * HEADS, "p (k h) -> p k h", h=2 * HEADS)

        sort_mem = own[:, :, :].rearrange("p t d -> p (t d)")
        o1 = 0
        small_sort = sort_mem[:, 0:4 * P].rearrange("p (a b) -> p a b", b=P)
        earlier = sort_mem[:, 4 * P:5 * P]
        junk2 = sort_mem[:, 5 * P:5 * P + 256]
        window_f = sort_mem[:, 7 * P:7 * P + EDGE_TILES]
        place_i = sort_mem[:, 11 * P:11 * P + EDGE_TILES].bitcast(I32)

        psum = [stack.enter_context(nc.psum_tensor(f"bank{i}", [P, 512], F32)) for i in range(8)]

        def dram(name, r, c):
            return nc.dram_tensor(name, (r, c), F32, kind="Internal").ap()

        t_u = dram("table_hidden", PADDED_NODES, DIM)
        t_x = [dram(f"table_hop{i}", PADDED_NODES, DIM) for i in range(HOPS)]
        t_g = dram("table_scaled", PADDED_NODES, DIM)
        t_h = dram("table_heads", PADDED_NODES, ATT_ROW)
        t_as = dram("table_a_src", PADDED_NODES, HEADS)
        t_am = dram("table_a_dst_max", WINDOWED_NODES, 2 * HEADS)
        t_sort = nc.dram_tensor("table_edges_by_src", (PADDED_EDGES, RECORD), I32, kind="Internal").ap()
        t_run = dram("table_running_max", P * EDGE_TILES, HEADS)

        s_row = [pr.sem(f"rows_landed{k}") for k in range(UNROLL)]
        s_hot = pr.sem("onehot_built")
        s_mm = pr.sem("tile_multiplied")
        s_acc = pr.sem("tile_accumulated")
        s_load = [pr.sem(f"load{k}") for k in range(3)]
        s_tab = pr.sem("table_written")
        s_out = pr.sem("output_written")
        passes = [0]

        def tile_rows(j):
            return LAST_ROWS if j == NODE_TILES - 1 else P

        turn, reader = [0], {}

        def bank():
            i = 4 + turn[0] % 4
            turn[0] += 1
            return i, psum[i], reader.get(i)

        def bank3():
            i = 4 + turn[0] % 4
            if i == 7:
                turn[0] += 1
                i = 4
            turn[0] += 1
            return i, psum[i], reader.get(i)

        V = lambda fn, *w: pr.op("dve", fn, *w)
        A = lambda fn, *w: pr.op("act", fn, *w)
        T = lambda fn, *w: pr.op("pe", fn, *w)

        pr.op("pool", lambda e: e.iota(iota_i, [[1, P]], base=0, channel_multiplier=0))
        c_iota = pr.op("pool", lambda e: e.iota(part_i[:, :], [[0, 1]], base=0, channel_multiplier=1))
        l_edge = None
        for o, i in ((src[:, :], a["src_t"]), (dst[:, :], a["dst_t"]), (weight[:, :], a["w_t"]),
                     (base[:, :], a["dst_t"][0:1, :].broadcast_to([P, EDGE_TILES]))):
            l_edge = pr.dma("sp", s_load[0], o, i)
        l_x = pr.dma("act", s_load[1], x[:, :, :], a["x"].rearrange("(t p) d -> p t d", p=P))
        s_w = pr.sem("weights_loaded")
        W = lambda o, i: pr.dma("sp", s_w, o, i)
        w_a4 = w_a[:, :].rearrange("p (s k n) -> p s k n", s=2, k=K_IN)
        for s, n in enumerate(("w1l", "w1r")):
            W(w_a4[:, s, :, :], a[n].rearrange("(k p) n -> p k n", p=P))
        for s, n in enumerate(("w2l", "w2r")):
            W(w_b[:, :, s * DIM:(s + 1) * DIM], a[n].rearrange("(k p) n -> p k n", p=P))
        for s, n in enumerate(("wn", "ws")):
            for h in range(HOPS):
                W(w_c[:, h, s, :, :], a[n][h].rearrange("(k p) n -> p k n", p=P))
        W(b1[:, :], a["b1"])
        for r, n in ((B_HID2, "b2"), (B_L2, "l2b"), (B_ATT, "l3bias"), (B_GAMMA, "gamma"), (B_BETA, "beta")):
            W(brow[:, r, :], a[n].broadcast_to([P, DIM]))
        for h in range(HOPS):
            W(brow[:, B_HOP + h, :], a["bn"][h:h + 1, :].broadcast_to([P, DIM]))
            W(own[:, h, 0:DIM], a["bs"][h:h + 1, :].broadcast_to([P, DIM]))
        for r, n in enumerate(("att_src", "att_dst")):
            l_w = W(att[:, r, :], a[n].broadcast_to([P, DIM]))

        c1 = V(lambda e: e.tensor_copy(iota[:, :], iota_i), c_iota)
        c2 = V(lambda e: e.tensor_copy(part[:, :], part_i[:, :]))
        c_id = V(lambda e: e.tensor_scalar(ident[:, :], iota[:, :], part[:, 0:1], None, ALU.is_equal), c2)
        c_one = V(lambda e: e.memset(ones[:, :], 1.0))
        c_zb = V(lambda e: e.memset(zeros_b[:, :], 0.0))
        V(lambda e: e.memset(eps[:, :], LN_EPS))
        V(lambda e: e.tensor_tensor(local[:, :], dst[:, :], base[:, :], ALU.subtract), l_edge)
        s1 = V(lambda e: e.tensor_scalar(src_i, src[:, :], 7, None, ALU.arith_shift_right))
        s2 = V(lambda e: e.tensor_copy(src_hi[:, :], src_i), s1)
        V(lambda e: e.scalar_tensor_tensor(out=src_lo[:, :], in0=src_hi[:, :], scalar=-float(P), in1=src[:, :],
                                           op0=ALU.mult, op1=ALU.add), s2)
        c_edges = V(lambda e: e.tensor_tensor(brow[:, B_HOP:B_HOP + HOPS, :], brow[:, B_HOP:B_HOP + HOPS, :],
                                              own[:, 0:HOPS, 0:DIM], ALU.add), l_w)

        pr.queue["pe"].append(lambda e: e.sem_inc(s_mm, UNROLL))
        pr.queue["dve"].append(lambda e: e.sem_inc(s_acc, PSUM_RING))

        def transposes(read, ready):
            tok = None
            free = pr.last("pe")
            for j in range(NODE_TILES):
                i, ps, freed = bank()
                t = read(j)
                T(lambda e, ps=ps, t=t: e.transpose(ps[:, 0:P], t[:, 0:P], ident[:, :]), freed, ready(j), c_id)
                m = T(lambda e, ps=ps, t=t: e.transpose(ps[:, P:2 * P], t[:, P:2 * P], ident[:, :]))
                tok = A(lambda e, ps=ps, j=j: e.copy(xT[:, :, j * P:(j + 1) * P],
                                                     ps[:, 0:DIM].rearrange("p (k n) -> p k n", k=K_IN)), m, free)
                reader[i] = tok
            return tok

        def edge_pass(table, ready, edges, width=DIM, planes=K_IN, weighted=False, count_in=False, count_out=False,
                      attention=None):
            index, local, base, weight = edges
            n = passes[0]
            passes[0] += 1
            mm0, acc0, hot0 = UNROLL + n * EDGE_TILES, PSUM_RING + n * EDGE_TILES, n * EDGE_TILES
            row0 = n * TURNS

            def pool(e):
                e.wait_ge(*ready)
                e.wait_ge(*c_edges)
                for t in range(EDGE_TILES):
                    e.wait_ge(s_mm, mm0 + t - UNROLL + 1)
                    e.indirect_dma_start(out=rows[:, t % UNROLL, 0:width], out_offset=None, in_=table,
                                         in_offset=bass.IndirectOffsetOnAxis(ap=index[:, t:t + 1], axis=0)
                                         ).then_inc(s_row[t % UNROLL], 16)

            pr.queue["pool"].append(pool)

            agg_read = pr.last("pe")
            zeroed = V(lambda e: e.memset(agg[:, 0:planes, :], 0.0), agg_read, c_edges)
            if attention is not None:
                pr.queue["dve"].append(lambda e: e.wait_ge(*attention))

            def dve(e):
                regs = [e.alloc_register(f"window{n}_{k}") for k in range(UNROLL)]
                e.wait_ge(*zeroed)
                with e.Fori(0, TURNS) as i:
                    e.load(regs, base[0:1, bass.ds(i * UNROLL, UNROLL)])
                    at = [e.snap(r, min_val=0, max_val=PADDED_NODES) for r in regs]
                    for k in range(UNROLL + LAG):
                        if k < UNROLL:
                            e.wait_ge(s_mm, i * UNROLL + (mm0 - UNROLL + k + 1))
                            col = bass.ds(i * UNROLL + k, 1)
                            if count_out:
                                e.tensor_scalar(src_lo_hot[:, k, :], iota[:, :], src_lo[:, col], None, ALU.is_equal)
                                e.tensor_scalar(src_hi_hot[:, k, 0:NODE_TILES], iota[:, 0:NODE_TILES],
                                                src_hi[:, col], None, ALU.is_equal).then_inc(s_hist, 1)
                            hot = (e.tensor_scalar(onehot[:, k, :], iota[:, :], local[:, col], weight[:, col],
                                                   ALU.is_equal, ALU.mult) if weighted else
                                   e.tensor_scalar(onehot[:, k, :], iota[:, :], local[:, col], None, ALU.is_equal))
                            if attention is None:
                                hot.then_inc(s_hot, 1)
                            else:
                                e.wait_ge(s_row[k], i * 16 + (16 * row0 + 16))
                                g = rows[:, k, :].rearrange("p (h c) -> p h c", h=HEADS)
                                p = p_edge[:, bass.ds((i * UNROLL + k) * HEADS, HEADS)]
                                e.tensor_tensor(g, g, p.unsqueeze(2).broadcast_to([P, HEADS, HEAD_ROW]),
                                                ALU.mult).then_inc(s_hot, 1)
                        if k >= LAG:
                            k2 = k - LAG
                            e.wait_ge(s_mm, i * UNROLL + (mm0 + k2 + 1))
                            e.wait_ge(s_acc, i * UNROLL + (acc0 + k2))
                            w = agg[:, 0:planes, bass.ds(at[k2], P)]
                            s = psum[k2 % PSUM_RING][:, 0:planes * P].rearrange("p (k n) -> p k n", k=planes)
                            e.tensor_tensor(w, w, s, ALU.add).then_inc(s_acc, 1)

            pr.queue["dve"].append(dve)

            if count_out:
                T(lambda e: e.matmul(psum[7][:, 0:NODE_TILES], zeros_b[:, :], zeros_b[:, 0:NODE_TILES], start=True,
                                     stop=False, skip_group_check=True), c_zb, reader.get(7))

            def pe(e):
                with e.Fori(0, TURNS) as i:
                    for k in range(UNROLL):
                        e.wait_ge(s_hot, i * UNROLL + (hot0 + k + 1))
                        e.wait_ge(s_row[k], i * 16 + (16 * row0 + 16))
                        e.wait_ge(s_acc, i * UNROLL + (acc0 - PSUM_RING + k + 1))
                        ps = psum[k % PSUM_RING]
                        if count_out:
                            e.wait_ge(s_hist, i * UNROLL + (k + 1))
                            e.matmul(psum[7][:, 0:NODE_TILES], src_lo_hot[:, k, :], src_hi_hot[:, k, 0:NODE_TILES],
                                     start=False, stop=False, skip_group_check=True)
                        cuts = [rows[:, k, 0:P], rows[:, k, P:2 * P]]
                        if count_in:
                            cuts.append(ones[:, :])
                        if attention is not None:
                            cuts.append(rows[:, k, ATT_ROW - P:ATT_ROW])
                        for c, lhs in enumerate(cuts):
                            m = e.matmul(ps[:, c * P:(c + 1) * P], lhs, onehot[:, k, :], start=True, stop=True)
                        m.then_inc(s_mm, 1)

            pr.queue["pe"].append(pe)
            return s_acc, acc0 + EDGE_TILES

        def layer_norm(load_y, finish, after=None):
            toks = []
            for j in range(NODE_TILES):
                t = load_y(j)
                b = V(lambda e, j=j: e.bn_stats(stats[:, j, :], x[:, j, :]), t)
                toks.append(V(lambda e, j=j: e.bn_aggr(mv[:, j, :], stats[:, j, :]), b))
            r = inverse_std(toks[-1])
            for j in range(NODE_TILES):
                o = V(lambda e, j=j: e.tensor_scalar(x[:, j, :], x[:, j, :], mv[:, j, 0:1], rstd[:, j:j + 1],
                                                     ALU.subtract, ALU.mult), r)
                finish(j, o)

        def inverse_std(ready):
            q = A(lambda e: e.activation(rstd[:, :], mv[:, :, 1], ACT.Sqrt, bias=eps[:, 0:1]), ready)
            return V(lambda e: e.reciprocal(rstd[:, :], rstd[:, :]), q)

        s_hist = pr.sem("src_onehot_built")
        by_dst = (src, local, base, None)

        xt_ready = transposes(lambda j: x[:, j, :], lambda j: l_x)
        pass_done = edge_pass(a["x"], l_edge, by_dst, planes=3, count_in=True)

        cnt = agg[:, 2, :]
        cum = hidden[0:1, 0:PADDED_NODES]
        i, ps, freed = bank()
        unit = ones[0:1, 0:1]
        sc = V(lambda e: e.tensor_tensor_scan(cum, unit.broadcast_to([1, PADDED_NODES]), cnt[0:1, 0:PADDED_NODES],
                                              0.0, ALU.mult, ALU.add), pass_done, c_one)
        for j in range(NODE_TILES):
            T(lambda e, j=j, ps=ps: e.matmul(ps[:, j:j + 1], cnt[0:1, j * P:(j + 1) * P], ones[0:1, 0:1],
                                             start=True, stop=True), freed, sc)
            m = T(lambda e, j=j, ps=ps: e.matmul(ps[:, 32 + j:33 + j], cum[0:1, j * P:(j + 1) * P],
                                                 ones[0:1, 0:1], start=True, stop=True))
        V(lambda e, ps=ps: e.tensor_copy(ends[:, :], ps[:, 32:32 + NODE_TILES]), m)
        t1 = V(lambda e, ps=ps: e.tensor_copy(in_cnt[:, :], ps[:, 0:NODE_TILES]))
        reader[i] = t1
        t2 = V(lambda e: e.tensor_scalar(mask[:, :], in_cnt[:, :], 0.0, None, ALU.is_gt), t1)
        V(lambda e: e.tensor_scalar(maskb[:, :], mask[:, :], 1.0, BIG, ALU.subtract, ALU.mult), t2)
        t3 = V(lambda e: e.tensor_scalar(rcnt[:, :], in_cnt[:, :], 1.0, None, ALU.max))
        V(lambda e: e.reciprocal(rcnt[:, :], rcnt[:, :]), t3)
        t4 = V(lambda e: e.tensor_scalar(cnt, cnt, 1.0, None, ALU.max), m)
        t5 = V(lambda e: e.reciprocal(cnt, cnt), t4)
        scaled = V(lambda e: e.tensor_tensor(agg[:, 0:K_IN, :], agg[:, 0:K_IN, :],
                                             cnt.unsqueeze(1).broadcast_to([P, K_IN, WINDOWED_NODES]), ALU.mult), t5)
        xb = V(lambda e: e.tensor_tensor(own[:, :, 0:DIM], x[:, :, :],
                                         brow[:, B_HID2:B_HID2 + 1, :].broadcast_to([P, NODE_TILES, DIM]), ALU.add),
               l_x, c_edges)

        hid = hidden[:, :].rearrange("p (b m n) -> p b m n", b=2, m=K_HID)
        hid_read = {0: sc, 1: sc}
        staged = {}
        wr = None
        nchunk = -(-PADDED_NODES // 512)
        for c in range(nchunk):
            n0, n1 = c * 512, min((c + 1) * 512, PADDED_NODES)
            wdt = n1 - n0
            made = []
            for mt in range(K_HID):
                i, ps, freed = bank()
                pairs = [(w_a4[:, s, k, mt * P:(mt + 1) * P], (agg if s == 0 else xT)[:, k, n0:n1])
                         for s in range(2) for k in range(K_IN)]
                for q, (l, r) in enumerate(pairs):
                    m = T(lambda e, q=q, l=l, r=r, ps=ps, wdt=wdt: e.matmul(ps[:, 0:wdt], l, r, start=(q == 0), stop=(q == 3)),
                          freed if q == 0 else None, scaled if q == 0 else None, xt_ready if q == 0 else None, l_w)
                tok = A(lambda e, ps=ps, c=c, mt=mt, wdt=wdt: e.activation(hid[:, c % 2, mt, 0:wdt], ps[:, 0:wdt], ACT.Relu,
                                                                  bias=b1[:, mt:mt + 1]), m, hid_read[c % 2])
                reader[i] = tok
                made.append(tok)
            for jj in range(wdt // P):
                j = n0 // P + jj
                i, ps, freed = bank()
                for mt in range(K_HID):
                    m = T(lambda e, ps=ps, c=c, mt=mt, jj=jj: e.matmul(ps[:, :], hid[:, c % 2, mt, jj * P:(jj + 1) * P],
                                                                       w_b[:, mt, :], start=(mt == 0), stop=(mt == K_HID - 1)),
                          freed if mt == 0 else None, made[-1])
                hid_read[c % 2] = m
                cp = A(lambda e, ps=ps, j=j: e.copy(stage[:, j % 4, 0:DIM], ps[:, 0:DIM]), m, staged.get(j % 4))
                reader[i] = V(lambda e, ps=ps, j=j: e.tensor_tensor(own[:, j, 0:DIM], own[:, j, 0:DIM], ps[:, DIM:2 * DIM],
                                                                    ALU.add), m, xb, cp)
                staged[j % 4] = wr = pr.dma("sp", stage_sem(pr, j % 4), t_u[j * P:(j + 1) * P, :],
                                            stage[:, j % 4, 0:DIM], cp)
        table = all_staged(pr, staged)
        pass_done = edge_pass(t_u, table, by_dst, count_out=True)

        deg_copied = V(lambda e: e.tensor_copy(out_cnt[:, :], psum[7][:, 0:NODE_TILES]), pass_done)
        d1 = V(lambda e: e.tensor_scalar(rdeg[:, :], out_cnt[:, :], 1.0, None, ALU.max), deg_copied)
        reader[7] = deg_copied
        d2 = A(lambda e: e.activation(rdeg[:, :], rdeg[:, :], ACT.Sqrt), d1)
        V(lambda e: e.reciprocal(rdeg[:, :], rdeg[:, :]), d2)

        def y0(j):
            i, ps, freed = bank()
            T(lambda e, ps=ps, j=j: e.transpose(ps[:, 0:P], agg[:, 0, j * P:(j + 1) * P], ident[:, :]), freed, pass_done)
            m = T(lambda e, ps=ps, j=j: e.transpose(ps[:, P:2 * P], agg[:, 1, j * P:(j + 1) * P], ident[:, :]))
            reader[i] = V(lambda e, ps=ps, j=j: e.scalar_tensor_tensor(
                out=x[:, j, :], in0=ps[:, 0:DIM], scalar=rcnt[:, j:j + 1], in1=own[:, j, 0:DIM],
                op0=ALU.mult, op1=ALU.add), m)
            return reader[i]

        x_tok = {}

        def keep(j, tok):
            x_tok[j] = tok

        layer_norm(y0, keep)

        def write_table(tab, src_ap, tok, width=DIM):
            t = None
            for j in range(NODE_TILES):
                t = pr.dma("sp", s_tab, tab[j * P:(j + 1) * P, :], src_ap(j), tok(j))
            return t

        def own_product(weights, bias=None):
            tok = None
            for j in range(NODE_TILES):
                i, ps, freed = bank()
                for k in range(K_IN):
                    m = T(lambda e, ps=ps, j=j, k=k: e.matmul(ps[:, 0:DIM], xT[:, k, j * P:(j + 1) * P], weights[:, k, :],
                                                              start=(k == 0), stop=(k == K_IN - 1)), freed, xt_ready)
                if bias is None:
                    tok = A(lambda e, ps=ps, j=j: e.copy(own[:, j, 0:DIM], ps[:, 0:DIM]), m, pr.last("dve"))
                else:
                    tok = V(lambda e, ps=ps, j=j: e.tensor_tensor(own[:, j, 0:DIM], ps[:, 0:DIM], brow[:, bias, :], ALU.add), m)
                reader[i] = tok
            return tok

        def sort_by_source():
            row = agg[0:1, 0, 0:PADDED_NODES]
            before = agg[0:1, 1, 0:PADDED_NODES]
            start = small_sort[:, 0, 0:NODE_TILES]
            i, ps, freed = bank()
            free = pr.last("pe")
            deg_row = None
            for j in range(NODE_TILES):
                i, ps, freed = bank()
                m = T(lambda e, ps=ps, j=j: e.matmul(ps[0:1, 0:P], out_cnt[:, j:j + 1], ident[:, :], start=True, stop=True),
                      freed, deg_copied, free)
                deg_row = V(lambda e, ps=ps, j=j: e.tensor_copy(row[:, j * P:(j + 1) * P], ps[0:1, 0:P]), m)
                reader[i] = deg_row
            t = V(lambda e: e.tensor_tensor_scan(before, unit.broadcast_to([1, PADDED_NODES]), row, 0.0, ALU.mult, ALU.add), deg_row)
            t = V(lambda e: e.tensor_tensor(before, before, row, ALU.subtract), t)
            i, ps, freed = bank()
            for j in range(NODE_TILES):
                m = T(lambda e, ps=ps, j=j: e.matmul(ps[:, j:j + 1], before[:, j * P:(j + 1) * P], ones[0:1, 0:1],
                                                     start=True, stop=True), freed, t)
            started = V(lambda e, ps=ps: e.tensor_copy(start, ps[:, 0:NODE_TILES]), m)
            reader[i] = started

            words = agg[:, 2, :].bitcast(I32)
            rec = words[:, 0:EDGE_TILES * RECORD].rearrange("p (t r) -> p t r", r=RECORD)
            sorted_rec = words[:, EDGE_TILES * RECORD:2 * EDGE_TILES * RECORD]
            t = V(lambda e: e.memset(rec, 0), started)
            V(lambda e: e.tensor_copy(rec[:, :, 0], dst[:, :]), t)
            V(lambda e: e.tensor_copy(rec[:, :, 1], src[:, :]))
            rec_ok = V(lambda e: e.tensor_copy(rec[:, :, 2], weight[:, :].bitcast(I32)))
            srcf = window_f
            t = V(lambda e: e.tensor_copy(srcf, src[:, :]))
            earlier_ok = V(lambda e: e.tensor_scalar(earlier, iota[:, :], part[:, 0:1], None, ALU.is_lt))

            src_row = rows[:, :, :].rearrange("p a b -> p (a b)")[:, 0:2 * UNROLL * P].bitcast(I32)
            hid_i = hidden[:, :].bitcast(I32)
            row_lo = hid_i[:, 0:UNROLL * P]
            lo_T = [hidden[:, (1 + b) * UNROLL * P:(2 + b) * UNROLL * P] for b in range(2)]
            junk = hidden[:, 3 * UNROLL * P:3 * UNROLL * P + P]
            s_sr = [pr.sem(f"src_row_landed{k}") for k in range(2)]
            s_moved = pr.sem("records_moved")
            ranks = small_sort[:, 1, :]
            pos_f = small_sort[:, 2, :]
            snap = [small_sort[:, 3, b * 32:b * 32 + NODE_TILES] for b in range(2)]
            counts = psum[7][:, 0:NODE_TILES]
            first = T(lambda e: e.matmul(counts, ident[:, :], start, start=True, stop=False, skip_group_check=True),
                      started, reader.get(7))
            counted, expanded, row_free, group_read, snap_read = first, {}, {}, {}, {}
            prev_places = None
            for g in range(TURNS):
                b = g % 2
                cols = slice(g * UNROLL, (g + 1) * UNROLL)
                sr = src_row[:, b * UNROLL * P:(b + 1) * UNROLL * P]
                landed = pr.dma("act", s_sr[b], sr,
                                a["src_run"][0:1, 1 + g * UNROLL * P:1 + (g + 1) * UNROLL * P].broadcast_to([P, UNROLL * P]),
                                row_free.get(g - 2), (s_mm, UNROLL + passes[0] * EDGE_TILES))
                t = V(lambda e, sr=sr: e.tensor_scalar(row_lo, sr, P - 1, None, ALU.bitwise_and), landed, prev_places)
                lo_ok = V(lambda e, b=b: e.tensor_scalar(lo_T[b], row_lo, part[:, 0:1], None, ALU.is_equal), t,
                          expanded.get(g - 2))
                V(lambda e, cols=cols: e.tensor_tensor(
                    src_lo_hot[:, :, :], iota[:, :].unsqueeze(1).broadcast_to([P, UNROLL, P]),
                    src_lo[:, cols].unsqueeze(2).broadcast_to([P, UNROLL, P]), ALU.is_equal), counted if g else None)
                hot = V(lambda e, cols=cols: e.tensor_tensor(
                    src_hi_hot[:, :, 0:NODE_TILES], iota[:, 0:NODE_TILES].unsqueeze(1).broadcast_to([P, UNROLL, NODE_TILES]),
                    src_hi[:, cols].unsqueeze(2).broadcast_to([P, UNROLL, NODE_TILES]), ALU.is_equal))
                for k in range(UNROLL):
                    rk = V(lambda e, k=k, g=g, sr=sr, b=b: e.scalar_tensor_tensor(
                        out=junk, in0=sr[:, k * P:(k + 1) * P], scalar=srcf[:, g * UNROLL + k:g * UNROLL + k + 1], in1=earlier,
                        op0=ALU.is_equal, op1=ALU.mult, accum_out=ranks[:, b * UNROLL + k:b * UNROLL + k + 1]),
                        earlier_ok, pr.last("dve"))
                row_free[g] = rk
                i, ps, freed = ebank(g)
                for k in range(UNROLL):
                    sn = A(lambda e, k=k: e.copy(snap[k % 2], counts), counted, snap_read.get(k % 2))
                    snap_read[k % 2] = T(lambda e, ps=ps, k=k, b=b: e.matmul(
                        ps[:, k * NODE_TILES:(k + 1) * NODE_TILES], lo_T[b][:, k * P:(k + 1) * P], snap[k % 2],
                        start=True, stop=True), freed if k == 0 else None, sn, lo_ok)
                    counted = T(lambda e, k=k: e.matmul(counts, src_lo_hot[:, k, :], src_hi_hot[:, k, 0:NODE_TILES],
                                                        start=False, stop=False, skip_group_check=True), hot)
                expanded[g] = snap_read[(UNROLL - 1) % 2]
                picked = junk2[:, 0:UNROLL * NODE_TILES].rearrange("p (k n) -> p k n", n=NODE_TILES)
                t = V(lambda e, ps=ps, picked=picked: e.tensor_tensor(
                    picked, ps[:, 0:UNROLL * NODE_TILES].rearrange("p (k n) -> p k n", n=NODE_TILES),
                    src_hi_hot[:, :, 0:NODE_TILES], ALU.mult), expanded[g], pr.last("dve"))
                reader[i] = t
                pf, rkg = pos_f[:, 0:UNROLL], ranks[:, b * UNROLL:(b + 1) * UNROLL]
                hf, hi_g = pos_f[:, UNROLL:2 * UNROLL], pos_f[:, 2 * UNROLL:3 * UNROLL].bitcast(I32)
                pi = pos_f[:, 3 * UNROLL:4 * UNROLL].bitcast(I32)
                place = place_i[:, cols]
                t = V(lambda e, picked=picked, pf=pf: e.tensor_reduce(pf, picked, AX_X, ALU.add), t)
                t = V(lambda e, pf=pf, rkg=rkg: e.tensor_tensor(pf, pf, rkg, ALU.add), t)
                t = V(lambda e, pf=pf, pi=pi: e.tensor_copy(pi, pf), t)
                t = V(lambda e, pi=pi, hi_g=hi_g: e.tensor_scalar(hi_g, pi, 7, None, ALU.arith_shift_right), t)
                t = V(lambda e, hf=hf, hi_g=hi_g: e.tensor_copy(hf, hi_g), t)
                t = V(lambda e, pf=pf, hf=hf: e.scalar_tensor_tensor(out=pf, in0=hf, scalar=-float(P), in1=pf, op0=ALU.mult, op1=ALU.add), t)
                t = V(lambda e, pf=pf, hf=hf: e.scalar_tensor_tensor(out=pf, in0=pf, scalar=float(EDGE_TILES), in1=hf,
                                                                op0=ALU.mult, op1=ALU.add), t)
                prev_places = V(lambda e, pf=pf, place=place: e.tensor_copy(place, pf), t)

                def move(e, g=g, ready=prev_places):
                    e.wait_ge(*ready)
                    e.wait_ge(*rec_ok)
                    for t in range(g * UNROLL, (g + 1) * UNROLL):
                        e.indirect_dma_start(out=t_sort, out_offset=bass.IndirectOffsetOnAxis(ap=place_i[:, t:t + 1], axis=0),
                                             in_=rec[:, t, :], in_offset=None).then_inc(s_moved, 16)

                pr.queue["pool"].append(move)
            reader[7] = pr.last("act")
            s_back = pr.sem("sorted_records_loaded")
            back = pr.dma("sp", s_back, sorted_rec, t_sort.rearrange("(p t) r -> p (t r)", p=P), (s_moved, 16 * EDGE_TILES))
            sr3 = sorted_rec.rearrange("p (t r) -> p t r", r=RECORD)

            V(lambda e: e.tensor_copy(dst[:, :], sr3[:, :, 0]), back, prev_places)
            V(lambda e: e.tensor_copy(weight[:, :].bitcast(I32), sr3[:, :, 2]))
            V(lambda e: e.tensor_copy(src_hi[:, :].bitcast(I32), sr3[:, :, 1]))
            t = V(lambda e: e.tensor_copy(srcf, sr3[:, :, 1]))
            i, ps, freed = bank()
            m = T(lambda e, ps=ps: e.matmul(ps[:, 0:EDGE_TILES], ones[0:1, :], srcf[0:1, :], start=True, stop=True), freed, t)
            by_src_ok = V(lambda e, ps=ps: e.tensor_tensor(src_lo[:, :], srcf, ps[:, 0:EDGE_TILES], ALU.subtract), m)
            reader[i] = by_src_ok
            pr.queue["pool"].append(lambda e: e.wait_ge(*by_src_ok))
            pr.queue["dve"].append(lambda e: e.wait_ge(*by_src_ok))
            return dst, src_lo, src_hi[:, :].bitcast(I32), weight

        def ebank(g):
            return bank3()

        table = write_table(t_x[0], lambda j: x[:, j, :], lambda j: x_tok[j])
        xt_ready = transposes(lambda j: x[:, j, :], lambda j: x_tok[j])
        w2 = w_a[:, 0:2 * K_IN * DIM].rearrange("p (s k n) -> p s k n", s=2, k=K_IN)
        w3 = w_a[:, 2 * K_IN * DIM:3 * K_IN * DIM].rearrange("p (k n) -> p k n", k=K_IN)
        free = pr.last("pe")
        s_w2 = pr.sem("late_weights_loaded")
        pr.dma("sp", s_w2, w2[:, 0, :, :], a["l2w1"].rearrange("(k p) n -> p k n", p=P), free)
        pr.dma("sp", s_w2, w2[:, 1, :, :], a["l2w2"].rearrange("(k p) n -> p k n", p=P))
        l_w2 = pr.dma("sp", s_w2, w3, a["l3w"].rearrange("(k p) n -> p k n", p=P))

        by_src = sort_by_source()
        for hop in range(HOPS):
            own_ready = own_product(w_c[:, hop, 1, :, :], B_HOP + hop)
            pass_done = edge_pass(t_x[hop], table, by_src, weighted=True)

            def neighbours(j, hop=hop):
                i, ps, freed = bank()
                for k in range(K_IN):
                    m = T(lambda e, ps=ps, j=j, k=k, hop=hop: e.matmul(ps[:, 0:DIM], agg[:, k, j * P:(j + 1) * P],
                                                              w_c[:, hop, 0, k, :], start=(k == 0), stop=(k == K_IN - 1)),
                          freed, pass_done)
                return i, ps, m

            if hop < HOPS - 1:
                toks = {}
                dmas = {}
                relu_read, elu_read = {}, {}
                for j in range(NODE_TILES):
                    i, ps, m = neighbours(j)
                    s = j % 4
                    h0 = V(lambda e, ps=ps, j=j: e.tensor_tensor(own[:, j, 0:DIM], ps[:, 0:DIM], own[:, j, 0:DIM], ALU.add), m)
                    reader[i] = h0
                    h1 = V(lambda e, j=j, s=s: e.tensor_scalar(tmp[:, s, 0:DIM], own[:, j, 0:DIM], 0.0, None, ALU.min), h0)
                    h2 = A(lambda e, s=s: e.activation(tmp[:, s, 0:DIM], tmp[:, s, 0:DIM], ACT.Exp), h1)
                    h3 = V(lambda e, j=j: e.tensor_scalar(own[:, j, 0:DIM], own[:, j, 0:DIM], 0.0, None, ALU.max), h1)
                    toks[j] = V(lambda e, j=j, s=s: e.scalar_tensor_tensor(
                        out=own[:, j, 0:DIM], in0=tmp[:, s, 0:DIM], scalar=-1.0, in1=own[:, j, 0:DIM],
                        op0=ALU.add, op1=ALU.add), h2, h3)
                table = write_table(t_x[hop + 1], lambda j: own[:, j, 0:DIM], lambda j: toks[j])
                xt_ready = transposes(lambda j: own[:, j, :], lambda j: toks[j])
                pr.queue["dve"].append(lambda e, table=table: e.wait_ge(*table))

        def y1(j):
            i, ps, m = neighbours(j)
            t = V(lambda e, ps=ps, j=j: e.tensor_tensor(own[:, j, 0:DIM], ps[:, 0:DIM], own[:, j, 0:DIM], ALU.add), m)
            reader[i] = t
            return V(lambda e, j=j: e.tensor_tensor(x[:, j, :], x[:, j, :], own[:, j, 0:DIM], ALU.add), t)

        pr.queue["dve"].append(lambda e, table=table: e.wait_ge(*table))
        layer_norm(y1, keep)

        toks, g_dma = {}, {}
        for j in range(NODE_TILES):
            s = j % 4
            t = V(lambda e, j=j, s=s: e.tensor_scalar(stage[:, s, 0:DIM], x[:, j, :], rdeg[:, j:j + 1], None, ALU.mult),
                  x_tok[j], staged.get(s))
            staged[s] = pr.dma("sp", stage_sem(pr, s), t_g[j * P:(j + 1) * P, :], stage[:, s, 0:DIM], t)
        table = all_staged(pr, staged)
        xt_ready = transposes(lambda j: x[:, j, :], lambda j: x_tok[j])
        pr.queue["pe"].append(lambda e: e.wait_ge(*l_w2))
        own_ready = own_product(w2[:, 0, :, :])
        pass_done = edge_pass(t_g, table, by_dst)
        prod = V(lambda e: e.tensor_tensor(xT[:, :, :], xT[:, :, :], agg[:, 0:K_IN, 0:PADDED_NODES], ALU.mult),
                 pass_done, pr.last("pe"))
        nrm = {}
        for j in range(NODE_TILES):
            i, ps, freed = bank()
            pairs = [(agg, 0, k) for k in range(K_IN)] + [(xT, 1, k) for k in range(K_IN)]
            for q, (l, s, k) in enumerate(pairs):
                m = T(lambda e, ps=ps, j=j, l=l, s=s, k=k, q=q: e.matmul(ps[:, 0:DIM], l[:, k, j * P:(j + 1) * P], w2[:, s, k, :],
                                                                     start=(q == 0), stop=(q == 3)), freed, prod)
            o = own[:, j, 0:DIM]
            t = V(lambda e, ps=ps, j=j, o=o: e.scalar_tensor_tensor(out=o, in0=ps[:, 0:DIM], scalar=rdeg[:, j:j + 1], in1=o,
                                                               op0=ALU.mult, op1=ALU.add), m, own_ready)
            reader[i] = t
            t = V(lambda e, j=j, o=o: e.scalar_tensor_tensor(out=o, in0=o, scalar=mask[:, j:j + 1], in1=brow[:, B_L2, :],
                                                        op0=ALU.mult, op1=ALU.add), t)
            t = V(lambda e, o=o: e.scalar_tensor_tensor(out=o, in0=o, scalar=0.01, in1=o, op0=ALU.mult, op1=ALU.max), t)
            nrm[j] = A(lambda e, j=j, o=o: e.activation(tmp[:, j % 4, 0:DIM], o, ACT.Square, accum_out=sq[:, j:j + 1]), t, nrm.get(j - 4))
        t = V(lambda e: e.tensor_scalar(sq[:, :], sq[:, :], 1e-24, None, ALU.max), nrm[NODE_TILES - 1])
        t = A(lambda e: e.activation(sq[:, :], sq[:, :], ACT.Sqrt), t)
        rn = V(lambda e: e.reciprocal(sq[:, :], sq[:, :]), t)
        layer_norm(lambda j: V(lambda e, j=j: e.scalar_tensor_tensor(
            out=x[:, j, :], in0=own[:, j, 0:DIM], scalar=sq[:, j:j + 1], in1=x[:, j, :], op0=ALU.mult, op1=ALU.add), rn), keep)

        xt_ready = transposes(lambda j: x[:, j, :], lambda j: x_tok[j])
        heads = lambda ap: ap.rearrange("p (h c) -> p h c", h=HEADS)
        h_rows = own[:, :, :].rearrange("p t (h c) -> p t h c", h=HEADS)
        h1 = V(lambda e: e.memset(own[:, :, :], 1.0), pr.last("dve"))
        tok = None
        for j in range(NODE_TILES):
            i, ps, freed = bank()
            for k in range(K_IN):
                m = T(lambda e, ps=ps, j=j, k=k: e.matmul(ps[:, 0:DIM], xT[:, k, j * P:(j + 1) * P], w3[:, k, :],
                                                          start=(k == 0), stop=(k == K_IN - 1)), freed, xt_ready)
            cp = A(lambda e, ps=ps, j=j: e.copy(h_rows[:, j, :, 0:HEAD_DIM], heads(ps[:, 0:DIM])), m, h1)
            for r, dest in enumerate((a_src, a_dst)):
                t = V(lambda e, ps=ps, r=r: e.tensor_tensor(tmp[:, r, 0:DIM], ps[:, 0:DIM], att[:, r, :], ALU.mult), m, cp, tok)
                tok = V(lambda e, j=j, r=r, dest=dest: e.tensor_reduce(dest[:, j, :], heads(tmp[:, r, 0:DIM]), AX_X, ALU.add), t)
            reader[i] = t
        tok_h = cp
        w_h = write_table(t_h, lambda j: own[:, j, :], lambda j: tok_h)
        w_as = pr.dma("sp", s_tab, t_as.rearrange("(t p) h -> p t h", p=P), a_src[:, :, :], tok)

        p_all = hidden[:, 0:EDGE_TILES * HEADS]
        p_edge = p_all
        s_gas = pr.sem("edge_a_src_landed")

        def gather_a_src(e):
            e.wait_ge(*w_as)
            for t in range(EDGE_TILES):
                e.indirect_dma_start(out=p_all[:, t * HEADS:(t + 1) * HEADS], out_offset=None, in_=t_as,
                                     in_offset=bass.IndirectOffsetOnAxis(ap=src[:, t:t + 1], axis=0)).then_inc(s_gas, 16)

        pr.queue["pool"].append(gather_a_src)
        g_as = (s_gas, 16 * EDGE_TILES)

        runs, seg, prev = agg[:, 0, :], agg[:, 1, :], agg[:, 2, :]
        seg_i, prev_i = seg.bitcast(I32), prev.bitcast(I32)
        s_seg = pr.sem("scan_dst_loaded")
        free = pr.last("pe")
        for r in range(SCAN_ROWS):
            pr.dma("act", s_seg, seg_i[r * HEADS:(r + 1) * HEADS, :],
                   a["dst_run"][0:1, 1 + r * SCAN_LEN:1 + (r + 1) * SCAN_LEN].broadcast_to([HEADS, SCAN_LEN]), free, pr.last("dve"))
            l_seg = pr.dma("act", s_seg, prev_i[r * HEADS:(r + 1) * HEADS, :],
                           a["dst_run"][0:1, r * SCAN_LEN:(r + 1) * SCAN_LEN].broadcast_to([HEADS, SCAN_LEN]))
        t = V(lambda e: e.tensor_tensor(seg, seg_i, prev_i, ALU.not_equal), l_seg)
        seg_ok = V(lambda e: e.tensor_scalar(seg, seg, -BIG, None, ALU.mult), t)
        by_step = V(lambda e: e.tensor_copy(prev.rearrange("p (k r h) -> p k r h", r=SCAN_ROWS, k=SCAN_TILES),
                                            p_all.rearrange("p (r k h) -> p k r h", r=SCAN_ROWS, k=SCAN_TILES)), seg_ok, g_as)
        got = None
        for k in range(SCAN_TILES):
            i, ps, freed = bank()
            m = T(lambda e, ps=ps, k=k: e.transpose(ps[:, 0:P], prev[:, k * P:(k + 1) * P], ident[:, :]), freed, by_step)
            got = V(lambda e, ps=ps, k=k: e.tensor_copy(runs[:, k * P:(k + 1) * P], ps[:, 0:P]), m)
            reader[i] = got
        run1 = V(lambda e: e.tensor_tensor_scan(prev, seg, runs, -BIG, ALU.add, ALU.max), got)
        low = V(lambda e: e.tensor_reduce(small[:, 0, 0:1], seg, AX_X, ALU.min))
        i, ps, freed = bank()
        T(lambda e, ps=ps: e.transpose(ps[0:1, 0:P], prev[:, SCAN_LEN - 1:SCAN_LEN], ident[:, :]), freed, run1)
        m = T(lambda e, ps=ps: e.transpose(ps[0:1, P:2 * P], small[:, 0, 0:1], ident[:, :]), low)
        c = V(lambda e, ps=ps: e.tensor_copy(small[0:1, 1, :], ps[0:1, 0:P]), m)
        c = V(lambda e, ps=ps: e.tensor_copy(small[0:1, 2, :], ps[0:1, P:2 * P]))
        reader[i] = c
        c = V(lambda e: e.memset(small[0:1, 3, 0:HEADS], -BIG), c)
        for h in range(HEADS):
            by_run = lambda q, lo, n, h=h: small[0:1, q, :].rearrange("p (r h) -> p r h", h=HEADS)[:, lo:lo + n, h]
            c = V(lambda e, f=by_run: e.tensor_tensor_scan(f(3, 1, SCAN_ROWS - 1), f(2, 0, SCAN_ROWS - 1), f(1, 0, SCAN_ROWS - 1),
                                                           -BIG, ALU.add, ALU.max), c)
        i, ps, freed = bank()
        m = T(lambda e, ps=ps: e.matmul(ps[:, 0:1], small[0:1, 3, :], ones[0:1, 0:1], start=True, stop=True), freed, c)
        c = V(lambda e, ps=ps: e.tensor_copy(small[:, 0, 1:2], ps[:, 0:1]), m)
        reader[i] = c
        run2 = V(lambda e: e.tensor_tensor_scan(prev, seg, runs, small[:, 0, 1:2], ALU.add, ALU.max), c)
        back = runs[:, :].rearrange("p (r k h) -> p k r h", r=SCAN_ROWS, k=SCAN_TILES)
        for k in range(SCAN_TILES):
            i, ps, freed = bank()
            m = T(lambda e, ps=ps, k=k: e.transpose(ps[:, 0:P], prev[:, k * P:(k + 1) * P], ident[:, :]), freed, run2)
            got = V(lambda e, ps=ps, k=k: e.tensor_copy(back[:, k, :, :], ps[:, 0:P].rearrange("p (r h) -> p r h", h=HEADS)), m)
            reader[i] = got
        w_run = pr.dma("sp", s_tab, t_run.rearrange("(p t) h -> p (t h)", p=P), runs, got)
        pos, pos_hi = small[:, 0, 0:NODE_TILES], small[:, 1, 0:NODE_TILES]
        pos_i, hi_i = small[:, 2, 0:NODE_TILES].bitcast(I32), small[:, 3, 0:NODE_TILES].bitcast(I32)
        t = V(lambda e: e.tensor_scalar(pos, ends[:, :], 1.0, 0.0, ALU.subtract, ALU.max), got)
        t = V(lambda e: e.tensor_copy(pos_i, pos), t)
        t = V(lambda e: e.tensor_scalar(hi_i, pos_i, 7, None, ALU.arith_shift_right), t)
        t = V(lambda e: e.tensor_copy(pos_hi, hi_i), t)
        t = V(lambda e: e.scalar_tensor_tensor(out=pos, in0=pos_hi, scalar=-float(P), in1=pos, op0=ALU.mult, op1=ALU.add), t)
        t = V(lambda e: e.scalar_tensor_tensor(out=pos, in0=pos, scalar=float(EDGE_TILES), in1=pos_hi, op0=ALU.mult, op1=ALU.add), t)
        last_row = V(lambda e: e.tensor_copy(pos_i, pos), t)
        mx = tmp[:, 0, 0:NODE_TILES * HEADS]
        mx3 = mx.rearrange("p (t h) -> p t h", h=HEADS)
        s_last = pr.sem("segment_max_landed")

        def gather_last(e):
            e.wait_ge(*w_run)
            e.wait_ge(*last_row)
            for j in range(NODE_TILES):
                e.indirect_dma_start(out=mx[:, j * HEADS:(j + 1) * HEADS], out_offset=None, in_=t_run,
                                     in_offset=bass.IndirectOffsetOnAxis(ap=pos_i[:, j:j + 1], axis=0)).then_inc(s_last, 16)

        pr.queue["pool"].append(gather_last)
        g_last = (s_last, 16 * NODE_TILES)
        nh = [P, NODE_TILES, HEADS]
        ad3, m3 = am[:, 0:NODE_TILES, 0:HEADS], am[:, 0:NODE_TILES, HEADS:2 * HEADS]
        z3 = tmp[:, 1, 0:NODE_TILES * HEADS].rearrange("p (t h) -> p t h", h=HEADS)
        t = V(lambda e: e.memset(am[:, :, :], 0.0))
        t = V(lambda e: e.tensor_copy(ad3, a_dst[:, :, :]), t)
        t = V(lambda e: e.tensor_tensor(mx3, mx3, mask[:, :].unsqueeze(2).broadcast_to(nh), ALU.mult), g_last, t)
        t = V(lambda e: e.tensor_tensor(mx3, mx3, maskb[:, :].unsqueeze(2).broadcast_to(nh), ALU.add), t)
        t = V(lambda e: e.tensor_tensor(mx3, mx3, a_src[:, :, :], ALU.max), t)
        t = V(lambda e: e.tensor_tensor(mx3, mx3, a_dst[:, :, :], ALU.add), t)
        t = V(lambda e: e.scalar_tensor_tensor(out=m3, in0=mx3, scalar=0.2, in1=mx3, op0=ALU.mult, op1=ALU.max), t)
        u = V(lambda e: e.tensor_tensor(z3, a_src[:, :, :], a_dst[:, :, :], ALU.add), t)
        u = V(lambda e: e.scalar_tensor_tensor(out=z3, in0=z3, scalar=0.2, in1=z3, op0=ALU.mult, op1=ALU.max), u)
        u = V(lambda e: e.tensor_tensor(z3, z3, m3, ALU.subtract), u)
        ps_tok = A(lambda e: e.activation(p_self[:, :, :], z3, ACT.Exp), u)
        w_am = pr.dma("sp", s_tab, t_am.rearrange("(t p) h -> p t h", p=P), am[:, :, :], t)

        dst_row = rows[:, :, :].rearrange("p a b -> p (a b)")[:, 0:2 * UNROLL * P].bitcast(I32)
        colid = src_hi
        cid = V(lambda e: e.tensor_copy(colid[:, :], base[:, :]))
        cid = V(lambda e: e.tensor_scalar(colid[:, :], colid[:, :], part[:, 0:1], None, ALU.add), cid)
        s_dr = [pr.sem(f"dst_row_landed{k}") for k in range(2)]
        s_win = [pr.sem(f"window_landed{k}") for k in range(UNROLL)]
        s_exp = pr.sem("window_multiplied")
        sp_regs = []

        def win_regs(e):
            sp_regs.extend(e.alloc_register(f"win{k}") for k in range(UNROLL))
            e.wait_ge(*w_am)

        pr.queue["sp"].append(win_regs)
        drow_tok, grp_mm, drow_free, grp_tok = {}, {}, {}, {}
        for i in range(TURNS):
            drow_tok[i] = pr.dma("act", s_dr[i % 2], dst_row[:, (i % 2) * UNROLL * P:(i % 2 + 1) * UNROLL * P],
                                 a["dst_run"][0:1, 1 + i * UNROLL * P:1 + (i + 1) * UNROLL * P].broadcast_to([P, UNROLL * P]),
                                 drow_free.get(i - 2), (s_mm, UNROLL + passes[0] * EDGE_TILES))

            def windows(e, i=i):
                e.load(sp_regs, base[0:1, i * UNROLL:(i + 1) * UNROLL])
                at = [e.snap(r, min_val=0, max_val=PADDED_NODES) for r in sp_regs]
                for k in range(UNROLL):
                    if i:
                        e.wait_ge(s_exp, (i - 1) * UNROLL + k + 1)
                    e.dma_start(window[:, k, :], t_am[bass.ds(at[k], P), :]).then_inc(s_win[k], 16)

            pr.queue["sp"].append(windows)
            bi, ps, freed = bank()
            for k in range(UNROLL):
                st = V(lambda e, i=i, k=k: e.tensor_scalar(onehot[:, k, :], dst_row[:, ((i % 2) * UNROLL + k) * P:((i % 2) * UNROLL + k + 1) * P],
                                                           colid[:, i * UNROLL + k:i * UNROLL + k + 1], None, ALU.is_equal),
                       drow_tok[i], (s_exp, (i - 1) * UNROLL + k + 1) if i else cid)
                pr.op("pe", lambda e, ps=ps, k=k: e.matmul(ps[:, k * 2 * HEADS:(k + 1) * 2 * HEADS], onehot[:, k, :], window[:, k, :],
                                                           start=True, stop=True), freed if k == 0 else None, st,
                      (s_win[k], 16 * (i + 1)), sem=s_exp)
            drow_free[i] = st
            got = ps[:, 0:UNROLL * 2 * HEADS].rearrange("p (t h) -> p t h", h=2 * HEADS)
            pe3 = p_all[:, i * UNROLL * HEADS:(i + 1) * UNROLL * HEADS].rearrange("p (t h) -> p t h", h=HEADS)
            t = V(lambda e, pe3=pe3, got=got: e.tensor_tensor(pe3, pe3, got[:, :, 0:HEADS], ALU.add), (s_exp, (i + 1) * UNROLL), g_as)
            t = V(lambda e, pe3=pe3: e.scalar_tensor_tensor(out=pe3, in0=pe3, scalar=0.2, in1=pe3, op0=ALU.mult, op1=ALU.max), t)
            t = V(lambda e, pe3=pe3, got=got: e.tensor_tensor(pe3, pe3, got[:, :, HEADS:2 * HEADS], ALU.subtract), t)
            reader[bi] = t
            t = V(lambda e, pe3=pe3: e.tensor_scalar(pe3, pe3, 0.0, None, ALU.min), t)
            exp_done = A(lambda e, pe3=pe3: e.activation(pe3, pe3, ACT.Exp), t)

        pr.queue["pe"].append(lambda e: e.wait_ge(*exp_done))
        pr.queue["dve"].append(lambda e: e.wait_ge(s_exp, EDGE_TILES))
        pr.queue["dve"].append(lambda e: e.wait_ge(*w_run))
        pr.queue["pool"].append(lambda e: e.wait_ge(*exp_done))
        pass_done = edge_pass(t_h, w_h, by_dst, width=ATT_ROW, planes=3, attention=exp_done)

        def attended(j):
            i, ps, freed = bank()
            for c in range(3):
                m = T(lambda e, ps=ps, j=j, c=c: e.transpose(ps[:, c * P:(c + 1) * P], agg[:, c, j * P:(j + 1) * P], ident[:, :]),
                      freed, pass_done)
            o = h_rows[:, j, :, :]
            of = own[:, j, :]
            s = j % 4
            t = V(lambda e, j=j, o=o: e.tensor_tensor(o, o, p_self[:, j, :].unsqueeze(2).broadcast_to([P, HEADS, HEAD_ROW]), ALU.mult),
                  ps_tok, w_h)
            V(lambda e, of=of, ps=ps: e.tensor_tensor(of[:, 0:DIM], of[:, 0:DIM], ps[:, 0:DIM], ALU.add), m, t)
            t = V(lambda e, of=of, ps=ps: e.tensor_tensor(of[:, DIM:ATT_ROW], of[:, DIM:ATT_ROW], ps[:, 3 * P - HEADS:3 * P], ALU.add))
            reader[i] = t
            t = V(lambda e, j=j, o=o: e.tensor_scalar(a_dst[:, j, :], o[:, :, HEAD_DIM], 1e-16, None, ALU.add), t)
            t = V(lambda e, j=j: e.reciprocal(a_dst[:, j, :], a_dst[:, j, :]), t)
            t = V(lambda e, j=j, o=o, s=s: e.tensor_tensor(heads(tmp[:, s, 0:DIM]), o[:, :, 0:HEAD_DIM],
                                                    a_dst[:, j, :].unsqueeze(2).broadcast_to([P, HEADS, HEAD_DIM]), ALU.mult), t)
            t = V(lambda e, of=of, s=s: e.tensor_tensor(of[:, 0:DIM], tmp[:, s, 0:DIM], brow[:, B_ATT, :], ALU.add), t)
            t = V(lambda e, j=j, of=of: e.bn_stats(stats[:, j, :], of[:, 0:DIM]), t)
            return V(lambda e, j=j: e.bn_aggr(mv[:, j, :], stats[:, j, :]), t)

        for j in range(NODE_TILES):
            t = attended(j)
        r = inverse_std(t)

        def y3(j):
            o = own[:, j, 0:DIM]
            t = V(lambda e, j=j, o=o: e.scalar_tensor_tensor(out=o, in0=o, scalar=mv[:, j, 0:1], in1=brow[:, B_GAMMA, :],
                                                        op0=ALU.subtract, op1=ALU.mult), r)
            t = V(lambda e, j=j, o=o: e.scalar_tensor_tensor(out=o, in0=o, scalar=rstd[:, j:j + 1], in1=brow[:, B_BETA, :],
                                                        op0=ALU.mult, op1=ALU.add), t)
            return V(lambda e, j=j, o=o: e.tensor_tensor(x[:, j, :], x[:, j, :], o, ALU.add), t)

        def store(j, tok):
            n = tile_rows(j)
            pr.dma("sp" if j % 2 else "act", s_out, out[j * P:j * P + n, :], x[0:n, j, :], tok)

        layer_norm(y3, store)
        for e in ("sp", "act"):
            pr.queue[e].append(lambda g: g.wait_ge(s_out, 16 * NODE_TILES))
        pr.queue["sp"].append(lambda g: g.wait_ge(s_tab, pr.count[s_tab.name]))

        block = stack.enter_context(nc.Block())
        pr.run(block)


STAGE_SEMS = {}


def stage_sem(pr, k):
    key = (id(pr), k)
    if key not in STAGE_SEMS:
        STAGE_SEMS[key] = pr.sem(f"stage_written{k}")
    return STAGE_SEMS[key]


class AllStaged:
    pass


def all_staged(pr, staged):
    toks = list(staged.values())
    done = pr.done["sp"]
    pr.count[done.name] = pr.count.get(done.name, 0) + 1

    def emit(eng):
        for s, v in toks:
            eng.wait_ge(s, v)
        eng.sem_inc(done, 1)

    pr.queue["sp"].append(emit)
    return done, pr.count[done.name]


def kernel(**inputs):
    import concourse.bacc as bacc
    from concourse.bass_utils import run_bass_kernel_spmd as run

    arr = {n: np.asarray(v) for n, v in inputs.items()}

    def tiled(v, fill):
        flat = np.full((PADDED_EDGES,), fill, v.dtype)
        flat[:EDGES] = v
        return np.ascontiguousarray(flat.reshape(EDGE_TILES, P).T)

    def t(v):
        return np.ascontiguousarray(np.swapaxes(v, -1, -2))

    x_rows = np.zeros((PADDED_NODES, DIM), arr["x"].dtype)
    x_rows[:NODES] = arr["x"]
    src_run, dst_run = (np.full((1, PADDED_EDGES + 1), PAD_NODE, arr[n].dtype) for n in ("src", "dst"))
    for run_of, n in ((src_run, "src"), (dst_run, "dst")):
        run_of[0, 0] = -1
        run_of[0, 1:EDGES + 1] = arr[n]
    data = {
        "x": x_rows,
        "src_t": tiled(arr["src"], PAD_NODE),
        "dst_t": tiled(arr["dst"], PAD_NODE),
        "w_t": tiled(arr["edge_weight"], 0),
        "src_run": src_run, "dst_run": dst_run,
        "w1l": t(arr["L0_gnn_W1l"]), "w1r": t(arr["L0_gnn_W1r"]),
        "w2l": t(arr["L0_gnn_W2l"]), "w2r": t(arr["L0_gnn_W2r"]),
        "b1": t(arr["L0_gnn_b1l"].reshape(K_HID, P)),
        "b2": arr["L0_gnn_b2l"].reshape(1, DIM),
        "wn": t(arr["L1_gnn_Wn"]), "ws": t(arr["L1_gnn_Ws"]),
        "bn": arr["L1_gnn_bn"], "bs": arr["L1_gnn_bs"],
        "l2w1": arr["L2_gnn_W1"], "l2w2": arr["L2_gnn_W2"], "l2b": arr["L2_gnn_b"].reshape(1, DIM),
        "l3w": arr["L3_gnn_W"],
        "att_src": arr["L3_gnn_att_src"].reshape(1, DIM), "att_dst": arr["L3_gnn_att_dst"].reshape(1, DIM),
        "l3bias": arr["L3_gnn_bias"].reshape(1, DIM),
        "gamma": arr["L3_gnn_ln_gamma"].reshape(1, DIM), "beta": arr["L3_gnn_ln_beta"].reshape(1, DIM),
    }
    nc = bacc.Bacc("TRN2", target_bir_lowering=False, num_devices=1)
    aps = {n: nc.dram_tensor(n, v.shape, mybir.dt.from_np(v.dtype), kind="ExternalInput").ap()
           for n, v in data.items()}
    out = nc.dram_tensor("out", (NODES, DIM), F32, kind="ExternalOutput").ap()
    residual_gnn(nc, aps, out)
    r = run(nc, [data], core_ids=[0])
    return r.results[0]["out"]
```

```python
from contextlib import ExitStack

import numpy as np
import concourse.bass as bass
from concourse import mybir

F32 = mybir.dt.float32
BF16 = mybir.dt.bfloat16
I32 = mybir.dt.int32
ALU = mybir.AluOpType
ACT = mybir.ActivationFunctionType
AX_X = mybir.AxisListType.X

P = 128
NODES = 3125
EDGES = 53125
DIM = 256
HIDDEN = 512
HOPS = 3
HEADS = 8
HEAD_DIM = DIM // HEADS
HEAD_ROW = HEAD_DIM + 1
ATT_ROW = HEADS * HEAD_ROW
NODE_TILES = -(-NODES // P)
PADDED_NODES = NODE_TILES * P
LAST_ROWS = NODES - (NODE_TILES - 1) * P
WINDOWED_NODES = PADDED_NODES + P
EDGE_TILES = 416
PADDED_EDGES = EDGE_TILES * P
UNROLL = 8
GROUP = 4
GROUPS = UNROLL // GROUP
TURNS = EDGE_TILES // UNROLL
CONTROL = UNROLL + GROUPS
SCAN_ROWS = P // HEADS
SCAN_TILES = EDGE_TILES // SCAN_ROWS
SCAN_LEN = SCAN_TILES * P
PAD_NODE = PADDED_NODES - 1
RECORD = 4
BIG = 1.0e30
LN_EPS = 1e-5
K_IN = DIM // P
K_HID = HIDDEN // P


class Program:

    ENGINES = ("pe", "dve", "act", "pool", "sp")

    def __init__(self, nc, stack):
        self.nc, self.stack = nc, stack
        self.queue = {e: [] for e in self.ENGINES}
        self.done = {e: stack.enter_context(nc.semaphore(f"done_{e}")) for e in self.ENGINES}
        self.count = {}

    def sem(self, name):
        return self.stack.enter_context(self.nc.semaphore(name))

    def op(self, e, fn, *waits, sem=None, by=1):
        sem = self.done[e] if sem is None else sem
        self.count[sem.name] = self.count.get(sem.name, 0) + by
        waits = [w for w in waits if w is not None]

        def emit(eng):
            for s, v in waits:
                eng.wait_ge(s, v)
            fn(eng).then_inc(sem, by)

        self.queue[e].append(emit)
        return sem, self.count[sem.name]

    def dma(self, e, sem, out, in_, *waits):
        return self.op(e, lambda eng: eng.dma_start(out, in_), *waits, sem=sem, by=16)

    def last(self, e):
        return self.done[e], self.count.get(self.done[e].name, 0)

    def run(self, block):
        names = dict(pe=block.tensor, dve=block.vector, act=block.scalar, pool=block.gpsimd, sp=block.sync)
        for e, deco in names.items():
            def body(eng, e=e):
                for emit in self.queue[e]:
                    emit(eng)
            deco(body)


def residual_gnn(nc, a, out):
    with ExitStack() as stack:
        pr = Program(nc, stack)

        def sb(name, shape, dt=F32):
            return stack.enter_context(nc.sbuf_tensor(name, shape, dt))

        x = sb("x_nodes", [P, NODE_TILES, DIM])
        xT = sb("x_features", [P, K_IN, PADDED_NODES])
        agg = sb("aggregate", [P, 3, WINDOWED_NODES])
        own = sb("own_term", [P, NODE_TILES, ATT_ROW])
        rows = sb("gathered_rows", [P, UNROLL, ATT_ROW])
        onehot = sb("edge_to_window", [P, UNROLL, P])
        src_lo_hot = sb("src_lo_onehot", [P, UNROLL, P], BF16)
        src_hi_hot = sb("src_hi_onehot", [P, UNROLL, 32], BF16)
        w_a = sb("weights_a", [P, 2048])
        w_b = sb("weights_b", [P, K_HID, 2 * DIM])
        w_c = sb("weights_c", [P, HOPS, 2, K_IN, DIM])
        hidden = sb("hidden", [P, 2 * K_HID * 512])
        tmp = sb("tmp", [P, 4, ATT_ROW])
        stage = tmp
        src = sb("src", [P, EDGE_TILES], I32)
        src_i = hidden[:, 0:EDGE_TILES].bitcast(I32)
        src_lo = sb("src_lo", [P, EDGE_TILES])
        src_hi = sb("src_hi", [P, EDGE_TILES])
        dst = sb("dst", [P, EDGE_TILES], I32)
        base = sb("window_base", [P, EDGE_TILES], I32)
        control_dst, control_src = (sb(f"control_by_{n}", [P, TURNS * CONTROL], I32) for n in ("dst", "src"))
        local = sb("dst_in_window", [P, EDGE_TILES])
        weight = sb("edge_weight", [P, EDGE_TILES])
        iota_i = hidden[:, EDGE_TILES:EDGE_TILES + P].bitcast(I32)
        iota = sb("iota", [P, P])
        part_i = sb("partition_i", [P, 1], I32)
        part = sb("partition", [P, 1])
        ident = sb("identity", [P, P])
        ones = sb("ones", [P, P])
        zeros_b = sb("zeros_bf16", [P, P], BF16)
        b1 = sb("bias_hidden", [P, K_HID])
        brow = sb("bias_rows", [P, 8, DIM])
        B_HID2, B_HOP, B_L2, B_ATT, B_GAMMA, B_BETA = 0, 1, 4, 5, 6, 7
        att = sb("attention_vectors", [P, 2, DIM])
        stats = sb("ln_stats", [P, NODE_TILES, 6])
        mv = sb("ln_mean_var", [P, NODE_TILES, 2])
        rstd = sb("ln_rstd", [P, NODE_TILES])
        out_cnt = sb("out_count", [P, NODE_TILES])
        eps = sb("eps", [P, 1])
        in_cnt = sb("in_count", [P, NODE_TILES])
        rcnt = sb("inverse_count", [P, NODE_TILES])
        mask = sb("has_edges", [P, NODE_TILES])
        maskb = sb("no_edge_bias", [P, NODE_TILES])
        ends = sb("segment_end", [P, NODE_TILES])
        rdeg = sb("inverse_root_degree", [P, NODE_TILES])
        sq = sb("squares", [P, NODE_TILES])
        late, at = w_c[:, :, :, :, :].rearrange("p a b c d -> p (a b c d)"), [0]

        def part_of_late(n, pattern, **dims):
            lo = at[0]
            at[0] += n
            return late[:, lo:lo + n].rearrange(pattern, **dims)

        a_src, a_dst, p_self = (part_of_late(NODE_TILES * HEADS, "p (t h) -> p t h", h=HEADS) for _ in range(3))
        am = part_of_late((NODE_TILES + 1) * 2 * HEADS, "p (t h) -> p t h", h=2 * HEADS)
        small = part_of_late(4 * P, "p (a b) -> p a b", b=P)
        window = part_of_late(UNROLL * 2 * HEADS, "p (k h) -> p k h", h=2 * HEADS)

        sort_mem = own[:, :, :].rearrange("p t d -> p (t d)")
        o1 = 0
        small_sort = sort_mem[:, 0:4 * P].rearrange("p (a b) -> p a b", b=P)
        earlier = sort_mem[:, 4 * P:5 * P]
        junk2 = sort_mem[:, 5 * P:5 * P + 256]
        window_f = sort_mem[:, 7 * P:7 * P + EDGE_TILES]
        place_i = sort_mem[:, 11 * P:11 * P + EDGE_TILES].bitcast(I32)

        psum = [stack.enter_context(nc.psum_tensor(f"bank{i}", [P, 512], F32)) for i in range(8)]

        def dram(name, r, c):
            return nc.dram_tensor(name, (r, c), F32, kind="Internal").ap()

        t_u = dram("table_hidden", PADDED_NODES, DIM)
        t_x = [dram(f"table_hop{i}", PADDED_NODES, DIM) for i in range(HOPS)]
        t_g = dram("table_scaled", PADDED_NODES, DIM)
        t_h = dram("table_heads", PADDED_NODES, ATT_ROW)
        t_as = dram("table_a_src", PADDED_NODES, HEADS)
        t_am = dram("table_a_dst_max", WINDOWED_NODES, 2 * HEADS)
        t_sort = nc.dram_tensor("table_edges_by_src", (PADDED_EDGES, RECORD), I32, kind="Internal").ap()
        t_run = dram("table_running_max", P * EDGE_TILES, HEADS)

        s_row = [pr.sem(f"rows_landed{k}") for k in range(2 * UNROLL)]
        row_rounds = [0, 0]
        s_hot = pr.sem("onehot_built")
        s_mm = pr.sem("tile_multiplied")
        s_acc = pr.sem("tile_accumulated")
        s_load = [pr.sem(f"load{k}") for k in range(3)]
        s_tab = pr.sem("table_written")
        s_out = pr.sem("output_written")
        passes = [0]
        spare_rows = [w_a[:, 0:GROUP * ATT_ROW],
                      w_b[:, :, :].rearrange("p a b -> p (a b)")[:, 0:GROUP * ATT_ROW]]

        def tile_rows(j):
            return LAST_ROWS if j == NODE_TILES - 1 else P

        turn, reader = [0], {}

        def bank():
            i = 4 + turn[0] % 4
            turn[0] += 1
            return i, psum[i], reader.get(i)

        def bank3():
            i = 4 + turn[0] % 4
            if i == 7:
                turn[0] += 1
                i = 4
            turn[0] += 1
            return i, psum[i], reader.get(i)

        V = lambda fn, *w: pr.op("dve", fn, *w)
        A = lambda fn, *w: pr.op("act", fn, *w)
        T = lambda fn, *w: pr.op("pe", fn, *w)

        pr.op("pool", lambda e: e.iota(iota_i, [[1, P]], base=0, channel_multiplier=0))
        c_iota = pr.op("pool", lambda e: e.iota(part_i[:, :], [[0, 1]], base=0, channel_multiplier=1))
        l_edge = None
        for o, i in ((src[:, :], a["src_t"]), (dst[:, :], a["dst_t"]), (weight[:, :], a["w_t"]),
                     (base[:, :], a["dst_t"][0:1, :].broadcast_to([P, EDGE_TILES]))):
            l_edge = pr.dma("sp", s_load[0], o, i)
        l_x = pr.dma("act", s_load[1], x[:, :, :], a["x"].rearrange("(t p) d -> p t d", p=P))
        s_w = pr.sem("weights_loaded")
        W = lambda o, i: pr.dma("sp", s_w, o, i)
        w_a4 = w_a[:, :].rearrange("p (s k n) -> p s k n", s=2, k=K_IN)
        for s, n in enumerate(("w1l", "w1r")):
            W(w_a4[:, s, :, :], a[n].rearrange("(k p) n -> p k n", p=P))
        for s, n in enumerate(("w2l", "w2r")):
            W(w_b[:, :, s * DIM:(s + 1) * DIM], a[n].rearrange("(k p) n -> p k n", p=P))
        for s, n in enumerate(("wn", "ws")):
            for h in range(HOPS):
                W(w_c[:, h, s, :, :], a[n][h].rearrange("(k p) n -> p k n", p=P))
        W(b1[:, :], a["b1"])
        for r, n in ((B_HID2, "b2"), (B_L2, "l2b"), (B_ATT, "l3bias"), (B_GAMMA, "gamma"), (B_BETA, "beta")):
            W(brow[:, r, :], a[n].broadcast_to([P, DIM]))
        for h in range(HOPS):
            W(brow[:, B_HOP + h, :], a["bn"][h:h + 1, :].broadcast_to([P, DIM]))
            W(own[:, h, 0:DIM], a["bs"][h:h + 1, :].broadcast_to([P, DIM]))
        for r, n in enumerate(("att_src", "att_dst")):
            l_w = W(att[:, r, :], a[n].broadcast_to([P, DIM]))

        c1 = V(lambda e: e.tensor_copy(iota[:, :], iota_i), c_iota)
        c2 = V(lambda e: e.tensor_copy(part[:, :], part_i[:, :]))
        c_id = V(lambda e: e.tensor_scalar(ident[:, :], iota[:, :], part[:, 0:1], None, ALU.is_equal), c2)
        c_one = V(lambda e: e.memset(ones[:, :], 1.0))
        c_zb = V(lambda e: e.memset(zeros_b[:, :], 0.0))
        V(lambda e: e.memset(eps[:, :], LN_EPS))

        def place_windows(control, nodes, first, positions, ready):
            by_group = [P, EDGE_TILES // GROUP, GROUP]
            g3 = lambda ap: ap.rearrange("p (g k) -> p g k", k=GROUP)
            head = g3(first)[:, :, 0:1]
            wide, mixed = hidden[:, 0:EDGE_TILES // GROUP], hidden[:, P:P + EDGE_TILES]
            n = EDGE_TILES // GROUP
            t = V(lambda e: e.tensor_tensor(wide[:, 0:n - 1], g3(first)[:, 1:n, 0], g3(first)[:, 0:n - 1, 0], ALU.subtract), ready)
            V(lambda e: e.tensor_scalar(wide[:, n - 1:n], g3(first)[:, n - 1, 0:1], -1.0, float(PAD_NODE), ALU.mult, ALU.add), ready)
            t = V(lambda e: e.tensor_scalar(wide, wide, float(P), None, ALU.is_ge), pr.last("dve"))
            t = V(lambda e: e.tensor_tensor(g3(mixed), g3(first), head.broadcast_to(by_group), ALU.subtract), t)
            t = V(lambda e: e.tensor_tensor(g3(mixed), g3(mixed), wide.unsqueeze(2).broadcast_to(by_group), ALU.mult), t)
            t = V(lambda e: e.tensor_tensor(g3(mixed), g3(mixed), head.broadcast_to(by_group), ALU.add), t)
            c3 = control[:, :].rearrange("p (t c) -> p t c", c=CONTROL)
            V(lambda e: e.tensor_tensor(positions, nodes, mixed, ALU.subtract), t)
            V(lambda e: e.tensor_copy(c3[:, :, 0:UNROLL], mixed.rearrange("p (t k) -> p t k", k=UNROLL)), t)
            return V(lambda e: e.tensor_copy(c3[:, :, UNROLL:CONTROL], wide.rearrange("p (t k) -> p t k", k=GROUPS)), t)

        s1 = V(lambda e: e.tensor_scalar(src_i, src[:, :], 7, None, ALU.arith_shift_right), l_edge)
        s2 = V(lambda e: e.tensor_copy(src_hi[:, :], src_i), s1)
        V(lambda e: e.scalar_tensor_tensor(out=src_lo[:, :], in0=src_hi[:, :], scalar=-float(P), in1=src[:, :],
                                           op0=ALU.mult, op1=ALU.add), s2)
        c_edges = V(lambda e: e.tensor_tensor(brow[:, B_HOP:B_HOP + HOPS, :], brow[:, B_HOP:B_HOP + HOPS, :],
                                              own[:, 0:HOPS, 0:DIM], ALU.add), l_w)

        base_f = hidden[:, 1024:1024 + EDGE_TILES]
        bf = V(lambda e: e.tensor_copy(base_f, base[:, :]), l_edge)
        c_edges = place_windows(control_dst, dst[:, :], base_f, local[:, :], bf)

        pr.queue["pe"].append(lambda e: e.sem_inc(s_mm, UNROLL))
        pr.queue["dve"].append(lambda e: e.sem_inc(s_acc, 2 * GROUP))

        def transposes(read, ready):
            tok = None
            free = pr.last("pe")
            for j in range(NODE_TILES):
                i, ps, freed = bank()
                t = read(j)
                T(lambda e, ps=ps, t=t: e.transpose(ps[:, 0:P], t[:, 0:P], ident[:, :]), freed, ready(j), c_id)
                m = T(lambda e, ps=ps, t=t: e.transpose(ps[:, P:2 * P], t[:, P:2 * P], ident[:, :]))
                tok = A(lambda e, ps=ps, j=j: e.copy(xT[:, :, j * P:(j + 1) * P],
                                                     ps[:, 0:DIM].rearrange("p (k n) -> p k n", k=K_IN)), m, free)
                reader[i] = tok
            return tok

        def edge_pass(table, ready, edges, width=DIM, planes=K_IN, count_in=False, count_out=False,
                      attention=None):
            index, position, weight, control = edges
            n = passes[0]
            passes[0] += 1
            mm0, acc0, hot0 = UNROLL + n * EDGE_TILES, 2 * GROUP + n * EDGE_TILES, n * EDGE_TILES
            att = attention
            places = [rows[:, g * GROUP:(g + 1) * GROUP, :] for g in range(GROUPS)]
            if att is not None:
                places += [w.rearrange("p (k c) -> p k c", c=ATT_ROW) for w in spare_rows]
            ring = len(places) * GROUP
            slot = lambda k: places[k // GROUP][:, k % GROUP, :]
            half = ring // UNROLL

            def landed(e, i, k):
                e.wait_ge(s_row[i[1] * UNROLL + k], i[0] * 16 + (16 * rounds[i[1]] + 16))

            rounds = [row_rounds[h] for h in range(half)]
            for h in range(half):
                row_rounds[h] += TURNS // half

            def pool(e):
                e.wait_ge(*ready)
                e.wait_ge(*c_edges)
                for t in range(EDGE_TILES):
                    e.wait_ge(s_mm, mm0 + max(t - ring + 1, 1 - UNROLL))
                    e.indirect_dma_start(out=slot(t % ring)[:, 0:width], out_offset=None, in_=table,
                                         in_offset=bass.IndirectOffsetOnAxis(ap=index[:, t:t + 1], axis=0)
                                         ).then_inc(s_row[t % ring], 16)

            pr.queue["pool"].append(pool)

            agg_read = pr.last("pe")
            zeroed = V(lambda e: e.memset(agg[:, 0:planes, :], 0.0), agg_read, c_edges)

            def onehots(e, i, g, at_row):
                lo, hi = g * GROUP, (g + 1) * GROUP
                if not (isinstance(i, int) and i == 0 and n == 0):
                    e.wait_ge(s_mm, i * UNROLL + (mm0 - UNROLL + hi))
                cols = bass.ds(i * UNROLL + lo, GROUP)
                if count_out:
                    e.tensor_tensor(src_lo_hot[:, lo:hi, :], iota[:, :].unsqueeze(1).broadcast_to([P, GROUP, P]),
                                    src_lo[:, cols].unsqueeze(2).broadcast_to([P, GROUP, P]), ALU.is_equal)
                    e.tensor_tensor(src_hi_hot[:, lo:hi, 0:NODE_TILES],
                                    iota[:, 0:NODE_TILES].unsqueeze(1).broadcast_to([P, GROUP, NODE_TILES]),
                                    src_hi[:, cols].unsqueeze(2).broadcast_to([P, GROUP, NODE_TILES]),
                                    ALU.is_equal).then_inc(s_hist, GROUP)
                if weight is not None:
                    for k in range(lo, hi):
                        col = bass.ds(i * UNROLL + k, 1)
                        e.tensor_scalar(onehot[:, k, :], iota[:, :], position[:, col], weight[:, col],
                                        ALU.is_equal, ALU.mult).then_inc(s_hot, 1)
                    return
                hot = e.tensor_tensor(onehot[:, lo:hi, :], iota[:, :].unsqueeze(1).broadcast_to([P, GROUP, P]),
                                      position[:, cols].unsqueeze(2).broadcast_to([P, GROUP, P]), ALU.is_equal)
                if att is None:
                    hot.then_inc(s_hot, GROUP)
                else:
                    weigh(e, i, g, at_row).then_inc(s_hot, GROUP)

            def weigh(e, i, g, at_row):
                for k in range(g * GROUP, (g + 1) * GROUP):
                    landed(e, at_row, k)
                return att.weigh(e, i, g, places[at_row[1] * GROUPS + g])

            def each_turn(e, turn):
                def one_round(q, last):
                    for h in range(half):
                        here = (q, h)
                        after = (q, h + 1) if h + 1 < half else (q + 1, 0)
                        turn(q * half + h, not (last and h == half - 1), here, after)

                with e.Fori(0, TURNS // half - 1) as q:
                    one_round(q, False)
                one_round(TURNS // half - 1, True)

            def dve_turn(e, i, regs, ahead, after):
                e.load(regs, control[0:1, bass.ds(i * CONTROL, CONTROL)])
                at = [e.snap(r, min_val=0, max_val=PADDED_NODES) for r in regs[0:UNROLL]]
                wide = [e.snap(r, min_val=0, max_val=1) for r in regs[UNROLL:CONTROL]]
                if att is not None and ahead:
                    att.expand(e, i + 1)
                for g in range(GROUPS):
                    def add(k, tiles):
                        e.wait_ge(s_mm, i * UNROLL + (mm0 + k + tiles))
                        e.wait_ge(s_acc, i * UNROLL + (acc0 + k))
                        w = agg[:, 0:planes, bass.ds(at[k], P)]
                        bank_of = 2 * g + (k % 2 if tiles == 1 else 0)
                        s = psum[bank_of][:, 0:planes * P].rearrange("p (k n) -> p k n", k=planes)
                        e.tensor_tensor(w, w, s, ALU.add).then_inc(s_acc, tiles)

                    with e.If(wide[g]):
                        for k in range(g * GROUP, (g + 1) * GROUP):
                            add(k, 1)
                    with e.Else():
                        add(g * GROUP, GROUP)
                    if ahead:
                        if att is not None and g == 0:
                            att.exponents(e, i + 1)
                        onehots(e, i + 1, g, after)

            def dve(e):
                regs = [e.alloc_register(f"control{n}_{k}") for k in range(CONTROL)]
                e.wait_ge(*zeroed)
                if att is not None:
                    att.expand(e, 0)
                    att.exponents(e, 0)
                for g in range(GROUPS):
                    onehots(e, 0, g, (0, 0))
                each_turn(e, lambda i, ahead, here, after: dve_turn(e, i, regs, ahead, after))

            pr.queue["dve"].append(dve)

            if count_out:
                T(lambda e: e.matmul(psum[7][:, 0:NODE_TILES], zeros_b[:, :], zeros_b[:, 0:NODE_TILES], start=True,
                                     stop=False, skip_group_check=True), c_zb, reader.get(7))

            def pe_turn(e, i, regs, ahead, here):
                e.load(regs, control[0:1, bass.ds(i * CONTROL + UNROLL, GROUPS)])
                wide = [e.snap(r, min_val=0, max_val=1) for r in regs]
                for g in range(GROUPS):
                    def multiply(k, alone):
                        e.wait_ge(s_hot, i * UNROLL + (hot0 + k + 1))
                        landed(e, here, k)
                        row = slot(here[1] * UNROLL + k)
                        first = k % GROUP == 0
                        if first:
                            e.wait_ge(s_acc, i * UNROLL + (acc0 + k - GROUP))
                        elif alone and k % GROUP >= 2:
                            e.wait_ge(s_acc, i * UNROLL + (acc0 + k - 1))
                        ps = psum[2 * g + (k % 2 if alone else 0)]
                        if count_out:
                            e.wait_ge(s_hist, i * UNROLL + (k + 1))
                            e.matmul(psum[7][:, 0:NODE_TILES], src_lo_hot[:, k, :], src_hi_hot[:, k, 0:NODE_TILES],
                                     start=False, stop=False, skip_group_check=True)
                        cuts = [row[:, 0:P], row[:, P:2 * P]]
                        if count_in:
                            cuts.append(ones[:, :])
                        if att is not None:
                            cuts.append(row[:, ATT_ROW - P:ATT_ROW])
                        for c, lhs in enumerate(cuts):
                            m = e.matmul(ps[:, c * P:(c + 1) * P], lhs, onehot[:, k, :],
                                         start=(alone or first) and c == 0,
                                         stop=(alone or k % GROUP == GROUP - 1) and c == len(cuts) - 1,
                                         skip_group_check=True)
                        m.then_inc(s_mm, 1)

                    tiles = range(g * GROUP, (g + 1) * GROUP)
                    with e.If(wide[g]):
                        for k in tiles:
                            multiply(k, True)
                    with e.Else():
                        for k in tiles:
                            multiply(k, False)
                    if att is not None and g == 0 and ahead:
                        att.multiply(e, i + 1)

            def pe(e):
                regs = [e.alloc_register(f"wide{n}_{k}") for k in range(GROUPS)]
                e.wait_ge(*c_edges)
                if att is not None:
                    att.multiply(e, 0)
                each_turn(e, lambda i, ahead, here, after: pe_turn(e, i, regs, ahead, here))

            pr.queue["pe"].append(pe)
            return s_acc, acc0 + EDGE_TILES

        def layer_norm(load_y, finish, after=None):
            toks = []
            for j in range(NODE_TILES):
                t = load_y(j)
                b = V(lambda e, j=j: e.bn_stats(stats[:, j, :], x[:, j, :]), t)
                toks.append(V(lambda e, j=j: e.bn_aggr(mv[:, j, :], stats[:, j, :]), b))
            r = inverse_std(toks[-1])
            for j in range(NODE_TILES):
                o = V(lambda e, j=j: e.tensor_scalar(x[:, j, :], x[:, j, :], mv[:, j, 0:1], rstd[:, j:j + 1],
                                                     ALU.subtract, ALU.mult), r)
                finish(j, o)

        def inverse_std(ready):
            q = A(lambda e: e.activation(rstd[:, :], mv[:, :, 1], ACT.Sqrt, bias=eps[:, 0:1]), ready)
            return V(lambda e: e.reciprocal(rstd[:, :], rstd[:, :]), q)

        s_hist = pr.sem("src_onehot_built")
        by_dst = (src, local, None, control_dst)

        xt_ready = transposes(lambda j: x[:, j, :], lambda j: l_x)
        pass_done = edge_pass(a["x"], l_edge, by_dst, planes=3, count_in=True, count_out=True)

        deg_copied = V(lambda e: e.tensor_copy(out_cnt[:, :], psum[7][:, 0:NODE_TILES]), pass_done)
        d1 = V(lambda e: e.tensor_scalar(rdeg[:, :], out_cnt[:, :], 1.0, None, ALU.max), deg_copied)
        reader[7] = deg_copied
        d2 = A(lambda e: e.activation(rdeg[:, :], rdeg[:, :], ACT.Sqrt), d1)
        V(lambda e: e.reciprocal(rdeg[:, :], rdeg[:, :]), d2)

        cnt = agg[:, 2, :]
        cum = hidden[0:1, 0:PADDED_NODES]
        i, ps, freed = bank()
        unit = ones[0:1, 0:1]
        sc = V(lambda e: e.tensor_tensor_scan(cum, unit.broadcast_to([1, PADDED_NODES]), cnt[0:1, 0:PADDED_NODES],
                                              0.0, ALU.mult, ALU.add), pass_done, c_one)
        for j in range(NODE_TILES):
            T(lambda e, j=j, ps=ps: e.matmul(ps[:, j:j + 1], cnt[0:1, j * P:(j + 1) * P], ones[0:1, 0:1],
                                             start=True, stop=True), freed, sc)
            m = T(lambda e, j=j, ps=ps: e.matmul(ps[:, 32 + j:33 + j], cum[0:1, j * P:(j + 1) * P],
                                                 ones[0:1, 0:1], start=True, stop=True))
        V(lambda e, ps=ps: e.tensor_copy(ends[:, :], ps[:, 32:32 + NODE_TILES]), m)
        t1 = V(lambda e, ps=ps: e.tensor_copy(in_cnt[:, :], ps[:, 0:NODE_TILES]))
        reader[i] = t1
        t2 = V(lambda e: e.tensor_scalar(mask[:, :], in_cnt[:, :], 0.0, None, ALU.is_gt), t1)
        V(lambda e: e.tensor_scalar(maskb[:, :], mask[:, :], 1.0, BIG, ALU.subtract, ALU.mult), t2)
        t3 = V(lambda e: e.tensor_scalar(rcnt[:, :], in_cnt[:, :], 1.0, None, ALU.max))
        V(lambda e: e.reciprocal(rcnt[:, :], rcnt[:, :]), t3)
        t4 = V(lambda e: e.tensor_scalar(cnt, cnt, 1.0, None, ALU.max), m)
        t5 = V(lambda e: e.reciprocal(cnt, cnt), t4)
        scaled = V(lambda e: e.tensor_tensor(agg[:, 0:K_IN, :], agg[:, 0:K_IN, :],
                                             cnt.unsqueeze(1).broadcast_to([P, K_IN, WINDOWED_NODES]), ALU.mult), t5)
        xb = V(lambda e: e.tensor_tensor(own[:, :, 0:DIM], x[:, :, :],
                                         brow[:, B_HID2:B_HID2 + 1, :].broadcast_to([P, NODE_TILES, DIM]), ALU.add),
               l_x, c_edges)

        hid = hidden[:, :].rearrange("p (b m n) -> p b m n", b=2, m=K_HID)
        hid_read = {0: sc, 1: sc}
        staged = {}
        wr = None
        nchunk = -(-PADDED_NODES // 512)
        for c in range(nchunk):
            n0, n1 = c * 512, min((c + 1) * 512, PADDED_NODES)
            wdt = n1 - n0
            made = []
            for mt in range(K_HID):
                i, ps, freed = bank()
                pairs = [(w_a4[:, s, k, mt * P:(mt + 1) * P], (agg if s == 0 else xT)[:, k, n0:n1])
                         for s in range(2) for k in range(K_IN)]
                for q, (l, r) in enumerate(pairs):
                    m = T(lambda e, q=q, l=l, r=r, ps=ps, wdt=wdt: e.matmul(ps[:, 0:wdt], l, r, start=(q == 0), stop=(q == 3)),
                          freed if q == 0 else None, scaled if q == 0 else None, xt_ready if q == 0 else None, l_w)
                tok = A(lambda e, ps=ps, c=c, mt=mt, wdt=wdt: e.activation(hid[:, c % 2, mt, 0:wdt], ps[:, 0:wdt], ACT.Relu,
                                                                  bias=b1[:, mt:mt + 1]), m, hid_read[c % 2])
                reader[i] = tok
                made.append(tok)
            for jj in range(wdt // P):
                j = n0 // P + jj
                i, ps, freed = bank()
                for mt in range(K_HID):
                    m = T(lambda e, ps=ps, c=c, mt=mt, jj=jj: e.matmul(ps[:, :], hid[:, c % 2, mt, jj * P:(jj + 1) * P],
                                                                       w_b[:, mt, :], start=(mt == 0), stop=(mt == K_HID - 1)),
                          freed if mt == 0 else None, made[-1])
                hid_read[c % 2] = m
                cp = A(lambda e, ps=ps, j=j: e.copy(stage[:, j % 4, 0:DIM], ps[:, 0:DIM]), m, staged.get(j % 4))
                reader[i] = V(lambda e, ps=ps, j=j: e.tensor_tensor(own[:, j, 0:DIM], own[:, j, 0:DIM], ps[:, DIM:2 * DIM],
                                                                    ALU.add), m, xb, cp)
                staged[j % 4] = wr = pr.dma("sp", stage_sem(pr, j % 4), t_u[j * P:(j + 1) * P, :],
                                            stage[:, j % 4, 0:DIM], cp)
        table = all_staged(pr, staged)
        pass_done = edge_pass(t_u, table, by_dst)

        def y0(j):
            i, ps, freed = bank()
            T(lambda e, ps=ps, j=j: e.transpose(ps[:, 0:P], agg[:, 0, j * P:(j + 1) * P], ident[:, :]), freed, pass_done)
            m = T(lambda e, ps=ps, j=j: e.transpose(ps[:, P:2 * P], agg[:, 1, j * P:(j + 1) * P], ident[:, :]))
            reader[i] = V(lambda e, ps=ps, j=j: e.scalar_tensor_tensor(
                out=x[:, j, :], in0=ps[:, 0:DIM], scalar=rcnt[:, j:j + 1], in1=own[:, j, 0:DIM],
                op0=ALU.mult, op1=ALU.add), m)
            return reader[i]

        x_tok = {}

        def keep(j, tok):
            x_tok[j] = tok

        layer_norm(y0, keep)

        def write_table(tab, src_ap, tok, width=DIM):
            t = None
            for j in range(NODE_TILES):
                t = pr.dma("sp", s_tab, tab[j * P:(j + 1) * P, :], src_ap(j), tok(j))
            return t

        def own_product(weights, bias=None):
            tok = None
            for j in range(NODE_TILES):
                i, ps, freed = bank()
                for k in range(K_IN):
                    m = T(lambda e, ps=ps, j=j, k=k: e.matmul(ps[:, 0:DIM], xT[:, k, j * P:(j + 1) * P], weights[:, k, :],
                                                              start=(k == 0), stop=(k == K_IN - 1)), freed, xt_ready)
                if bias is None:
                    tok = A(lambda e, ps=ps, j=j: e.copy(own[:, j, 0:DIM], ps[:, 0:DIM]), m, pr.last("dve"))
                else:
                    tok = V(lambda e, ps=ps, j=j: e.tensor_tensor(own[:, j, 0:DIM], ps[:, 0:DIM], brow[:, bias, :], ALU.add), m)
                reader[i] = tok
            return tok

        def sort_by_source():
            row = agg[0:1, 0, 0:PADDED_NODES]
            before = agg[0:1, 1, 0:PADDED_NODES]
            start = small_sort[:, 0, 0:NODE_TILES]
            i, ps, freed = bank()
            free = pr.last("pe")
            deg_row = None
            for j in range(NODE_TILES):
                i, ps, freed = bank()
                m = T(lambda e, ps=ps, j=j: e.matmul(ps[0:1, 0:P], out_cnt[:, j:j + 1], ident[:, :], start=True, stop=True),
                      freed, deg_copied, free)
                deg_row = V(lambda e, ps=ps, j=j: e.tensor_copy(row[:, j * P:(j + 1) * P], ps[0:1, 0:P]), m)
                reader[i] = deg_row
            t = V(lambda e: e.tensor_tensor_scan(before, unit.broadcast_to([1, PADDED_NODES]), row, 0.0, ALU.mult, ALU.add), deg_row)
            t = V(lambda e: e.tensor_tensor(before, before, row, ALU.subtract), t)
            i, ps, freed = bank()
            for j in range(NODE_TILES):
                m = T(lambda e, ps=ps, j=j: e.matmul(ps[:, j:j + 1], before[:, j * P:(j + 1) * P], ones[0:1, 0:1],
                                                     start=True, stop=True), freed, t)
            started = V(lambda e, ps=ps: e.tensor_copy(start, ps[:, 0:NODE_TILES]), m)
            reader[i] = started

            words = agg[:, 2, :].bitcast(I32)
            rec = words[:, 0:EDGE_TILES * RECORD].rearrange("p (t r) -> p t r", r=RECORD)
            sorted_rec = words[:, EDGE_TILES * RECORD:2 * EDGE_TILES * RECORD]
            t = V(lambda e: e.memset(rec, 0), started)
            V(lambda e: e.tensor_copy(rec[:, :, 0], dst[:, :]), t)
            V(lambda e: e.tensor_copy(rec[:, :, 1], src[:, :]))
            rec_ok = V(lambda e: e.tensor_copy(rec[:, :, 2], weight[:, :].bitcast(I32)))
            srcf = window_f
            t = V(lambda e: e.tensor_copy(srcf, src[:, :]))
            earlier_ok = V(lambda e: e.tensor_scalar(earlier, iota[:, :], part[:, 0:1], None, ALU.is_lt))

            src_row = rows[:, :, :].rearrange("p a b -> p (a b)")[:, 0:2 * UNROLL * P].bitcast(I32)
            hid_i = hidden[:, :].bitcast(I32)
            row_lo = hid_i[:, 0:UNROLL * P]
            lo_T = [hidden[:, (1 + b) * UNROLL * P:(2 + b) * UNROLL * P] for b in range(2)]
            junk = hidden[:, 3 * UNROLL * P:3 * UNROLL * P + P]
            s_sr = [pr.sem(f"src_row_landed{k}") for k in range(2)]
            s_moved = pr.sem("records_moved")
            ranks = small_sort[:, 1, :]
            pos_f = small_sort[:, 2, :]
            snap = [small_sort[:, 3, b * 32:b * 32 + NODE_TILES] for b in range(2)]
            counts = psum[7][:, 0:NODE_TILES]
            first = T(lambda e: e.matmul(counts, ident[:, :], start, start=True, stop=False, skip_group_check=True),
                      started, reader.get(7))
            counted, expanded, row_free, group_read, snap_read = first, {}, {}, {}, {}
            prev_places = None
            for g in range(TURNS):
                b = g % 2
                cols = slice(g * UNROLL, (g + 1) * UNROLL)
                sr = src_row[:, b * UNROLL * P:(b + 1) * UNROLL * P]
                landed = pr.dma("act", s_sr[b], sr,
                                a["src_run"][0:1, 1 + g * UNROLL * P:1 + (g + 1) * UNROLL * P].broadcast_to([P, UNROLL * P]),
                                row_free.get(g - 2), (s_mm, UNROLL + passes[0] * EDGE_TILES))
                t = V(lambda e, sr=sr: e.tensor_scalar(row_lo, sr, P - 1, None, ALU.bitwise_and), landed, prev_places)
                lo_ok = V(lambda e, b=b: e.tensor_scalar(lo_T[b], row_lo, part[:, 0:1], None, ALU.is_equal), t,
                          expanded.get(g - 2))
                V(lambda e, cols=cols: e.tensor_tensor(
                    src_lo_hot[:, :, :], iota[:, :].unsqueeze(1).broadcast_to([P, UNROLL, P]),
                    src_lo[:, cols].unsqueeze(2).broadcast_to([P, UNROLL, P]), ALU.is_equal), counted if g else None)
                hot = V(lambda e, cols=cols: e.tensor_tensor(
                    src_hi_hot[:, :, 0:NODE_TILES], iota[:, 0:NODE_TILES].unsqueeze(1).broadcast_to([P, UNROLL, NODE_TILES]),
                    src_hi[:, cols].unsqueeze(2).broadcast_to([P, UNROLL, NODE_TILES]), ALU.is_equal))
                for k in range(UNROLL):
                    rk = V(lambda e, k=k, g=g, sr=sr, b=b: e.scalar_tensor_tensor(
                        out=junk, in0=sr[:, k * P:(k + 1) * P], scalar=srcf[:, g * UNROLL + k:g * UNROLL + k + 1], in1=earlier,
                        op0=ALU.is_equal, op1=ALU.mult, accum_out=ranks[:, b * UNROLL + k:b * UNROLL + k + 1]),
                        earlier_ok, pr.last("dve"))
                row_free[g] = rk
                i, ps, freed = ebank(g)
                for k in range(UNROLL):
                    sn = A(lambda e, k=k: e.copy(snap[k % 2], counts), counted, snap_read.get(k % 2))
                    snap_read[k % 2] = T(lambda e, ps=ps, k=k, b=b: e.matmul(
                        ps[:, k * NODE_TILES:(k + 1) * NODE_TILES], lo_T[b][:, k * P:(k + 1) * P], snap[k % 2],
                        start=True, stop=True), freed if k == 0 else None, sn, lo_ok)
                    counted = T(lambda e, k=k: e.matmul(counts, src_lo_hot[:, k, :], src_hi_hot[:, k, 0:NODE_TILES],
                                                        start=False, stop=False, skip_group_check=True), hot)
                expanded[g] = snap_read[(UNROLL - 1) % 2]
                picked = junk2[:, 0:UNROLL * NODE_TILES].rearrange("p (k n) -> p k n", n=NODE_TILES)
                t = V(lambda e, ps=ps, picked=picked: e.tensor_tensor(
                    picked, ps[:, 0:UNROLL * NODE_TILES].rearrange("p (k n) -> p k n", n=NODE_TILES),
                    src_hi_hot[:, :, 0:NODE_TILES], ALU.mult), expanded[g], pr.last("dve"))
                reader[i] = t
                pf, rkg = pos_f[:, 0:UNROLL], ranks[:, b * UNROLL:(b + 1) * UNROLL]
                hf, hi_g = pos_f[:, UNROLL:2 * UNROLL], pos_f[:, 2 * UNROLL:3 * UNROLL].bitcast(I32)
                pi = pos_f[:, 3 * UNROLL:4 * UNROLL].bitcast(I32)
                place = place_i[:, cols]
                t = V(lambda e, picked=picked, pf=pf: e.tensor_reduce(pf, picked, AX_X, ALU.add), t)
                t = V(lambda e, pf=pf, rkg=rkg: e.tensor_tensor(pf, pf, rkg, ALU.add), t)
                t = V(lambda e, pf=pf, pi=pi: e.tensor_copy(pi, pf), t)
                t = V(lambda e, pi=pi, hi_g=hi_g: e.tensor_scalar(hi_g, pi, 7, None, ALU.arith_shift_right), t)
                t = V(lambda e, hf=hf, hi_g=hi_g: e.tensor_copy(hf, hi_g), t)
                t = V(lambda e, pf=pf, hf=hf: e.scalar_tensor_tensor(out=pf, in0=hf, scalar=-float(P), in1=pf, op0=ALU.mult, op1=ALU.add), t)
                t = V(lambda e, pf=pf, hf=hf: e.scalar_tensor_tensor(out=pf, in0=pf, scalar=float(EDGE_TILES), in1=hf,
                                                                op0=ALU.mult, op1=ALU.add), t)
                prev_places = V(lambda e, pf=pf, place=place: e.tensor_copy(place, pf), t)

                def move(e, g=g, ready=prev_places):
                    e.wait_ge(*ready)
                    e.wait_ge(*rec_ok)
                    for t in range(g * UNROLL, (g + 1) * UNROLL):
                        e.indirect_dma_start(out=t_sort, out_offset=bass.IndirectOffsetOnAxis(ap=place_i[:, t:t + 1], axis=0),
                                             in_=rec[:, t, :], in_offset=None).then_inc(s_moved, 16)

                pr.queue["pool"].append(move)
            reader[7] = pr.last("act")
            s_back = pr.sem("sorted_records_loaded")
            back = pr.dma("sp", s_back, sorted_rec, t_sort.rearrange("(p t) r -> p (t r)", p=P), (s_moved, 16 * EDGE_TILES))
            sr3 = sorted_rec.rearrange("p (t r) -> p t r", r=RECORD)

            V(lambda e: e.tensor_copy(dst[:, :], sr3[:, :, 0]), back, prev_places)
            V(lambda e: e.tensor_copy(weight[:, :].bitcast(I32), sr3[:, :, 2]))
            t = V(lambda e: e.tensor_copy(srcf, sr3[:, :, 1]))
            i, ps, freed = bank()
            m = T(lambda e, ps=ps: e.matmul(ps[:, 0:EDGE_TILES], ones[0:1, :], srcf[0:1, :], start=True, stop=True), freed, t)
            first = V(lambda e, ps=ps: e.tensor_copy(src_hi[:, :], ps[:, 0:EDGE_TILES]), m)
            reader[i] = first
            by_src_ok = place_windows(control_src, srcf, src_hi[:, :], src_lo[:, :], first)
            pr.queue["pe"].append(lambda e: e.wait_ge(*by_src_ok))
            pr.queue["pool"].append(lambda e: e.wait_ge(*by_src_ok))
            pr.queue["dve"].append(lambda e: e.wait_ge(*by_src_ok))
            return dst, src_lo, weight, control_src

        def ebank(g):
            return bank3()

        table = write_table(t_x[0], lambda j: x[:, j, :], lambda j: x_tok[j])
        xt_ready = transposes(lambda j: x[:, j, :], lambda j: x_tok[j])
        w2 = w_a[:, 0:2 * K_IN * DIM].rearrange("p (s k n) -> p s k n", s=2, k=K_IN)
        w3 = w_a[:, 2 * K_IN * DIM:3 * K_IN * DIM].rearrange("p (k n) -> p k n", k=K_IN)
        free = pr.last("pe")
        s_w2 = pr.sem("late_weights_loaded")
        pr.dma("sp", s_w2, w2[:, 0, :, :], a["l2w1"].rearrange("(k p) n -> p k n", p=P), free)
        pr.dma("sp", s_w2, w2[:, 1, :, :], a["l2w2"].rearrange("(k p) n -> p k n", p=P))
        l_w2 = pr.dma("sp", s_w2, w3, a["l3w"].rearrange("(k p) n -> p k n", p=P))

        by_src = sort_by_source()
        for hop in range(HOPS):
            own_ready = own_product(w_c[:, hop, 1, :, :], B_HOP + hop)
            pass_done = edge_pass(t_x[hop], table, by_src)

            def neighbours(j, hop=hop):
                i, ps, freed = bank()
                for k in range(K_IN):
                    m = T(lambda e, ps=ps, j=j, k=k, hop=hop: e.matmul(ps[:, 0:DIM], agg[:, k, j * P:(j + 1) * P],
                                                              w_c[:, hop, 0, k, :], start=(k == 0), stop=(k == K_IN - 1)),
                          freed, pass_done)
                return i, ps, m

            if hop < HOPS - 1:
                toks = {}
                dmas = {}
                relu_read, elu_read = {}, {}
                for j in range(NODE_TILES):
                    i, ps, m = neighbours(j)
                    s = j % 4
                    h0 = V(lambda e, ps=ps, j=j: e.tensor_tensor(own[:, j, 0:DIM], ps[:, 0:DIM], own[:, j, 0:DIM], ALU.add), m)
                    reader[i] = h0
                    h1 = V(lambda e, j=j, s=s: e.tensor_scalar(tmp[:, s, 0:DIM], own[:, j, 0:DIM], 0.0, None, ALU.min), h0)
                    h2 = A(lambda e, s=s: e.activation(tmp[:, s, 0:DIM], tmp[:, s, 0:DIM], ACT.Exp), h1)
                    h3 = V(lambda e, j=j: e.tensor_scalar(own[:, j, 0:DIM], own[:, j, 0:DIM], 0.0, None, ALU.max), h1)
                    toks[j] = V(lambda e, j=j, s=s: e.scalar_tensor_tensor(
                        out=own[:, j, 0:DIM], in0=tmp[:, s, 0:DIM], scalar=-1.0, in1=own[:, j, 0:DIM],
                        op0=ALU.add, op1=ALU.add), h2, h3)
                table = write_table(t_x[hop + 1], lambda j: own[:, j, 0:DIM], lambda j: toks[j])
                xt_ready = transposes(lambda j: own[:, j, :], lambda j: toks[j])
                pr.queue["dve"].append(lambda e, table=table: e.wait_ge(*table))

        def y1(j):
            i, ps, m = neighbours(j)
            t = V(lambda e, ps=ps, j=j: e.tensor_tensor(own[:, j, 0:DIM], ps[:, 0:DIM], own[:, j, 0:DIM], ALU.add), m)
            reader[i] = t
            return V(lambda e, j=j: e.tensor_tensor(x[:, j, :], x[:, j, :], own[:, j, 0:DIM], ALU.add), t)

        pr.queue["dve"].append(lambda e, table=table: e.wait_ge(*table))
        layer_norm(y1, keep)

        toks, g_dma = {}, {}
        for j in range(NODE_TILES):
            s = j % 4
            t = V(lambda e, j=j, s=s: e.tensor_scalar(stage[:, s, 0:DIM], x[:, j, :], rdeg[:, j:j + 1], None, ALU.mult),
                  x_tok[j], staged.get(s))
            staged[s] = pr.dma("sp", stage_sem(pr, s), t_g[j * P:(j + 1) * P, :], stage[:, s, 0:DIM], t)
        table = all_staged(pr, staged)
        xt_ready = transposes(lambda j: x[:, j, :], lambda j: x_tok[j])
        pr.queue["pe"].append(lambda e: e.wait_ge(*l_w2))
        own_ready = own_product(w2[:, 0, :, :])
        pass_done = edge_pass(t_g, table, by_dst)
        prod = V(lambda e: e.tensor_tensor(xT[:, :, :], xT[:, :, :], agg[:, 0:K_IN, 0:PADDED_NODES], ALU.mult),
                 pass_done, pr.last("pe"))
        nrm = {}
        for j in range(NODE_TILES):
            i, ps, freed = bank()
            pairs = [(agg, 0, k) for k in range(K_IN)] + [(xT, 1, k) for k in range(K_IN)]
            for q, (l, s, k) in enumerate(pairs):
                m = T(lambda e, ps=ps, j=j, l=l, s=s, k=k, q=q: e.matmul(ps[:, 0:DIM], l[:, k, j * P:(j + 1) * P], w2[:, s, k, :],
                                                                     start=(q == 0), stop=(q == 3)), freed, prod)
            o = own[:, j, 0:DIM]
            t = V(lambda e, ps=ps, j=j, o=o: e.scalar_tensor_tensor(out=o, in0=ps[:, 0:DIM], scalar=rdeg[:, j:j + 1], in1=o,
                                                               op0=ALU.mult, op1=ALU.add), m, own_ready)
            reader[i] = t
            t = V(lambda e, j=j, o=o: e.scalar_tensor_tensor(out=o, in0=o, scalar=mask[:, j:j + 1], in1=brow[:, B_L2, :],
                                                        op0=ALU.mult, op1=ALU.add), t)
            t = V(lambda e, o=o: e.scalar_tensor_tensor(out=o, in0=o, scalar=0.01, in1=o, op0=ALU.mult, op1=ALU.max), t)
            nrm[j] = A(lambda e, j=j, o=o: e.activation(tmp[:, j % 4, 0:DIM], o, ACT.Square, accum_out=sq[:, j:j + 1]), t, nrm.get(j - 4))
        t = V(lambda e: e.tensor_scalar(sq[:, :], sq[:, :], 1e-24, None, ALU.max), nrm[NODE_TILES - 1])
        t = A(lambda e: e.activation(sq[:, :], sq[:, :], ACT.Sqrt), t)
        rn = V(lambda e: e.reciprocal(sq[:, :], sq[:, :]), t)
        layer_norm(lambda j: V(lambda e, j=j: e.scalar_tensor_tensor(
            out=x[:, j, :], in0=own[:, j, 0:DIM], scalar=sq[:, j:j + 1], in1=x[:, j, :], op0=ALU.mult, op1=ALU.add), rn), keep)

        xt_ready = transposes(lambda j: x[:, j, :], lambda j: x_tok[j])
        heads = lambda ap: ap.rearrange("p (h c) -> p h c", h=HEADS)
        h_rows = own[:, :, :].rearrange("p t (h c) -> p t h c", h=HEADS)
        h1 = V(lambda e: e.memset(own[:, :, :], 1.0), pr.last("dve"))
        tok = None
        for j in range(NODE_TILES):
            i, ps, freed = bank()
            for k in range(K_IN):
                m = T(lambda e, ps=ps, j=j, k=k: e.matmul(ps[:, 0:DIM], xT[:, k, j * P:(j + 1) * P], w3[:, k, :],
                                                          start=(k == 0), stop=(k == K_IN - 1)), freed, xt_ready)
            cp = A(lambda e, ps=ps, j=j: e.copy(h_rows[:, j, :, 0:HEAD_DIM], heads(ps[:, 0:DIM])), m, h1)
            for r, dest in enumerate((a_src, a_dst)):
                t = V(lambda e, ps=ps, r=r: e.tensor_tensor(tmp[:, r, 0:DIM], ps[:, 0:DIM], att[:, r, :], ALU.mult), m, cp, tok)
                tok = V(lambda e, j=j, r=r, dest=dest: e.tensor_reduce(dest[:, j, :], heads(tmp[:, r, 0:DIM]), AX_X, ALU.add), t)
            reader[i] = t
        tok_h = cp
        tok_h_pe = m
        w_h = write_table(t_h, lambda j: own[:, j, :], lambda j: tok_h)
        w_as = pr.dma("sp", s_tab, t_as.rearrange("(t p) h -> p t h", p=P), a_src[:, :, :], tok)

        p_all = hidden[:, 0:EDGE_TILES * HEADS]
        p_edge = p_all
        s_gas = pr.sem("edge_a_src_landed")

        def gather_a_src(e):
            e.wait_ge(*w_as)
            for t in range(EDGE_TILES):
                e.indirect_dma_start(out=p_all[:, t * HEADS:(t + 1) * HEADS], out_offset=None, in_=t_as,
                                     in_offset=bass.IndirectOffsetOnAxis(ap=src[:, t:t + 1], axis=0)).then_inc(s_gas, 16)

        pr.queue["pool"].append(gather_a_src)
        g_as = (s_gas, 16 * EDGE_TILES)

        runs, seg, prev = agg[:, 0, :], agg[:, 1, :], agg[:, 2, :]
        seg_i, prev_i = seg.bitcast(I32), prev.bitcast(I32)
        s_seg = pr.sem("scan_dst_loaded")
        free = pr.last("pe")
        for r in range(SCAN_ROWS):
            pr.dma("act", s_seg, seg_i[r * HEADS:(r + 1) * HEADS, :],
                   a["dst_run"][0:1, 1 + r * SCAN_LEN:1 + (r + 1) * SCAN_LEN].broadcast_to([HEADS, SCAN_LEN]), free, pr.last("dve"))
            l_seg = pr.dma("act", s_seg, prev_i[r * HEADS:(r + 1) * HEADS, :],
                           a["dst_run"][0:1, r * SCAN_LEN:(r + 1) * SCAN_LEN].broadcast_to([HEADS, SCAN_LEN]))
        t = V(lambda e: e.tensor_tensor(seg, seg_i, prev_i, ALU.not_equal), l_seg)
        seg_ok = V(lambda e: e.tensor_scalar(seg, seg, -BIG, None, ALU.mult), t)
        by_step = V(lambda e: e.tensor_copy(prev.rearrange("p (k r h) -> p k r h", r=SCAN_ROWS, k=SCAN_TILES),
                                            p_all.rearrange("p (r k h) -> p k r h", r=SCAN_ROWS, k=SCAN_TILES)), seg_ok, g_as)
        got = None
        for k in range(SCAN_TILES):
            i, ps, freed = bank()
            m = T(lambda e, ps=ps, k=k: e.transpose(ps[:, 0:P], prev[:, k * P:(k + 1) * P], ident[:, :]), freed, by_step)
            got = V(lambda e, ps=ps, k=k: e.tensor_copy(runs[:, k * P:(k + 1) * P], ps[:, 0:P]), m)
            reader[i] = got
        run1 = V(lambda e: e.tensor_tensor_scan(prev, seg, runs, -BIG, ALU.add, ALU.max), got)
        low = V(lambda e: e.tensor_reduce(small[:, 0, 0:1], seg, AX_X, ALU.min))
        i, ps, freed = bank()
        T(lambda e, ps=ps: e.transpose(ps[0:1, 0:P], prev[:, SCAN_LEN - 1:SCAN_LEN], ident[:, :]), freed, run1)
        m = T(lambda e, ps=ps: e.transpose(ps[0:1, P:2 * P], small[:, 0, 0:1], ident[:, :]), low)
        c = V(lambda e, ps=ps: e.tensor_copy(small[0:1, 1, :], ps[0:1, 0:P]), m)
        c = V(lambda e, ps=ps: e.tensor_copy(small[0:1, 2, :], ps[0:1, P:2 * P]))
        reader[i] = c
        c = V(lambda e: e.memset(small[0:1, 3, 0:HEADS], -BIG), c)
        for h in range(HEADS):
            by_run = lambda q, lo, n, h=h: small[0:1, q, :].rearrange("p (r h) -> p r h", h=HEADS)[:, lo:lo + n, h]
            c = V(lambda e, f=by_run: e.tensor_tensor_scan(f(3, 1, SCAN_ROWS - 1), f(2, 0, SCAN_ROWS - 1), f(1, 0, SCAN_ROWS - 1),
                                                           -BIG, ALU.add, ALU.max), c)
        i, ps, freed = bank()
        m = T(lambda e, ps=ps: e.matmul(ps[:, 0:1], small[0:1, 3, :], ones[0:1, 0:1], start=True, stop=True), freed, c)
        c = V(lambda e, ps=ps: e.tensor_copy(small[:, 0, 1:2], ps[:, 0:1]), m)
        reader[i] = c
        run2 = V(lambda e: e.tensor_tensor_scan(prev, seg, runs, small[:, 0, 1:2], ALU.add, ALU.max), c)
        back = runs[:, :].rearrange("p (r k h) -> p k r h", r=SCAN_ROWS, k=SCAN_TILES)
        for k in range(SCAN_TILES):
            i, ps, freed = bank()
            m = T(lambda e, ps=ps, k=k: e.transpose(ps[:, 0:P], prev[:, k * P:(k + 1) * P], ident[:, :]), freed, run2)
            got = V(lambda e, ps=ps, k=k: e.tensor_copy(back[:, k, :, :], ps[:, 0:P].rearrange("p (r h) -> p r h", h=HEADS)), m)
            reader[i] = got
        w_run = pr.dma("sp", s_tab, t_run.rearrange("(p t) h -> p (t h)", p=P), runs, got)
        pos, pos_hi = small[:, 0, 0:NODE_TILES], small[:, 1, 0:NODE_TILES]
        pos_i, hi_i = small[:, 2, 0:NODE_TILES].bitcast(I32), small[:, 3, 0:NODE_TILES].bitcast(I32)
        t = V(lambda e: e.tensor_scalar(pos, ends[:, :], 1.0, 0.0, ALU.subtract, ALU.max), got)
        t = V(lambda e: e.tensor_copy(pos_i, pos), t)
        t = V(lambda e: e.tensor_scalar(hi_i, pos_i, 7, None, ALU.arith_shift_right), t)
        t = V(lambda e: e.tensor_copy(pos_hi, hi_i), t)
        t = V(lambda e: e.scalar_tensor_tensor(out=pos, in0=pos_hi, scalar=-float(P), in1=pos, op0=ALU.mult, op1=ALU.add), t)
        t = V(lambda e: e.scalar_tensor_tensor(out=pos, in0=pos, scalar=float(EDGE_TILES), in1=pos_hi, op0=ALU.mult, op1=ALU.add), t)
        last_row = V(lambda e: e.tensor_copy(pos_i, pos), t)
        mx = tmp[:, 0, 0:NODE_TILES * HEADS]
        mx3 = mx.rearrange("p (t h) -> p t h", h=HEADS)
        s_last = pr.sem("segment_max_landed")

        def gather_last(e):
            e.wait_ge(*w_run)
            e.wait_ge(*last_row)
            for j in range(NODE_TILES):
                e.indirect_dma_start(out=mx[:, j * HEADS:(j + 1) * HEADS], out_offset=None, in_=t_run,
                                     in_offset=bass.IndirectOffsetOnAxis(ap=pos_i[:, j:j + 1], axis=0)).then_inc(s_last, 16)

        pr.queue["pool"].append(gather_last)
        g_last = (s_last, 16 * NODE_TILES)
        nh = [P, NODE_TILES, HEADS]
        ad3, m3 = am[:, 0:NODE_TILES, 0:HEADS], am[:, 0:NODE_TILES, HEADS:2 * HEADS]
        z3 = tmp[:, 1, 0:NODE_TILES * HEADS].rearrange("p (t h) -> p t h", h=HEADS)
        t = V(lambda e: e.memset(am[:, :, :], 0.0))
        t = V(lambda e: e.tensor_copy(ad3, a_dst[:, :, :]), t)
        t = V(lambda e: e.tensor_tensor(mx3, mx3, mask[:, :].unsqueeze(2).broadcast_to(nh), ALU.mult), g_last, t)
        t = V(lambda e: e.tensor_tensor(mx3, mx3, maskb[:, :].unsqueeze(2).broadcast_to(nh), ALU.add), t)
        t = V(lambda e: e.tensor_tensor(mx3, mx3, a_src[:, :, :], ALU.max), t)
        t = V(lambda e: e.tensor_tensor(mx3, mx3, a_dst[:, :, :], ALU.add), t)
        t = V(lambda e: e.scalar_tensor_tensor(out=m3, in0=mx3, scalar=0.2, in1=mx3, op0=ALU.mult, op1=ALU.max), t)
        u = V(lambda e: e.tensor_tensor(z3, a_src[:, :, :], a_dst[:, :, :], ALU.add), t)
        u = V(lambda e: e.scalar_tensor_tensor(out=z3, in0=z3, scalar=0.2, in1=z3, op0=ALU.mult, op1=ALU.max), u)
        u = V(lambda e: e.tensor_tensor(z3, z3, m3, ALU.subtract), u)
        ps_tok = A(lambda e: e.activation(p_self[:, :, :], z3, ACT.Exp), u)
        w_am = pr.dma("sp", s_tab, t_am.rearrange("(t p) h -> p t h", p=P), am[:, :, :], t)

        xt_mem = xT[:, :, :].rearrange("p k n -> p (k n)")
        hot_T = xt_mem[:, 0:UNROLL * P].rearrange("p (k n) -> p k n", n=P)
        dst_row = xt_mem[:, UNROLL * P:2 * UNROLL * P].bitcast(I32)
        node_at = src_hi
        c3 = control_dst[:, :].rearrange("p (t c) -> p t c", c=CONTROL)
        t = V(lambda e: e.tensor_copy(node_at[:, :].rearrange("p (t k) -> p t k", k=UNROLL), c3[:, :, 0:UNROLL]))
        node_ok = V(lambda e: e.tensor_scalar(node_at[:, :], node_at[:, :], part[:, 0:1], None, ALU.add), t)
        s_dst_row = pr.sem("dst_row_landed")
        s_hot_T = pr.sem("transposed_onehot_built")
        s_window = [pr.sem(f"window_landed{k}") for k in range(UNROLL)]
        s_expanded = pr.sem("window_multiplied")
        s_step = pr.sem("exponent_step")
        s_z = pr.sem("exponents_made")
        s_p = pr.sem("edge_weights_made")
        bank_exp = psum[4]
        pr.queue["pe"].append(lambda e, read=reader[4]: e.wait_ge(*read))
        seen = bank_exp[:, 0:UNROLL * 2 * HEADS].rearrange("p (t h) -> p t h", h=2 * HEADS)

        class Attention:

            def expand(self, e, j):
                e.wait_ge(s_dst_row, j * 16 + 16)
                if not (isinstance(j, int) and j == 0):
                    e.wait_ge(s_expanded, j * UNROLL)
                e.tensor_tensor(hot_T, dst_row.rearrange("p (k n) -> p k n", n=P),
                                node_at[:, bass.ds(j * UNROLL, UNROLL)].unsqueeze(2).broadcast_to([P, UNROLL, P]),
                                ALU.is_equal).then_inc(s_hot_T, 1)

            def multiply(self, e, j):
                e.wait_ge(s_hot_T, j + 1)
                if not (isinstance(j, int) and j == 0):
                    e.wait_ge(s_z, j)
                for k in range(UNROLL):
                    e.wait_ge(s_window[k], j * 16 + 16)
                    e.matmul(bank_exp[:, k * 2 * HEADS:(k + 1) * 2 * HEADS], hot_T[:, k, :], window[:, k, :],
                             start=True, stop=True).then_inc(s_expanded, 1)

            def exponents(self, e, j):
                z = p_all[:, bass.ds(j * (UNROLL * HEADS), UNROLL * HEADS)].rearrange("p (t h) -> p t h", h=HEADS)
                e.wait_ge(s_expanded, j * UNROLL + UNROLL)
                e.tensor_tensor(z, z, seen[:, :, 0:HEADS], ALU.add).then_inc(s_step, 1)
                e.wait_ge(s_step, j * 3 + 1)
                e.scalar_tensor_tensor(out=z, in0=z, scalar=0.2, in1=z, op0=ALU.mult, op1=ALU.max).then_inc(s_step, 1)
                e.wait_ge(s_step, j * 3 + 2)
                e.tensor_tensor(z, z, seen[:, :, HEADS:2 * HEADS], ALU.subtract).then_inc(s_step, 1)
                e.wait_ge(s_step, j * 3 + 3)
                e.tensor_scalar(z, z, 0.0, None, ALU.min).then_inc(s_z, 1)

            def weigh(self, e, i, g, place):
                e.wait_ge(s_p, i + 1)
                n = GROUP * HEADS
                rows3 = place.rearrange("p k (h c) -> p (k h) c", c=HEAD_ROW)
                p = p_all[:, bass.ds(i * (UNROLL * HEADS) + g * n, n)]
                return e.tensor_tensor(rows3, rows3, p.unsqueeze(2).broadcast_to([P, n, HEAD_ROW]), ALU.mult)

        def attention_sp(e):
            regs = [e.alloc_register(f"window_row{k}") for k in range(UNROLL)]
            e.wait_ge(*w_am)

            def windows(j):
                e.load(regs, control_dst[0:1, bass.ds(j * CONTROL, UNROLL)])
                at = [e.snap(r, min_val=0, max_val=PADDED_NODES) for r in regs]
                for k in range(UNROLL):
                    if not (isinstance(j, int) and j == 0):
                        e.wait_ge(s_expanded, j * UNROLL + (k + 1 - UNROLL))
                    e.dma_start(window[:, k, :], t_am[bass.ds(at[k], P), :]).then_inc(s_window[k], 16)

            windows(0)
            with e.Fori(1, TURNS) as j:
                windows(j)

        def attention_act(e):
            def load(j):
                e.dma_start(dst_row, a["dst_run"][0:1, bass.ds(j * (UNROLL * P) + 1, UNROLL * P)]
                            .broadcast_to([P, UNROLL * P])).then_inc(s_dst_row, 16)

            def exp(j):
                e.wait_ge(s_z, j + 1)
                z = p_all[:, bass.ds(j * (UNROLL * HEADS), UNROLL * HEADS)]
                e.activation(z, z, ACT.Exp).then_inc(s_p, 1)

            e.wait_ge(*xt_free)
            load(0)
            with e.Fori(0, TURNS - 1) as j:
                e.wait_ge(s_hot_T, j + 1)
                load(j + 1)
                exp(j)
            exp(TURNS - 1)

        xt_free = tok_h_pe
        pr.queue["sp"].append(attention_sp)
        pr.queue["act"].append(attention_act)
        pr.queue["pe"].append(lambda e: e.wait_ge(*node_ok))
        pr.queue["dve"].append(lambda e: (e.wait_ge(*node_ok), e.wait_ge(*w_run), e.wait_ge(*g_as)))
        pass_done = edge_pass(t_h, w_h, by_dst, width=ATT_ROW, planes=3, attention=Attention())

        def attended(j):
            i, ps, freed = bank()
            for c in range(3):
                m = T(lambda e, ps=ps, j=j, c=c: e.transpose(ps[:, c * P:(c + 1) * P], agg[:, c, j * P:(j + 1) * P], ident[:, :]),
                      freed, pass_done)
            o = h_rows[:, j, :, :]
            of = own[:, j, :]
            s = j % 4
            t = V(lambda e, j=j, o=o: e.tensor_tensor(o, o, p_self[:, j, :].unsqueeze(2).broadcast_to([P, HEADS, HEAD_ROW]), ALU.mult),
                  ps_tok, w_h)
            V(lambda e, of=of, ps=ps: e.tensor_tensor(of[:, 0:DIM], of[:, 0:DIM], ps[:, 0:DIM], ALU.add), m, t)
            t = V(lambda e, of=of, ps=ps: e.tensor_tensor(of[:, DIM:ATT_ROW], of[:, DIM:ATT_ROW], ps[:, 3 * P - HEADS:3 * P], ALU.add))
            reader[i] = t
            t = V(lambda e, j=j, o=o: e.tensor_scalar(a_dst[:, j, :], o[:, :, HEAD_DIM], 1e-16, None, ALU.add), t)
            t = V(lambda e, j=j: e.reciprocal(a_dst[:, j, :], a_dst[:, j, :]), t)
            t = V(lambda e, j=j, o=o, s=s: e.tensor_tensor(heads(tmp[:, s, 0:DIM]), o[:, :, 0:HEAD_DIM],
                                                    a_dst[:, j, :].unsqueeze(2).broadcast_to([P, HEADS, HEAD_DIM]), ALU.mult), t)
            t = V(lambda e, of=of, s=s: e.tensor_tensor(of[:, 0:DIM], tmp[:, s, 0:DIM], brow[:, B_ATT, :], ALU.add), t)
            t = V(lambda e, j=j, of=of: e.bn_stats(stats[:, j, :], of[:, 0:DIM]), t)
            return V(lambda e, j=j: e.bn_aggr(mv[:, j, :], stats[:, j, :]), t)

        for j in range(NODE_TILES):
            t = attended(j)
        r = inverse_std(t)

        def y3(j):
            o = own[:, j, 0:DIM]
            t = V(lambda e, j=j, o=o: e.scalar_tensor_tensor(out=o, in0=o, scalar=mv[:, j, 0:1], in1=brow[:, B_GAMMA, :],
                                                        op0=ALU.subtract, op1=ALU.mult), r)
            t = V(lambda e, j=j, o=o: e.scalar_tensor_tensor(out=o, in0=o, scalar=rstd[:, j:j + 1], in1=brow[:, B_BETA, :],
                                                        op0=ALU.mult, op1=ALU.add), t)
            return V(lambda e, j=j, o=o: e.tensor_tensor(x[:, j, :], x[:, j, :], o, ALU.add), t)

        def store(j, tok):
            n = tile_rows(j)
            pr.dma("sp" if j % 2 else "act", s_out, out[j * P:j * P + n, :], x[0:n, j, :], tok)

        layer_norm(y3, store)
        for e in ("sp", "act"):
            pr.queue[e].append(lambda g: g.wait_ge(s_out, 16 * NODE_TILES))
        pr.queue["sp"].append(lambda g: g.wait_ge(s_tab, pr.count[s_tab.name]))

        block = stack.enter_context(nc.Block())
        pr.run(block)


STAGE_SEMS = {}


def stage_sem(pr, k):
    key = (id(pr), k)
    if key not in STAGE_SEMS:
        STAGE_SEMS[key] = pr.sem(f"stage_written{k}")
    return STAGE_SEMS[key]


class AllStaged:
    pass


def all_staged(pr, staged):
    toks = list(staged.values())
    done = pr.done["sp"]
    pr.count[done.name] = pr.count.get(done.name, 0) + 1

    def emit(eng):
        for s, v in toks:
            eng.wait_ge(s, v)
        eng.sem_inc(done, 1)

    pr.queue["sp"].append(emit)
    return done, pr.count[done.name]


def kernel(**inputs):
    import concourse.bacc as bacc
    from concourse.bass_utils import run_bass_kernel_spmd as run

    arr = {n: np.asarray(v) for n, v in inputs.items()}

    def tiled(v, fill):
        flat = np.full((PADDED_EDGES,), fill, v.dtype)
        flat[:EDGES] = v
        return np.ascontiguousarray(flat.reshape(EDGE_TILES, P).T)

    def t(v):
        return np.ascontiguousarray(np.swapaxes(v, -1, -2))

    x_rows = np.zeros((PADDED_NODES, DIM), arr["x"].dtype)
    x_rows[:NODES] = arr["x"]
    src_run, dst_run = (np.full((1, PADDED_EDGES + 1), PAD_NODE, arr[n].dtype) for n in ("src", "dst"))
    for run_of, n in ((src_run, "src"), (dst_run, "dst")):
        run_of[0, 0] = -1
        run_of[0, 1:EDGES + 1] = arr[n]
    data = {
        "x": x_rows,
        "src_t": tiled(arr["src"], PAD_NODE),
        "dst_t": tiled(arr["dst"], PAD_NODE),
        "w_t": tiled(arr["edge_weight"], 0),
        "src_run": src_run, "dst_run": dst_run,
        "w1l": t(arr["L0_gnn_W1l"]), "w1r": t(arr["L0_gnn_W1r"]),
        "w2l": t(arr["L0_gnn_W2l"]), "w2r": t(arr["L0_gnn_W2r"]),
        "b1": t(arr["L0_gnn_b1l"].reshape(K_HID, P)),
        "b2": arr["L0_gnn_b2l"].reshape(1, DIM),
        "wn": t(arr["L1_gnn_Wn"]), "ws": t(arr["L1_gnn_Ws"]),
        "bn": arr["L1_gnn_bn"], "bs": arr["L1_gnn_bs"],
        "l2w1": arr["L2_gnn_W1"], "l2w2": arr["L2_gnn_W2"], "l2b": arr["L2_gnn_b"].reshape(1, DIM),
        "l3w": arr["L3_gnn_W"],
        "att_src": arr["L3_gnn_att_src"].reshape(1, DIM), "att_dst": arr["L3_gnn_att_dst"].reshape(1, DIM),
        "l3bias": arr["L3_gnn_bias"].reshape(1, DIM),
        "gamma": arr["L3_gnn_ln_gamma"].reshape(1, DIM), "beta": arr["L3_gnn_ln_beta"].reshape(1, DIM),
    }
    nc = bacc.Bacc("TRN2", target_bir_lowering=False, num_devices=1)
    aps = {n: nc.dram_tensor(n, v.shape, mybir.dt.from_np(v.dtype), kind="ExternalInput").ap()
           for n, v in data.items()}
    out = nc.dram_tensor("out", (NODES, DIM), F32, kind="ExternalOutput").ap()
    residual_gnn(nc, aps, out)
    r = run(nc, [data], core_ids=[0])
    return r.results[0]["out"]
```

```python
from contextlib import ExitStack

import numpy as np
import concourse.bass as bass
from concourse import mybir

F32 = mybir.dt.float32
BF16 = mybir.dt.bfloat16
I32 = mybir.dt.int32
ALU = mybir.AluOpType
ACT = mybir.ActivationFunctionType
AX_X = mybir.AxisListType.X

P = 128
NODES = 3125
EDGES = 53125
DIM = 256
HIDDEN = 512
HOPS = 3
HEADS = 8
HEAD_DIM = DIM // HEADS
HEAD_ROW = HEAD_DIM + 1
ATT_ROW = HEADS * HEAD_ROW
NODE_TILES = -(-NODES // P)
TILES_AT_ONCE = 4
PADDED_NODES = NODE_TILES * P
LAST_ROWS = NODES - (NODE_TILES - 1) * P
WINDOWED_NODES = PADDED_NODES + P
EDGE_TILES = 416
PADDED_EDGES = EDGE_TILES * P
UNROLL = 8
RING_TURNS = 4
GROUP = 4
GROUPS = UNROLL // GROUP
TURNS = EDGE_TILES // UNROLL
GATHERED_TURNS = 22
CONTROL = UNROLL + GROUPS
SCAN_ROWS = P // HEADS
SCAN_TILES = EDGE_TILES // SCAN_ROWS
SCAN_LEN = SCAN_TILES * P
PAD_NODE = PADDED_NODES - 1
RECORD = 4
BIG = 1.0e30
LN_EPS = 1e-5
K_IN = DIM // P
K_HID = HIDDEN // P


class Program:

    ENGINES = ("pe", "dve", "act", "pool", "sp")

    def __init__(self, nc, stack):
        self.nc, self.stack = nc, stack
        self.queue = {e: [] for e in self.ENGINES}
        self.done = {e: stack.enter_context(nc.semaphore(f"done_{e}")) for e in self.ENGINES}
        self.count = {}

    def sem(self, name):
        return self.stack.enter_context(self.nc.semaphore(name))

    def op(self, e, fn, *waits, sem=None, by=1):
        sem = self.done[e] if sem is None else sem
        self.count[sem.name] = self.count.get(sem.name, 0) + by
        waits = [w for w in waits if w is not None]

        def emit(eng):
            for s, v in waits:
                eng.wait_ge(s, v)
            fn(eng).then_inc(sem, by)

        self.queue[e].append(emit)
        return sem, self.count[sem.name]

    def dma(self, e, sem, out, in_, *waits):
        return self.op(e, lambda eng: eng.dma_start(out, in_), *waits, sem=sem, by=16)

    def last(self, e):
        return self.done[e], self.count.get(self.done[e].name, 0)

    def run(self, block):
        names = dict(pe=block.tensor, dve=block.vector, act=block.scalar, pool=block.gpsimd, sp=block.sync)
        for e, deco in names.items():
            def body(eng, e=e):
                for emit in self.queue[e]:
                    emit(eng)
            deco(body)


def residual_gnn(nc, a, out):
    with ExitStack() as stack:
        pr = Program(nc, stack)

        def sb(name, shape, dt=F32):
            return stack.enter_context(nc.sbuf_tensor(name, shape, dt))

        x = sb("x_nodes", [P, NODE_TILES, DIM])
        xT = sb("x_features", [P, K_IN, PADDED_NODES])
        agg = sb("aggregate", [P, 3, WINDOWED_NODES])
        own = sb("own_term", [P, NODE_TILES, ATT_ROW])
        rows = sb("gathered_rows", [P, UNROLL, ATT_ROW])
        onehot = sb("edge_to_window", [P, UNROLL, P])
        src_lo_hot = sb("src_lo_onehot", [P, UNROLL, P], BF16)
        hi_hot = [sb(f"src_hi_onehot{b}", [P, UNROLL, 32], BF16) for b in range(2)]
        w_a = sb("weights_a", [P, 2048])
        w_b = sb("weights_b", [P, K_HID, 2 * DIM])
        w_c = sb("weights_c", [P, HOPS, 2, K_IN, DIM])
        hidden = sb("hidden", [P, 2 * K_HID * 512])
        tmp = sb("tmp", [P, 4, ATT_ROW])
        stage = tmp
        src = sb("src", [P, EDGE_TILES], I32)
        src_i = hidden[:, 0:EDGE_TILES].bitcast(I32)
        src_lo = sb("src_lo", [P, EDGE_TILES])
        src_hi = sb("src_hi", [P, EDGE_TILES])
        dst = sb("dst", [P, EDGE_TILES], I32)
        base = sb("window_base", [P, EDGE_TILES], I32)
        control_dst, control_src = (sb(f"control_by_{n}", [P, TURNS * CONTROL], I32) for n in ("dst", "src"))
        local = sb("dst_in_window", [P, EDGE_TILES])
        weight = sb("edge_weight", [P, EDGE_TILES])
        iota_i = hidden[:, EDGE_TILES:EDGE_TILES + P].bitcast(I32)
        iota = sb("iota", [P, P])
        part_i = sb("partition_i", [P, 1], I32)
        part = sb("partition", [P, 1])
        ident = sb("identity", [P, P])
        ones = sb("ones", [P, P])
        zeros_b = sb("zeros_bf16", [P, P], BF16)
        b1 = sb("bias_hidden", [P, K_HID])
        brow = sb("bias_rows", [P, 8, DIM])
        B_HID2, B_HOP, B_L2, B_ATT, B_GAMMA, B_BETA = 0, 1, 4, 5, 6, 7
        att = sb("attention_vectors", [P, 2, K_IN])
        head_of = sb("head_of_feature", [P, K_IN])
        att_heads = sb("attention_by_head", [P, K_IN, 2 * HEADS])
        stats = sb("ln_stats", [P, NODE_TILES, 6])
        mv = sb("ln_mean_var", [P, NODE_TILES, 2])
        rstd = sb("ln_rstd", [P, NODE_TILES])
        out_cnt = sb("out_count", [P, NODE_TILES])
        eps = sb("eps", [P, 1])
        in_cnt = sb("in_count", [P, NODE_TILES])
        rcnt = sb("inverse_count", [P, NODE_TILES])
        mask = sb("has_edges", [P, NODE_TILES])
        maskb = sb("no_edge_bias", [P, NODE_TILES])
        ends = sb("segment_end", [P, NODE_TILES])
        rdeg = sb("inverse_root_degree", [P, NODE_TILES])
        sq = sb("squares", [P, NODE_TILES])
        late, at = w_c[:, :, :, :, :].rearrange("p a b c d -> p (a b c d)"), [0]

        def part_of_late(n, pattern, **dims):
            lo = at[0]
            at[0] += n
            return late[:, lo:lo + n].rearrange(pattern, **dims)

        a_both = part_of_late(2 * NODE_TILES * HEADS, "p (r t h) -> p r t h", r=2, h=HEADS)
        a_src, a_dst = a_both[:, 0, :, :], a_both[:, 1, :, :]
        p_self = part_of_late(NODE_TILES * HEADS, "p (t h) -> p t h", h=HEADS)
        am = part_of_late((NODE_TILES + 1) * 2 * HEADS, "p (t h) -> p t h", h=2 * HEADS)
        small = part_of_late(4 * P, "p (a b) -> p a b", b=P)
        window = part_of_late(UNROLL * 2 * HEADS, "p (k h) -> p k h", h=2 * HEADS)

        sort_mem, sort_at = w_c[:, :, :, :, :].rearrange("p a b c d -> p (a b c d)"), [0]

        def part_of_sort(n):
            lo = sort_at[0]
            sort_at[0] += n
            return sort_mem[:, lo:lo + n]

        before_tile = [part_of_sort((UNROLL + 1) * NODE_TILES) for _ in range(2)]
        earlier = part_of_sort(P)
        triangle = earlier
        unread = [part_of_sort(P)]
        picked = part_of_sort(UNROLL * NODE_TILES)
        src_f, place_i = part_of_sort(EDGE_TILES), part_of_sort(EDGE_TILES).bitcast(I32)
        first_place, ranks = part_of_sort(NODE_TILES), part_of_sort(2 * UNROLL)
        place, place_lo, place_hi = (part_of_sort(UNROLL) for _ in range(3))

        psum = [stack.enter_context(nc.psum_tensor(f"bank{i}", [P, 512], F32)) for i in range(8)]

        def dram(name, r, c):
            return nc.dram_tensor(name, (r, c), F32, kind="Internal").ap()

        t_u = dram("table_hidden", PADDED_NODES, DIM)
        t_x = [dram(f"table_hop{i}", PADDED_NODES, DIM) for i in range(HOPS)]
        t_g = dram("table_scaled", PADDED_NODES, DIM)
        t_h = dram("table_heads", PADDED_NODES, ATT_ROW)
        t_as = dram("table_a_src", PADDED_NODES, HEADS)
        t_am = dram("table_a_dst_max", WINDOWED_NODES, 2 * HEADS)
        t_sort = nc.dram_tensor("table_edges_by_src", (PADDED_EDGES, RECORD), I32, kind="Internal").ap()
        t_run = dram("table_running_max", P * EDGE_TILES, HEADS)

        s_row = [pr.sem(f"rows_landed{k}") for k in range(RING_TURNS * UNROLL)]
        row_rounds = [0] * RING_TURNS
        s_hot = pr.sem("onehot_built")
        s_mm = pr.sem("tile_multiplied")
        s_acc = pr.sem("tile_accumulated")
        s_load = [pr.sem(f"{n}_loaded") for n in ("edges", "features")]
        s_tab = pr.sem("table_written")
        s_out = pr.sem("output_written")
        passes = [0]
        spare_rows = [w_a[:, 0:GROUP * ATT_ROW],
                      w_b[:, :, :].rearrange("p a b -> p (a b)")[:, 0:GROUP * ATT_ROW]]
        spare_rows += [xT[:, :, :].rearrange("p k n -> p (k n)")[:, 2 * UNROLL * P + g * GROUP * ATT_ROW:
                                                                 2 * UNROLL * P + (g + 1) * GROUP * ATT_ROW]
                       for g in range(RING_TURNS * GROUPS - GROUPS - len(spare_rows))]

        def tile_rows(j):
            return LAST_ROWS if j == NODE_TILES - 1 else P

        turn, reader, counting = [0], {}, [False]

        def bank():
            turn[0] += 1
            if counting[0] and turn[0] % 8 == 7:
                turn[0] += 1
            i = turn[0] % 8
            return i, psum[i], reader.get(i)

        V = lambda fn, *w: pr.op("dve", fn, *w)
        A = lambda fn, *w: pr.op("act", fn, *w)
        T = lambda fn, *w: pr.op("pe", fn, *w)

        pr.op("pool", lambda e: e.iota(iota_i, [[1, P]], base=0, channel_multiplier=0))
        c_iota = pr.op("pool", lambda e: e.iota(part_i[:, :], [[0, 1]], base=0, channel_multiplier=1))
        l_edge = None
        for o, i in ((src[:, :], a["src_t"]), (dst[:, :], a["dst_t"]), (weight[:, :], a["w_t"]),
                     (base[:, :], a["dst_t"][0:1, :].broadcast_to([P, EDGE_TILES]))):
            l_edge = pr.dma("sp", s_load[0], o, i)
        l_x = pr.dma("act", s_load[1], x[:, :, :], a["x"].rearrange("(t p) d -> p t d", p=P))
        s_w = pr.sem("weights_loaded")
        load_weights = lambda o, i: pr.dma("sp", s_w, o, i)
        w_a4 = w_a[:, :].rearrange("p (s k n) -> p s k n", s=2, k=K_IN)
        for s, n in enumerate(("w1l", "w1r")):
            load_weights(w_a4[:, s, :, :], a[n].rearrange("(k p) n -> p k n", p=P))
        for s, n in enumerate(("w2l", "w2r")):
            load_weights(w_b[:, :, s * DIM:(s + 1) * DIM], a[n].rearrange("(k p) n -> p k n", p=P))
        load_weights(b1[:, :], a["b1"])
        for r, n in ((B_HID2, "b2"), (B_L2, "l2b"), (B_ATT, "l3bias"), (B_GAMMA, "gamma"), (B_BETA, "beta")):
            load_weights(brow[:, r, :], a[n].broadcast_to([P, DIM]))
        for h in range(HOPS):
            load_weights(brow[:, B_HOP + h, :], a["bn"][h:h + 1, :].broadcast_to([P, DIM]))
            load_weights(own[:, h, 0:DIM], a["bs"][h:h + 1, :].broadcast_to([P, DIM]))
        for r, n in enumerate(("att_src", "att_dst")):
            l_w = load_weights(att[:, r, :], a[n])

        V(lambda e: e.tensor_copy(iota[:, :], iota_i), c_iota)
        c2 = V(lambda e: e.tensor_copy(part[:, :], part_i[:, :]))
        c_id = V(lambda e: e.tensor_scalar(ident[:, :], iota[:, :], part[:, 0:1], None, ALU.is_equal), c2)
        c_one = V(lambda e: e.memset(ones[:, :], 1.0))
        c_zb = V(lambda e: e.memset(zeros_b[:, :], 0.0))
        V(lambda e: e.memset(eps[:, :], LN_EPS))

        def place_windows(control, nodes, first, positions, ready):
            by_group = [P, EDGE_TILES // GROUP, GROUP]
            g3 = lambda ap: ap.rearrange("p (g k) -> p g k", k=GROUP)
            head = g3(first)[:, :, 0:1]
            wide, mixed = hidden[:, 0:EDGE_TILES // GROUP], hidden[:, P:P + EDGE_TILES]
            n = EDGE_TILES // GROUP
            t = V(lambda e: e.tensor_tensor(wide[:, 0:n - 1], g3(first)[:, 1:n, 0], g3(first)[:, 0:n - 1, 0], ALU.subtract), ready)
            V(lambda e: e.tensor_scalar(wide[:, n - 1:n], g3(first)[:, n - 1, 0:1], -1.0, float(PAD_NODE), ALU.mult, ALU.add), ready)
            t = V(lambda e: e.tensor_scalar(wide, wide, float(P), None, ALU.is_ge), pr.last("dve"))
            t = V(lambda e: e.tensor_tensor(g3(mixed), g3(first), head.broadcast_to(by_group), ALU.subtract), t)
            t = V(lambda e: e.tensor_tensor(g3(mixed), g3(mixed), wide.unsqueeze(2).broadcast_to(by_group), ALU.mult), t)
            t = V(lambda e: e.tensor_tensor(g3(mixed), g3(mixed), head.broadcast_to(by_group), ALU.add), t)
            c3 = control[:, :].rearrange("p (t c) -> p t c", c=CONTROL)
            V(lambda e: e.tensor_tensor(positions, nodes, mixed, ALU.subtract), t)
            V(lambda e: e.tensor_copy(c3[:, :, 0:UNROLL], mixed.rearrange("p (t k) -> p t k", k=UNROLL)), t)
            return V(lambda e: e.tensor_copy(c3[:, :, UNROLL:CONTROL], wide.rearrange("p (t k) -> p t k", k=GROUPS)), t)

        s1 = V(lambda e: e.tensor_scalar(src_i, src[:, :], 7, None, ALU.arith_shift_right), l_edge)
        s2 = V(lambda e: e.tensor_copy(src_hi[:, :], src_i), s1)
        V(lambda e: e.scalar_tensor_tensor(out=src_lo[:, :], in0=src_hi[:, :], scalar=-float(P), in1=src[:, :],
                                           op0=ALU.mult, op1=ALU.add), s2)
        c_edges = V(lambda e: e.tensor_tensor(brow[:, B_HOP:B_HOP + HOPS, :], brow[:, B_HOP:B_HOP + HOPS, :],
                                              own[:, 0:HOPS, 0:DIM], ALU.add), l_w)

        base_f = hidden[:, 1024:1024 + EDGE_TILES]
        bf = V(lambda e: e.tensor_copy(base_f, base[:, :]), l_edge)
        c_edges = place_windows(control_dst, dst[:, :], base_f, local[:, :], bf)

        pr.queue["pe"].append(lambda e: e.sem_inc(s_mm, UNROLL))
        pr.queue["dve"].append(lambda e: e.sem_inc(s_acc, 2 * GROUP))

        def transposes(read, ready):
            tok = None
            free = pr.last("pe")
            for j in range(NODE_TILES):
                i, ps, freed = bank()
                t = read(j)
                T(lambda e, ps=ps, t=t: e.transpose(ps[:, 0:P], t[:, 0:P], ident[:, :]), freed, ready(j), c_id)
                m = T(lambda e, ps=ps, t=t: e.transpose(ps[:, P:2 * P], t[:, P:2 * P], ident[:, :]))
                tok = A(lambda e, ps=ps, j=j: e.copy(xT[:, :, j * P:(j + 1) * P],
                                                     ps[:, 0:DIM].rearrange("p (k n) -> p k n", k=K_IN)), m, free)
                reader[i] = tok
            return tok

        TURN_BANK, OWN_BANK = 4, 5

        def edge_pass(table, ready, edges, width=DIM, planes=K_IN, count_in=False, count_out=False, after=None,
                      attention=None, beside=None, other_gathers=None):
            index, position, weight, control = edges
            n = passes[0]
            passes[0] += 1
            mm0, acc0, hot0 = UNROLL + n * EDGE_TILES, 2 * GROUP + n * EDGE_TILES, n * EDGE_TILES
            att = attention
            places = [rows[:, g * GROUP:(g + 1) * GROUP, :] for g in range(GROUPS)]
            if att is not None:
                places += [w.rearrange("p (k c) -> p k c", c=ATT_ROW) for w in spare_rows]
            ring = len(places) * GROUP
            slot = lambda k: places[k // GROUP][:, k % GROUP, :]
            half = ring // UNROLL

            def landed(e, i, k):
                e.wait_ge(s_row[i[1] * UNROLL + k], i[0] * 16 + (16 * rounds[i[1]] + 16))

            rounds = [row_rounds[h] for h in range(half)]
            for h in range(half):
                row_rounds[h] += TURNS // half

            def pool(e):
                e.wait_ge(*ready)
                e.wait_ge(*c_edges)
                if after is not None:
                    e.wait_ge(*after)
                for t in range(EDGE_TILES):
                    if t == 2 * UNROLL and other_gathers is not None:
                        other_gathers(e)
                    e.wait_ge(s_mm, mm0 + max(t - ring + 1, 1 - UNROLL))
                    e.indirect_dma_start(out=slot(t % ring)[:, 0:width], out_offset=None, in_=table,
                                         in_offset=bass.IndirectOffsetOnAxis(ap=index[:, t:t + 1], axis=0)
                                         ).then_inc(s_row[t % ring], 16)

            pr.queue["pool"].append(pool)

            banks_read = [reader[b] for b in range(2 * GROUPS) if b in reader]
            pr.queue["pe"].append(lambda e: [e.wait_ge(*w) for w in banks_read])
            agg_read = pr.last("pe")
            zeroed = V(lambda e: e.memset(agg[:, 0:planes, :], 0.0), agg_read, c_edges)

            def onehots(e, i, g, at_row):
                lo, hi = g * GROUP, (g + 1) * GROUP
                if not (isinstance(i, int) and i == 0 and n == 0):
                    e.wait_ge(s_mm, i * UNROLL + (mm0 - UNROLL + hi))
                cols = bass.ds(i * UNROLL + lo, GROUP)
                if count_out:
                    e.tensor_tensor(src_lo_hot[:, lo:hi, :], iota[:, :].unsqueeze(1).broadcast_to([P, GROUP, P]),
                                    src_lo[:, cols].unsqueeze(2).broadcast_to([P, GROUP, P]), ALU.is_equal)
                    e.tensor_tensor(hi_hot[0][:, lo:hi, 0:NODE_TILES],
                                    iota[:, 0:NODE_TILES].unsqueeze(1).broadcast_to([P, GROUP, NODE_TILES]),
                                    src_hi[:, cols].unsqueeze(2).broadcast_to([P, GROUP, NODE_TILES]),
                                    ALU.is_equal).then_inc(s_hist, GROUP)
                if weight is not None:
                    for k in range(lo, hi):
                        col = bass.ds(i * UNROLL + k, 1)
                        e.tensor_scalar(onehot[:, k, :], iota[:, :], position[:, col], weight[:, col],
                                        ALU.is_equal, ALU.mult).then_inc(s_hot, 1)
                    return
                hot = e.tensor_tensor(onehot[:, lo:hi, :], iota[:, :].unsqueeze(1).broadcast_to([P, GROUP, P]),
                                      position[:, cols].unsqueeze(2).broadcast_to([P, GROUP, P]), ALU.is_equal)
                if att is None:
                    hot.then_inc(s_hot, GROUP)
                else:
                    weigh(e, i, g, at_row).then_inc(s_hot, GROUP)

            def weigh(e, i, g, at_row):
                for k in range(g * GROUP, (g + 1) * GROUP):
                    landed(e, at_row, k)
                return att.weigh(e, i, g, places[at_row[1] * GROUPS + g])

            def each_turn(e, turn, with_turn=None):
                def one_round(q, last):
                    for h in range(half):
                        here = (q, h)
                        after = (q, h + 1) if h + 1 < half else (q + 1, 0)
                        turn(q * half + h, half - 1 - h if last else UNROLL, here, after)

                rounds_beside = 0 if beside is None else NODE_TILES
                if beside is not None:
                    with e.Fori(0, rounds_beside) as q:
                        before, behind = with_turn
                        before(e, q)
                        one_round(q, False)
                        behind(e, q)
                with e.Fori(rounds_beside, TURNS // half - 1) as q:
                    one_round(q, False)
                one_round(TURNS // half - 1, True)

            def dve_turn(e, i, regs, ahead, after):
                e.load(regs, control[0:1, bass.ds(i * CONTROL, CONTROL)])
                at = [e.snap(r, min_val=0, max_val=PADDED_NODES) for r in regs[0:UNROLL]]
                wide = [e.snap(r, min_val=0, max_val=1) for r in regs[UNROLL:CONTROL]]
                for g in range(GROUPS):
                    def add(k, tiles):
                        e.wait_ge(s_mm, i * UNROLL + (mm0 + k + tiles))
                        e.wait_ge(s_acc, i * UNROLL + (acc0 + k))
                        w = agg[:, 0:planes, bass.ds(at[k], P)]
                        bank_of = 2 * g + (k % 2 if tiles == 1 else 0)
                        s = psum[bank_of][:, 0:planes * P].rearrange("p (k n) -> p k n", k=planes)
                        e.tensor_tensor(w, w, s, ALU.add).then_inc(s_acc, tiles)

                    if att is not None and g == 1 and ahead > 1:
                        att.expand(e, i + 2)
                    with e.If(wide[g]):
                        for k in range(g * GROUP, (g + 1) * GROUP):
                            add(k, 1)
                    with e.Else():
                        add(g * GROUP, GROUP)
                    if ahead:
                        if att is not None and g == 0:
                            att.exponents(e, i + 1)
                        onehots(e, i + 1, g, after)

            def dve(e):
                regs = [e.alloc_register(f"control{n}_{k}") for k in range(CONTROL)]
                e.wait_ge(*zeroed)
                if att is not None:
                    att.expand(e, 0)
                    att.exponents(e, 0)
                for g in range(GROUPS):
                    onehots(e, 0, g, (0, 0))
                if att is not None:
                    att.expand(e, 1)
                each_turn(e, lambda i, ahead, here, after: dve_turn(e, i, regs, ahead, after),
                          beside and (lambda e, i: None, beside.dve))

            pr.queue["dve"].append(dve)

            if count_out:
                T(lambda e: e.matmul(psum[7][:, 0:NODE_TILES], zeros_b[:, :], zeros_b[:, 0:NODE_TILES], start=True,
                                     stop=False, skip_group_check=True), c_zb, reader.get(7))

            def pe_turn(e, i, regs, ahead, here):
                e.load(regs, control[0:1, bass.ds(i * CONTROL + UNROLL, GROUPS)])
                wide = [e.snap(r, min_val=0, max_val=1) for r in regs]
                for g in range(GROUPS):
                    def multiply(k, alone):
                        e.wait_ge(s_hot, i * UNROLL + (hot0 + k + 1))
                        landed(e, here, k)
                        row = slot(here[1] * UNROLL + k)
                        first = k % GROUP == 0
                        if first:
                            e.wait_ge(s_acc, i * UNROLL + (acc0 + k - GROUP))
                        elif alone and k % GROUP >= 2:
                            e.wait_ge(s_acc, i * UNROLL + (acc0 + k - 1))
                        ps = psum[2 * g + (k % 2 if alone else 0)]
                        if count_out:
                            e.wait_ge(s_hist, i * UNROLL + (k + 1))
                            e.matmul(psum[7][:, 0:NODE_TILES], src_lo_hot[:, k, :], hi_hot[0][:, k, 0:NODE_TILES],
                                     start=False, stop=False, skip_group_check=True)
                        cuts = [row[:, 0:P], row[:, P:2 * P]]
                        if count_in:
                            cuts.append(ones[:, :])
                        if att is not None:
                            cuts.append(row[:, ATT_ROW - P:ATT_ROW])
                        for c, lhs in enumerate(cuts):
                            m = e.matmul(ps[:, c * P:(c + 1) * P], lhs, onehot[:, k, :],
                                         start=(alone or first) and c == 0,
                                         stop=(alone or k % GROUP == GROUP - 1) and c == len(cuts) - 1,
                                         skip_group_check=True)
                        m.then_inc(s_mm, 1)

                    tiles = range(g * GROUP, (g + 1) * GROUP)
                    with e.If(wide[g]):
                        for k in tiles:
                            multiply(k, True)
                    with e.Else():
                        for k in tiles:
                            multiply(k, False)
                    if att is not None and g == 0 and ahead:
                        att.multiply(e, i + 1)

            def pe(e):
                regs = [e.alloc_register(f"wide{n}_{k}") for k in range(GROUPS)]
                e.wait_ge(*c_edges)
                if att is not None:
                    att.multiply(e, 0)
                each_turn(e, lambda i, ahead, here, after: pe_turn(e, i, regs, ahead, here),
                          beside and (beside.transpose, beside.multiply))

            pr.queue["pe"].append(pe)
            return s_acc, acc0 + EDGE_TILES

        def in_groups(*stages):
            in_order(*reversed(list(enumerate(stages))))

        def in_order(*stages):
            groups = [range(lo, min(lo + TILES_AT_ONCE, NODE_TILES)) for lo in range(0, NODE_TILES, TILES_AT_ONCE)]
            for s in range(len(groups) + max(behind for behind, _ in stages)):
                for behind, stage in stages:
                    if 0 <= s - behind < len(groups):
                        stage(groups[s - behind])

        tiles = lambda ap, g: ap[:, g[0]:g[-1] + 1]

        def mean_and_root(rows_of, g, ready):
            for j in g:
                V(lambda e, j=j: e.bn_stats(stats[:, j, :], rows_of(j)), ready)
            t = pr.last("dve")
            for j in g:
                t = V(lambda e, j=j: e.bn_aggr(mv[:, j, :], stats[:, j, :]), t)
            return A(lambda e: e.activation(tiles(rstd, g), tiles(mv, g)[:, :, 1], ACT.Sqrt, bias=eps[:, 0:1]), t)

        def normalize(g, root):
            r = V(lambda e: e.reciprocal(tiles(rstd, g), tiles(rstd, g)), root)
            return [V(lambda e, j=j: e.tensor_scalar(x[:, j, :], x[:, j, :], mv[:, j, 0:1], rstd[:, j:j + 1],
                                                     ALU.subtract, ALU.mult), r) for j in g]

        def write_rows(table, rows_of, g, ready):
            return pr.dma("sp", s_tab, table[g[0] * P:(g[-1] + 1) * P, :].rearrange("(t p) d -> p t d", p=P),
                          tiles(rows_of, g), ready)

        spare = xT[:, :, :].rearrange("p k n -> p (k n)").rearrange("p (t d) -> p t d", d=DIM)

        s_hist = pr.sem("src_onehot_built")
        by_dst = (src, local, None, control_dst)

        unit = ones[0:1, 0:1]

        words = agg[:, 2, :].bitcast(I32)
        record = words[:, 0:EDGE_TILES * RECORD].rearrange("p (t r) -> p t r", r=RECORD)
        sorted_words = words[:, EDGE_TILES * RECORD:2 * EDGE_TILES * RECORD]
        src_row_lo = [part_of_sort(UNROLL * P).bitcast(I32), sorted_words[:, 0:UNROLL * P]]
        unread += [sorted_words[:, n * P:(n + 1) * P].bitcast(F32) for n in (UNROLL, UNROLL + 1)]
        src_row = rows[:, :, :].rearrange("p a b -> p (a b)")[:, 0:2 * UNROLL * P].bitcast(I32)
        lo_T = onehot[:, :, :]
        s_src_row = [pr.sem(f"src_row_landed{k}") for k in range(2)]
        s_moved = pr.sem("records_moved")
        by_src_ok = [None]

        def make_records(free):
            t = V(lambda e: e.memset(record, 0), free)
            V(lambda e: e.tensor_copy(record[:, :, 0], dst[:, :]), t)
            V(lambda e: e.tensor_copy(record[:, :, 1], src[:, :]))
            return V(lambda e: e.tensor_copy(record[:, :, 2], weight[:, :].bitcast(I32)))

        def sort_steps(started, records_ok):
            read, row_read, made = {}, {}, {}
            carry = first_place

            def count(g):
                nonlocal carry
                b = g % 2
                cols = slice(g * UNROLL, (g + 1) * UNROLL)
                row = src_row[:, b * UNROLL * P:(b + 1) * UNROLL * P]
                landed = pr.dma("act", s_src_row[b], row,
                                a["src_run"][0:1, 1 + g * UNROLL * P:1 + (g + 1) * UNROLL * P].broadcast_to([P, UNROLL * P]),
                                row_read.get(g - 2), (s_mm, UNROLL + passes[0] * EDGE_TILES))
                t = V(lambda e: e.tensor_tensor(
                    src_lo_hot[:, :, :], iota[:, :].unsqueeze(1).broadcast_to([P, UNROLL, P]),
                    src_lo[:, cols].unsqueeze(2).broadcast_to([P, UNROLL, P]), ALU.is_equal), started, made.get("counted"))
                hot = V(lambda e: e.tensor_tensor(
                    hi_hot[b][:, :, 0:NODE_TILES], iota[:, 0:NODE_TILES].unsqueeze(1).broadcast_to([P, UNROLL, NODE_TILES]),
                    src_hi[:, cols].unsqueeze(2).broadcast_to([P, UNROLL, NODE_TILES]), ALU.is_equal), pr.last("dve"))
                V(lambda e: e.tensor_scalar(src_row_lo[b], row, P - 1, None, ALU.bitwise_and), landed)
                t = pr.last("dve")
                written = [t, t, t]
                for k in range(UNROLL):
                    t = written[k % 3] = V(lambda e, k=k: e.scalar_tensor_tensor(
                        out=unread[k % 3], in0=row[:, k * P:(k + 1) * P], scalar=src_f[:, g * UNROLL + k:g * UNROLL + k + 1],
                        in1=earlier, op0=ALU.is_equal, op1=ALU.mult,
                        accum_out=ranks[:, b * UNROLL + k:b * UNROLL + k + 1]), written[k % 3])
                row_read[g] = t
                blocks = psum[7][:, 0:(UNROLL + 1) * NODE_TILES].rearrange("p (k n) -> p k n", n=NODE_TILES)
                c = carry
                T(lambda e: e.matmul(blocks, ident[:, :], c.unsqueeze(1).broadcast_to([P, UNROLL + 1, NODE_TILES]),
                                     start=True, stop=False, skip_group_check=True), started, made.get("snap"), reader.get(7))
                for k in range(UNROLL):
                    m = T(lambda e, k=k: e.matmul(
                        blocks[:, k + 1:, :], src_lo_hot[:, k, :],
                        hi_hot[b][:, k, 0:NODE_TILES].unsqueeze(1).broadcast_to([P, UNROLL - k, NODE_TILES]),
                        start=False, stop=k == UNROLL - 1, skip_group_check=True), hot)
                made["counted"] = m
                made["snap"] = A(lambda e: e.copy(before_tile[b], psum[7][:, 0:(UNROLL + 1) * NODE_TILES]), m, read.get(g - 2))
                reader[7] = made["snap"]
                made[g] = made["snap"]
                carry = before_tile[b][:, UNROLL * NODE_TILES:(UNROLL + 1) * NODE_TILES]

            def look_up(g):
                b = g % 2
                lo_ok = V(lambda e: e.tensor_scalar(lo_T.rearrange("p k n -> p (k n)"), src_row_lo[b], part[:, 0:1], None,
                                                    ALU.is_equal), row_read[g], read.get(g - 1))
                i, ps, freed = bank()
                for k in range(UNROLL):
                    m = T(lambda e, k=k: e.matmul(ps[:, k * NODE_TILES:(k + 1) * NODE_TILES], lo_T[:, k, :],
                                                  before_tile[b][:, k * NODE_TILES:(k + 1) * NODE_TILES],
                                                  start=True, stop=True), freed if k == 0 else None, made[g], lo_ok)
                read[g] = m
                return i, ps, m

            def move_records(g, i, ps, m):
                b = g % 2
                cols = slice(g * UNROLL, (g + 1) * UNROLL)
                t = V(lambda e: e.tensor_tensor(
                    picked.rearrange("p (k n) -> p k n", n=NODE_TILES),
                    ps[:, 0:UNROLL * NODE_TILES].rearrange("p (k n) -> p k n", n=NODE_TILES),
                    hi_hot[b][:, :, 0:NODE_TILES], ALU.mult), m, pr.last("dve"))
                reader[i] = t
                t = V(lambda e: e.tensor_reduce(place, picked.rearrange("p (k n) -> p k n", n=NODE_TILES), AX_X, ALU.add), t)
                t = V(lambda e: e.tensor_tensor(place, place, ranks[:, b * UNROLL:(b + 1) * UNROLL], ALU.add), t)
                t = V(lambda e: e.tensor_copy(place_lo.bitcast(I32), place), t)
                t = V(lambda e: e.tensor_scalar(place_hi.bitcast(I32), place_lo.bitcast(I32), 7, None,
                                                ALU.arith_shift_right), t)
                t = V(lambda e: e.tensor_copy(place_lo, place_hi.bitcast(I32)), t)
                t = V(lambda e: e.scalar_tensor_tensor(out=place, in0=place_lo, scalar=-float(P), in1=place,
                                                       op0=ALU.mult, op1=ALU.add), t)
                t = V(lambda e: e.scalar_tensor_tensor(out=place, in0=place, scalar=float(EDGE_TILES), in1=place_lo,
                                                       op0=ALU.mult, op1=ALU.add), t)
                ready = V(lambda e: e.tensor_copy(place_i[:, cols], place), t)

                def move(e):
                    e.wait_ge(*ready)
                    e.wait_ge(*records_ok)
                    for t in range(g * UNROLL, (g + 1) * UNROLL):
                        e.indirect_dma_start(out=t_sort, out_offset=bass.IndirectOffsetOnAxis(ap=place_i[:, t:t + 1], axis=0),
                                             in_=record[:, t, :], in_offset=None).then_inc(s_moved, 16)

                pr.queue["pool"].append(move)

            for g in range(TURNS + 1):
                looked = look_up(g - 1) if g > 0 else None
                if g < TURNS:
                    count(g)
                if g > 0:
                    move_records(g - 1, *looked)
                yield

        def finish_sort():
            for _ in steps:
                pass
            counting[0] = False
            running_sum(in_cnt[:, :], True)
            s_back = pr.sem("sorted_records_loaded")
            back = pr.dma("sp", s_back, sorted_words, t_sort.rearrange("(p t) r -> p (t r)", p=P), (s_moved, 16 * EDGE_TILES))
            sorted_record = sorted_words.rearrange("p (t r) -> p t r", r=RECORD)
            V(lambda e: e.tensor_copy(dst[:, :], sorted_record[:, :, 0]), back)
            V(lambda e: e.tensor_copy(weight[:, :].bitcast(I32), sorted_record[:, :, 2]))
            t = V(lambda e: e.tensor_copy(src_f, sorted_record[:, :, 1]), pr.last("dve"))
            i, ps, freed = bank()
            m = T(lambda e: e.matmul(ps[:, 0:EDGE_TILES], ones[0:1, :], src_f[0:1, :], start=True, stop=True), freed, t)
            first = V(lambda e: e.tensor_copy(src_hi[:, :], ps[:, 0:EDGE_TILES]), m)
            reader[i] = first
            by_src_ok[0] = place_windows(control_src, src_f, src_hi[:, :], src_lo[:, :], first)
            for e in ("pe", "pool", "dve"):
                pr.queue[e].append(lambda g: g.wait_ge(*by_src_ok[0]))
            return dst, src_lo, weight, control_src

        xt_ready = transposes(lambda j: x[:, j, :], lambda j: l_x)
        pass_done = edge_pass(a["x"], l_edge, by_dst, planes=3, count_in=True, count_out=True)

        deg_copied = V(lambda e: e.tensor_copy(out_cnt[:, :], psum[7][:, 0:NODE_TILES]), pass_done)
        d1 = V(lambda e: e.tensor_scalar(rdeg[:, :], out_cnt[:, :], 1.0, None, ALU.max), deg_copied)
        reader[7] = deg_copied
        d2 = A(lambda e: e.activation(rdeg[:, :], rdeg[:, :], ACT.Sqrt), d1)
        V(lambda e: e.reciprocal(rdeg[:, :], rdeg[:, :]), d2)

        NODE_CHUNK = 512
        chunks = [(n0, min(n0 + NODE_CHUNK, PADDED_NODES)) for n0 in range(0, PADDED_NODES, NODE_CHUNK)]
        cnt = agg[:, 2, :]

        def running_sum(counts, including):
            i, ps, freed = bank()
            before = lambda n: ps[:, n * 32:n * 32 + NODE_TILES]
            tri = V(lambda e: e.tensor_scalar(triangle, iota[:, :], part[:, 0:1], None,
                                              ALU.is_ge if including else ALU.is_gt), pr.last("pe"))
            T(lambda e: e.matmul(before(0), triangle, counts, start=True, stop=True), freed, tri)
            m = T(lambda e: e.matmul(before(1), ones[:, :], counts, start=True, stop=True))
            total = picked[:, 0:NODE_TILES]
            t = V(lambda e: e.tensor_copy(total, before(1)), m)
            sums = first_place if not including else ends[:, :]
            t = V(lambda e: e.tensor_tensor_scan(sums, ones[:, 0:NODE_TILES], total, 0.0, ALU.mult, ALU.add), t)
            t = V(lambda e: e.tensor_tensor(sums, sums, total, ALU.subtract), t)
            reader[i] = t = V(lambda e: e.tensor_tensor(sums, sums, before(0), ALU.add), t)
            return t

        counting[0] = True
        i, ps, freed = bank()
        for j in range(NODE_TILES):
            in_cnt_ok = T(lambda e, j=j, ps=ps: e.matmul(ps[:, j:j + 1], cnt[0:1, j * P:(j + 1) * P], ones[0:1, 0:1],
                                                         start=True, stop=True), freed, pass_done)
        started = running_sum(out_cnt[:, :], False)
        reader[i] = t = V(lambda e, ps=ps: e.tensor_copy(in_cnt[:, :], ps[:, 0:NODE_TILES]), in_cnt_ok)
        t = V(lambda e: e.tensor_scalar(rcnt[:, :], in_cnt[:, :], 1.0, None, ALU.max), t)
        inverted = V(lambda e: e.reciprocal(rcnt[:, :], rcnt[:, :]), t)
        t = V(lambda e: e.tensor_scalar(mask[:, :], in_cnt[:, :], 0.0, None, ALU.is_gt))
        V(lambda e: e.tensor_scalar(maskb[:, :], mask[:, :], 1.0, BIG, ALU.subtract, ALU.mult), t)
        scaled = []
        for lo, hi in chunks:
            i, ps, freed = bank()
            for n in range(lo, hi, P):
                m = T(lambda e, ps=ps, n=n, lo=lo: e.matmul(ps[:, n - lo:n - lo + P],
                                                            rcnt[:, n // P:n // P + 1].broadcast_to([P, P]), ident[:, :],
                                                            start=True, stop=True), freed, inverted)
            reader[i] = t = V(lambda e, ps=ps, lo=lo, hi=hi: e.tensor_tensor(
                agg[:, 0:K_IN, lo:hi], agg[:, 0:K_IN, lo:hi],
                ps[:, 0:hi - lo].unsqueeze(1).broadcast_to([P, K_IN, hi - lo]), ALU.mult), m)
            scaled.append(t)
        records_ok = make_records(in_cnt_ok)
        V(lambda e: e.tensor_copy(src_f, src[:, :]))
        started = V(lambda e: e.tensor_scalar(earlier, iota[:, :], part[:, 0:1], None, ALU.is_lt), pr.last("pe"))
        xb = V(lambda e: e.tensor_tensor(own[:, :, 0:DIM], x[:, :, :],
                                         brow[:, B_HID2:B_HID2 + 1, :].broadcast_to([P, NODE_TILES, DIM]), ALU.add),
               l_x, c_edges, scaled[-1])

        hid = hidden[:, :].rearrange("p (b m n) -> p b m n", b=2, m=K_HID)
        hid_read = {0: None, 1: None}
        pieces = [0]
        steps = sort_steps(started, records_ok)

        def sort_beside(every):
            pieces[0] += 1
            if pieces[0] % every == 0:
                next(steps, None)

        staged = {}
        s_stage = [pr.sem(f"stage_written{k}") for k in range(4)]
        for c, (n0, n1) in enumerate(chunks):
            wdt = n1 - n0
            made = []
            for mt in range(K_HID):
                i, ps, freed = bank()
                pairs = [(w_a4[:, s, k, mt * P:(mt + 1) * P], (agg if s == 0 else xT)[:, k, n0:n1])
                         for s in range(2) for k in range(K_IN)]
                for q, (l, r) in enumerate(pairs):
                    m = T(lambda e, q=q, l=l, r=r, ps=ps, wdt=wdt: e.matmul(ps[:, 0:wdt], l, r, start=(q == 0), stop=(q == 3)),
                          freed if q == 0 else None, scaled[c], xt_ready if q == 0 else None, l_w)
                tok = A(lambda e, ps=ps, c=c, mt=mt, wdt=wdt: e.activation(hid[:, c % 2, mt, 0:wdt], ps[:, 0:wdt], ACT.Relu,
                                                                  bias=b1[:, mt:mt + 1]), m, hid_read[c % 2])
                reader[i] = tok
                sort_beside(2)
                made.append(tok)
            for jj in range(wdt // P):
                j = n0 // P + jj
                i, ps, freed = bank()
                for mt in range(K_HID):
                    m = T(lambda e, ps=ps, c=c, mt=mt, jj=jj: e.matmul(ps[:, :], hid[:, c % 2, mt, jj * P:(jj + 1) * P],
                                                                       w_b[:, mt, :], start=(mt == 0), stop=(mt == K_HID - 1)),
                          freed if mt == 0 else None, made[-1])
                hid_read[c % 2] = m
                sort_beside(2)
                cp = A(lambda e, ps=ps, j=j: e.copy(stage[:, j % 4, 0:DIM], ps[:, 0:DIM]), m, staged.get(j % 4))
                reader[i] = V(lambda e, ps=ps, j=j: e.tensor_tensor(own[:, j, 0:DIM], own[:, j, 0:DIM], ps[:, DIM:2 * DIM],
                                                                    ALU.add), m, xb, cp)
                staged[j % 4] = pr.dma("sp", s_stage[j % 4], t_u[j * P:(j + 1) * P, :],
                                            stage[:, j % 4, 0:DIM], cp)
        table = all_staged(pr, staged)
        pass_done = edge_pass(t_u, table, by_dst, after=pr.last("dve"))

        roots, written = {}, [None]

        def y0(g):
            for j in g:
                i, ps, freed = bank()
                T(lambda e, ps=ps, j=j: e.transpose(ps[:, 0:P], agg[:, 0, j * P:(j + 1) * P], ident[:, :]), freed, pass_done)
                m = T(lambda e, ps=ps, j=j: e.transpose(ps[:, P:2 * P], agg[:, 1, j * P:(j + 1) * P], ident[:, :]))
                reader[i] = V(lambda e, ps=ps, j=j: e.scalar_tensor_tensor(
                    out=x[:, j, :], in0=ps[:, 0:DIM], scalar=rcnt[:, j:j + 1], in1=own[:, j, 0:DIM],
                    op0=ALU.mult, op1=ALU.add), m)
            sort_beside(1)
            roots[g] = mean_and_root(lambda j: x[:, j, :], g, pr.last("dve"))

        def norm0(g):
            written[0] = write_rows(t_x[0], x, g, normalize(g, roots[g])[-1])
            sort_beside(1)

        in_groups(y0, norm0)
        x_normed = pr.last("dve")

        s_turned = pr.sem("tile_transposed")
        s_xt = pr.sem("features_copied")
        s_own_made = pr.sem("own_term_multiplied")
        s_own = pr.sem("own_term_stored")
        own_flat = own[:, :, :].rearrange("p t d -> p (t d)")
        x_flat = x[:, :, :].rearrange("p t d -> p (t d)")
        s_row_tile = pr.sem("row_tile_copied")
        halves = src_lo_hot[:, :, :].rearrange("p k n -> p (k n)").bitcast(F32)
        row_tile, turned_tile = halves[:, 0:DIM], halves[:, DIM:2 * DIM].rearrange("p (k n) -> p k n", k=K_IN)
        for e, sem in (("act", s_xt), ("dve", s_own), ("pe", s_turned), ("pe", s_own_made)):
            pr.queue[e].append(lambda g, sem=sem: g.sem_inc(sem, 1))

        class OwnProduct:

            count = [0]

            def __init__(self, rows_of, stride, ready, weights, bias=None, keep=False):
                self.rows_of, self.stride, self.weights, self.bias, self.keep = rows_of, stride, weights, bias, keep
                self.done = self.count[0] * NODE_TILES
                self.count[0] += 1
                banks_read = [reader[b] for b in (TURN_BANK, OWN_BANK) if b in reader]
                pr.queue["pe"].append(lambda e: [e.wait_ge(*w) for w in banks_read])
                pr.queue["act"].append(lambda e: e.wait_ge(*ready))
                pr.queue["act"].append(self.act)
                self.transposed = reader[TURN_BANK] = s_xt, self.done + NODE_TILES + 1
                self.stored = reader[OWN_BANK] = s_own, self.done + NODE_TILES + 1

            def act(self, e):
                with e.Fori(0, NODE_TILES) as i:
                    e.wait_ge(s_turned, i + (self.done + 1))
                    e.copy(row_tile, self.rows_of[:, bass.ds(i * self.stride, DIM)]).then_inc(s_row_tile, 1)
                    e.wait_ge(s_turned, i + (self.done + 2))
                    e.wait_ge(s_own_made, i + (self.done + 1))
                    turned = psum[TURN_BANK][:, 0:DIM].rearrange("p (k n) -> p k n", k=K_IN)
                    if self.keep:
                        e.copy(xT[:, :, bass.ds(i * P, P)], turned)
                    e.copy(turned_tile, turned).then_inc(s_xt, 1)

            def transpose(self, e, i):
                e.wait_ge(s_row_tile, i + (self.done + 1))
                e.wait_ge(s_xt, i + (self.done + 1))
                for k in range(K_IN):
                    m = e.transpose(psum[TURN_BANK][:, k * P:(k + 1) * P], row_tile[:, k * P:(k + 1) * P], ident[:, :])
                m.then_inc(s_turned, 1)

            def multiply(self, e, i):
                e.wait_ge(s_xt, i + (self.done + 2))
                e.wait_ge(s_own, i + (self.done + 1))
                for k in range(K_IN):
                    m = e.matmul(psum[OWN_BANK][:, 0:DIM], turned_tile[:, k, :], self.weights[:, k, :],
                                 start=(k == 0), stop=(k == K_IN - 1))
                m.then_inc(s_own_made, 1)

            def dve(self, e, i):
                e.wait_ge(s_own_made, i + (self.done + 2))
                o = own_flat[:, bass.ds(i * ATT_ROW, DIM)]
                if self.bias is None:
                    e.tensor_copy(o, psum[OWN_BANK][:, 0:DIM]).then_inc(s_own, 1)
                else:
                    e.tensor_tensor(o, psum[OWN_BANK][:, 0:DIM], brow[:, self.bias, :], ALU.add).then_inc(s_own, 1)

        table = written[0]
        own_rows = x_flat, DIM, x_normed
        w2 = w_a[:, 0:2 * K_IN * DIM].rearrange("p (s k n) -> p s k n", s=2, k=K_IN)
        w3_row = DIM + 2 * HEADS
        w3 = w_a[:, 2 * K_IN * DIM:2 * K_IN * DIM + K_IN * w3_row].rearrange("p (k n) -> p k n", k=K_IN)
        free = pr.last("pe")
        s_w2 = pr.sem("late_weights_loaded")
        pr.dma("sp", s_w2, w2[:, 0, :, :], a["l2w1"].rearrange("(k p) n -> p k n", p=P), free)
        pr.dma("sp", s_w2, w2[:, 1, :, :], a["l2w2"].rearrange("(k p) n -> p k n", p=P))
        l_w2 = pr.dma("sp", s_w2, w3[:, :, 0:DIM], a["l3w"].rearrange("(k p) n -> p k n", p=P))

        t = V(lambda e: e.tensor_scalar(part_i[:, :], part_i[:, :], 5, None, ALU.arith_shift_right), pr.last("dve"))
        t = V(lambda e: e.tensor_copy(head_of[:, 0:1], part_i[:, :]), t)
        for k in range(1, K_IN):
            t = V(lambda e, k=k: e.tensor_scalar(head_of[:, k:k + 1], head_of[:, 0:1], float(k * P // HEAD_DIM), None, ALU.add), t)
        for k in range(K_IN):
            for r in range(2):
                t = V(lambda e, k=k, r=r: e.tensor_scalar(att_heads[:, k, r * HEADS:(r + 1) * HEADS], iota[:, 0:HEADS],
                                                          head_of[:, k:k + 1], att[:, r, k:k + 1], ALU.is_equal, ALU.mult), t, l_w)
        for k in range(K_IN):
            i, ps, freed = bank()
            for c in range(K_IN):
                m = T(lambda e, ps=ps, k=k, c=c: e.transpose(ps[:, c * P:(c + 1) * P], w3[:, k, c * P:(c + 1) * P], ident[:, :]),
                      freed, l_w2)
            turned = V(lambda e, ps=ps: e.tensor_copy(tmp[:, 0, 0:DIM], ps[:, 0:DIM]), m, t)
            reader[i] = turned
            i, ps, freed = bank()
            for c in range(K_IN):
                m = T(lambda e, ps=ps, c=c: e.matmul(ps[:, 0:2 * HEADS], tmp[:, 0, c * P:(c + 1) * P], att_heads[:, c, :],
                                                     start=(c == 0), stop=(c == K_IN - 1)), freed, turned, *staged.values())
            reader[i] = t = V(lambda e, ps=ps, k=k: e.tensor_copy(w3[:, k, DIM:], ps[:, 0:2 * HEADS]), m, l_w2)

        by_src = finish_sort()
        s_wc = pr.sem("hop_weights_loaded")
        for s, n in enumerate(("wn", "ws")):
            for h in range(HOPS):
                l_wc = pr.dma("sp", s_wc, w_c[:, h, s, :, :], a[n][h].rearrange("(k p) n -> p k n", p=P), by_src_ok[0])
        pr.queue["pe"].append(lambda e: e.wait_ge(*l_wc))
        for hop in range(HOPS):
            pass_done = edge_pass(t_x[hop], table, by_src,
                                  beside=OwnProduct(*own_rows, w_c[:, hop, 1, :, :], B_HOP + hop))

            def neighbours(j, hop=hop):
                i, ps, freed = bank()
                for k in range(K_IN):
                    m = T(lambda e, ps=ps, j=j, k=k, hop=hop: e.matmul(ps[:, 0:DIM], agg[:, k, j * P:(j + 1) * P],
                                                              w_c[:, hop, 0, k, :], start=(k == 0), stop=(k == K_IN - 1)),
                          freed, pass_done)
                return i, ps, m

            if hop < HOPS - 1:
                exponential = {}

                def negative_part(g):
                    for j in g:
                        i, ps, m = neighbours(j)
                        reader[i] = t = V(lambda e, ps=ps, j=j: e.tensor_tensor(own[:, j, 0:DIM], ps[:, 0:DIM],
                                                                                own[:, j, 0:DIM], ALU.add), m)
                    t = V(lambda e: e.tensor_scalar(tiles(spare, g), tiles(own, g)[:, :, 0:DIM], 0.0, None, ALU.min), t)
                    exponential[g] = A(lambda e: e.activation(tiles(spare, g), tiles(spare, g), ACT.Exp), t)

                def elu(g):
                    h = tiles(own, g)[:, :, 0:DIM]
                    t = V(lambda e: e.tensor_scalar(h, h, 0.0, None, ALU.max), pr.last("dve"))
                    t = V(lambda e: e.scalar_tensor_tensor(out=h, in0=tiles(spare, g), scalar=-1.0, in1=h,
                                                           op0=ALU.add, op1=ALU.add), exponential[g], t)
                    written[0] = write_rows(t_x[hop + 1], own[:, :, 0:DIM], g, t)

                in_groups(negative_part, elu)
                table = written[0]
                own_rows = own_flat, ATT_ROW, pr.last("dve")
                pr.queue["dve"].append(lambda e, table=table: e.wait_ge(*table))

        def y1(g):
            for j in g:
                i, ps, m = neighbours(j)
                reader[i] = t = V(lambda e, ps=ps, j=j: e.tensor_tensor(own[:, j, 0:DIM], ps[:, 0:DIM],
                                                                        own[:, j, 0:DIM], ALU.add), m)
            t = V(lambda e: e.tensor_tensor(tiles(x, g), tiles(x, g), tiles(own, g)[:, :, 0:DIM], ALU.add), t)
            roots[g] = mean_and_root(lambda j: x[:, j, :], g, t)

        def norm1(g):
            for j, t in zip(g, normalize(g, roots[g])):
                t = A(lambda e, j=j: e.activation(spare[:, j, :], x[:, j, :], ACT.Copy, scale=rdeg[:, j:j + 1]), t)
            written[0] = write_rows(t_g, spare, g, t)

        in_groups(y1, norm1)

        pr.queue["pe"].append(lambda e: e.wait_ge(*l_w2))
        table = written[0]
        product = OwnProduct(x_flat, DIM, table, w2[:, 0, :, :], keep=True)
        own_ready = product.stored
        pass_done = edge_pass(t_g, table, by_dst, beside=product)
        cuts = [(lo, min(lo + TILES_AT_ONCE * P, PADDED_NODES)) for lo in range(0, PADDED_NODES, TILES_AT_ONCE * P)]
        prod = [V(lambda e, lo=lo, hi=hi: e.tensor_tensor(xT[:, :, lo:hi], xT[:, :, lo:hi], agg[:, 0:K_IN, lo:hi], ALU.mult),
                  pass_done, product.transposed) for lo, hi in cuts]
        heads = lambda ap: ap.rearrange("p (h c) -> p h c", h=HEADS)
        h_rows = own[:, :, :].rearrange("p t (h c) -> p t h c", h=HEADS)
        squared, turned_ok = {}, {}
        projected = [None] * 3

        def interact(g):
            o = tiles(own, g)[:, :, 0:DIM]
            for j in g:
                i, ps, freed = bank()
                pairs = [(agg, 0, k) for k in range(K_IN)] + [(xT, 1, k) for k in range(K_IN)]
                for q, (l, s, k) in enumerate(pairs):
                    m = T(lambda e, ps=ps, j=j, l=l, s=s, k=k, q=q: e.matmul(
                        ps[:, 0:DIM], l[:, k, j * P:(j + 1) * P], w2[:, s, k, :], start=(q == 0), stop=(q == 3)),
                        freed, prod[j // TILES_AT_ONCE])
                reader[i] = t = V(lambda e, ps=ps, j=j: e.scalar_tensor_tensor(
                    out=own[:, j, 0:DIM], in0=ps[:, 0:DIM], scalar=rdeg[:, j:j + 1], in1=own[:, j, 0:DIM],
                    op0=ALU.mult, op1=ALU.add), m, own_ready)
            last_product[g] = m
            for j in g:
                t = V(lambda e, j=j: e.scalar_tensor_tensor(
                    out=own[:, j, 0:DIM], in0=own[:, j, 0:DIM], scalar=mask[:, j:j + 1], in1=brow[:, B_L2, :],
                    op0=ALU.mult, op1=ALU.add), t)
            t = V(lambda e: e.scalar_tensor_tensor(out=o, in0=o, scalar=0.01, in1=o, op0=ALU.mult, op1=ALU.max), t)
            activated[g] = t

        def square(g):
            for j in g:
                sqd = A(lambda e, j=j: e.activation(tmp[:, j % 4, 0:DIM], own[:, j, 0:DIM], ACT.Square,
                                                    accum_out=sq[:, j:j + 1]), activated[g], squared.get(j - 4))
                squared[j] = sqd
            lengths[g] = sqd

        def length_and_norm(g):
            q = tiles(sq, g)
            t = V(lambda e: e.tensor_scalar(q, q, 1e-24, None, ALU.max), lengths[g])
            t = A(lambda e: e.activation(q, q, ACT.Sqrt), t)
            t = V(lambda e: e.reciprocal(q, q), t)
            for j in g:
                t2 = V(lambda e, j=j: e.scalar_tensor_tensor(out=x[:, j, :], in0=own[:, j, 0:DIM], scalar=sq[:, j:j + 1],
                                                             in1=x[:, j, :], op0=ALU.mult, op1=ALU.add), t)
            roots[g] = mean_and_root(lambda j: x[:, j, :], g, t2)

        def normalize_and_ones(g):
            ones_ok = V(lambda e: e.memset(tiles(h_rows, g)[:, :, :, HEAD_DIM:HEAD_ROW], 1.0), pr.last("dve"))
            normed[g] = ones_ok, normalize(g, roots[g])

        def project(g):
            ones_ok, rows_ok = normed[g]
            for j, row_ok in zip(g, rows_ok):
                i, ps, freed = bank()
                for k in range(K_IN):
                    m = T(lambda e, ps=ps, j=j, k=k: e.transpose(ps[:, k * P:(k + 1) * P], x[:, j, k * P:(k + 1) * P], ident[:, :]),
                          freed if k == 0 else None, row_ok if k == 0 else None)
                reader[i] = turned = A(lambda e, ps=ps, j=j: e.copy(
                    xT[:, :, j * P:(j + 1) * P], ps[:, 0:DIM].rearrange("p (k n) -> p k n", k=K_IN)), m, last_product[g])
                turned_ok[j] = turned
            for j in g:
                i, ps, freed = bank()
                for k in range(K_IN):
                    m = T(lambda e, ps=ps, j=j, k=k: e.matmul(ps[:, 0:DIM + 2 * HEADS], xT[:, k, j * P:(j + 1) * P],
                                                              w3[:, k, :], start=(k == 0), stop=(k == K_IN - 1)),
                          freed, turned_ok[j])
                A(lambda e, ps=ps, j=j: e.copy(h_rows[:, j, :, 0:HEAD_DIM], heads(ps[:, 0:DIM])), m, ones_ok)
                reader[i] = cp = A(lambda e, ps=ps, j=j: e.copy(
                    a_both[:, :, j, :], ps[:, DIM:DIM + 2 * HEADS].rearrange("p (r h) -> p r h", h=HEADS)))
            projected[0] = m
            write_rows(t_as, a_src, g, cp)
            projected[1] = write_rows(t_h, own, g, cp)
            projected[2] = cp

        last_product, activated, lengths, normed = {}, {}, {}, {}
        in_order((2, normalize_and_ones), (1, length_and_norm), (0, interact), (2, project), (0, square))
        last_projection, w_h, a_ok = projected

        p_all = hidden[:, 0:EDGE_TILES * HEADS]
        s_gas = pr.sem("edge_a_src_landed")

        def gather_a_src(e):
            e.wait_ge(*w_h)
            for t in range(GATHERED_TURNS * UNROLL):
                e.indirect_dma_start(out=p_all[:, t * HEADS:(t + 1) * HEADS], out_offset=None, in_=t_as,
                                     in_offset=bass.IndirectOffsetOnAxis(ap=src[:, t:t + 1], axis=0)).then_inc(s_gas, 16)

        pr.queue["pool"].append(gather_a_src)
        g_as = (s_gas, 16 * GATHERED_TURNS * UNROLL)

        runs, seg, prev = agg[:, 0, :], agg[:, 1, :], agg[:, 2, :]
        seg_i, prev_i = seg.bitcast(I32), prev.bitcast(I32)
        s_seg = pr.sem("scan_dst_loaded")
        free = pr.last("pe")
        for r in range(SCAN_ROWS):
            pr.dma("act", s_seg, seg_i[r * HEADS:(r + 1) * HEADS, :],
                   a["dst_run"][0:1, 1 + r * SCAN_LEN:1 + (r + 1) * SCAN_LEN].broadcast_to([HEADS, SCAN_LEN]), free, pr.last("dve"))
            l_seg = pr.dma("act", s_seg, prev_i[r * HEADS:(r + 1) * HEADS, :],
                           a["dst_run"][0:1, r * SCAN_LEN:(r + 1) * SCAN_LEN].broadcast_to([HEADS, SCAN_LEN]))
        t = V(lambda e: e.tensor_tensor(seg, seg_i, prev_i, ALU.not_equal), l_seg)
        seg_ok = V(lambda e: e.tensor_scalar(seg, seg, -BIG, None, ALU.mult), t)

        def expand_a_src():
            table = a_src.rearrange("p t h -> p (t h)")
            mem = xT[:, :, :].rearrange("p k n -> p (k n)")
            n = UNROLL * P
            row = [mem[:, b * n:(b + 1) * n].bitcast(I32) for b in range(2)]
            low = mem[:, 2 * n:3 * n].bitcast(I32)
            low_hot = [mem[:, (3 + b) * n:(4 + b) * n] for b in range(2)]
            high_hot = [hidden[:, EDGE_TILES * HEADS + b * UNROLL * NODE_TILES:
                               EDGE_TILES * HEADS + (b + 1) * UNROLL * NODE_TILES]
                        .rearrange("p (k n) -> p k n", n=NODE_TILES) for b in range(2)]
            chosen = agg[:, 0, 0:UNROLL * NODE_TILES * HEADS]
            by_tile = lambda ap: ap.rearrange("p (k n h) -> p k n h", n=NODE_TILES, h=HEADS)
            row_read, bank_read, multiplied, summed = {}, {}, {}, {}
            two = 2 * NODE_TILES * HEADS

            def choose(g):
                b = g % 2
                for q in range(UNROLL // 2):
                    t = V(lambda e, q=q: e.tensor_tensor(
                        by_tile(chosen[:, q * two:(q + 1) * two]), by_tile(psum[4 * b + q][:, 0:two]),
                        high_hot[b][:, 2 * q:2 * q + 2, :].unsqueeze(3).broadcast_to([P, 2, NODE_TILES, HEADS]),
                        ALU.mult), multiplied[g], summed.get(g - 1))
                    reader[4 * b + q] = t
                bank_read[g] = t
                summed[g] = V(lambda e: e.tensor_reduce(
                    p_all[:, g * UNROLL * HEADS:(g + 1) * UNROLL * HEADS].rearrange("p (k h) -> p k h", h=HEADS),
                    by_tile(chosen).rearrange("p k n h -> p k h n"), AX_X, ALU.add), t)
                return summed[g]

            low_read = None
            for g in range(GATHERED_TURNS, TURNS):
                b = g % 2
                landed = pr.dma("sp", s_src_row[b], row[b],
                                a["src_run"][0:1, 1 + g * n:1 + (g + 1) * n].broadcast_to([P, n]),
                                row_read.get(g - 2), last_projection)
                t = V(lambda e, b=b: e.tensor_scalar(low, row[b], P - 1, None, ALU.bitwise_and), landed, low_read)
                row_read[g] = t
                low_read = V(lambda e, b=b: e.tensor_scalar(low_hot[b], low, part[:, 0:1], None, ALU.is_equal), t, multiplied.get(g - 2))
                hot = V(lambda e, b=b, g=g: e.tensor_tensor(
                    high_hot[b], iota[:, 0:NODE_TILES].unsqueeze(1).broadcast_to([P, UNROLL, NODE_TILES]),
                    src_hi_of[:, g * UNROLL:(g + 1) * UNROLL].unsqueeze(2).broadcast_to([P, UNROLL, NODE_TILES]),
                    ALU.is_equal), src_hi_ready, bank_read.get(g - 2))
                for k in range(UNROLL):
                    m = T(lambda e, b=b, k=k: e.matmul(
                        psum[4 * b + k // 2][:, (k % 2) * (two // 2):(k % 2 + 1) * (two // 2)],
                        low_hot[b][:, k * P:(k + 1) * P], table, start=True, stop=True),
                        hot, a_ok, bank_read.get(g - 2), reader.get(4 * b + k // 2))
                multiplied[g] = m
                if g > GATHERED_TURNS:
                    choose(g - 1)
            return choose(TURNS - 1), m

        high = src_lo[:, :].bitcast(I32)
        src_hi_of = src_hi[:, :]
        t = V(lambda e: e.tensor_scalar(high, src[:, :], 7, None, ALU.arith_shift_right))
        src_hi_ready = V(lambda e: e.tensor_copy(src_hi_of, high), t)
        expanded, xt_free = expand_a_src()
        by_step = V(lambda e: e.tensor_copy(prev.rearrange("p (k r h) -> p k r h", r=SCAN_ROWS, k=SCAN_TILES),
                                            p_all.rearrange("p (r k h) -> p k r h", r=SCAN_ROWS, k=SCAN_TILES)), seg_ok, g_as, expanded)
        for k in range(SCAN_TILES):
            i, ps, freed = bank()
            m = T(lambda e, ps=ps, k=k: e.transpose(ps[:, 0:P], prev[:, k * P:(k + 1) * P], ident[:, :]), freed, by_step)
            got = V(lambda e, ps=ps, k=k: e.tensor_copy(runs[:, k * P:(k + 1) * P], ps[:, 0:P]), m)
            reader[i] = got
        run1 = V(lambda e: e.tensor_tensor_scan(prev, seg, runs, -BIG, ALU.add, ALU.max), got)
        low = V(lambda e: e.tensor_reduce(small[:, 0, 0:1], seg, AX_X, ALU.min))
        i, ps, freed = bank()
        T(lambda e, ps=ps: e.transpose(ps[0:1, 0:P], prev[:, SCAN_LEN - 1:SCAN_LEN], ident[:, :]), freed, run1)
        m = T(lambda e, ps=ps: e.transpose(ps[0:1, P:2 * P], small[:, 0, 0:1], ident[:, :]), low)
        c = V(lambda e, ps=ps: e.tensor_copy(small[0:1, 1, :], ps[0:1, 0:P]), m)
        c = V(lambda e, ps=ps: e.tensor_copy(small[0:1, 2, :], ps[0:1, P:2 * P]))
        reader[i] = c
        c = V(lambda e: e.memset(small[0:1, 3, 0:HEADS], -BIG), c)
        for h in range(HEADS):
            by_run = lambda q, lo, n, h=h: small[0:1, q, :].rearrange("p (r h) -> p r h", h=HEADS)[:, lo:lo + n, h]
            c = V(lambda e, f=by_run: e.tensor_tensor_scan(f(3, 1, SCAN_ROWS - 1), f(2, 0, SCAN_ROWS - 1), f(1, 0, SCAN_ROWS - 1),
                                                           -BIG, ALU.add, ALU.max), c)
        i, ps, freed = bank()
        m = T(lambda e, ps=ps: e.matmul(ps[:, 0:1], small[0:1, 3, :], ones[0:1, 0:1], start=True, stop=True), freed, c)
        c = V(lambda e, ps=ps: e.tensor_copy(small[:, 0, 1:2], ps[:, 0:1]), m)
        reader[i] = c
        run2 = V(lambda e: e.tensor_tensor_scan(prev, seg, runs, small[:, 0, 1:2], ALU.add, ALU.max), c)
        back = runs[:, :].rearrange("p (r k h) -> p k r h", r=SCAN_ROWS, k=SCAN_TILES)
        for k in range(SCAN_TILES):
            i, ps, freed = bank()
            m = T(lambda e, ps=ps, k=k: e.transpose(ps[:, 0:P], prev[:, k * P:(k + 1) * P], ident[:, :]), freed, run2)
            got = V(lambda e, ps=ps, k=k: e.tensor_copy(back[:, k, :, :], ps[:, 0:P].rearrange("p (r h) -> p r h", h=HEADS)), m)
            reader[i] = got
        w_run = pr.dma("sp", s_tab, t_run.rearrange("(p t) h -> p (t h)", p=P), runs, got)
        pos, pos_hi = small[:, 0, 0:NODE_TILES], small[:, 1, 0:NODE_TILES]
        pos_i, hi_i = small[:, 2, 0:NODE_TILES].bitcast(I32), small[:, 3, 0:NODE_TILES].bitcast(I32)
        t = V(lambda e: e.tensor_scalar(pos, ends[:, :], 1.0, 0.0, ALU.subtract, ALU.max), got)
        t = V(lambda e: e.tensor_copy(pos_i, pos), t)
        t = V(lambda e: e.tensor_scalar(hi_i, pos_i, 7, None, ALU.arith_shift_right), t)
        t = V(lambda e: e.tensor_copy(pos_hi, hi_i), t)
        t = V(lambda e: e.scalar_tensor_tensor(out=pos, in0=pos_hi, scalar=-float(P), in1=pos, op0=ALU.mult, op1=ALU.add), t)
        t = V(lambda e: e.scalar_tensor_tensor(out=pos, in0=pos, scalar=float(EDGE_TILES), in1=pos_hi, op0=ALU.mult, op1=ALU.add), t)
        last_row = V(lambda e: e.tensor_copy(pos_i, pos), t)
        mx = tmp[:, 0, 0:NODE_TILES * HEADS]
        mx3 = mx.rearrange("p (t h) -> p t h", h=HEADS)
        s_last = pr.sem("segment_max_landed")

        def gather_last(e):
            e.wait_ge(*w_run)
            e.wait_ge(*last_row)
            for j in range(NODE_TILES):
                e.indirect_dma_start(out=mx[:, j * HEADS:(j + 1) * HEADS], out_offset=None, in_=t_run,
                                     in_offset=bass.IndirectOffsetOnAxis(ap=pos_i[:, j:j + 1], axis=0)).then_inc(s_last, 16)

        g_last = (s_last, 16 * NODE_TILES)
        V(lambda e: e.tensor_tensor(x[:, :, :], x[:, :, :], brow[:, B_BETA:B_BETA + 1, :].broadcast_to([P, NODE_TILES, DIM]),
                                    ALU.add), last_projection)
        nh = [P, NODE_TILES, HEADS]
        ad3, m3 = am[:, 0:NODE_TILES, 0:HEADS], am[:, 0:NODE_TILES, HEADS:2 * HEADS]
        z3 = tmp[:, 1, 0:NODE_TILES * HEADS].rearrange("p (t h) -> p t h", h=HEADS)
        t = V(lambda e: e.memset(am[:, :, :], 0.0))
        t = V(lambda e: e.tensor_copy(ad3, a_dst[:, :, :]), t)
        t = V(lambda e: e.tensor_tensor(mx3, mx3, mask[:, :].unsqueeze(2).broadcast_to(nh), ALU.mult), g_last, t)
        t = V(lambda e: e.tensor_tensor(mx3, mx3, maskb[:, :].unsqueeze(2).broadcast_to(nh), ALU.add), t)
        t = V(lambda e: e.tensor_tensor(mx3, mx3, a_src[:, :, :], ALU.max), t)
        t = V(lambda e: e.tensor_tensor(mx3, mx3, a_dst[:, :, :], ALU.add), t)
        t = V(lambda e: e.scalar_tensor_tensor(out=m3, in0=mx3, scalar=0.2, in1=mx3, op0=ALU.mult, op1=ALU.max), t)
        u = V(lambda e: e.tensor_tensor(z3, a_src[:, :, :], a_dst[:, :, :], ALU.add), t)
        u = V(lambda e: e.scalar_tensor_tensor(out=z3, in0=z3, scalar=0.2, in1=z3, op0=ALU.mult, op1=ALU.max), u)
        u = V(lambda e: e.tensor_tensor(z3, z3, m3, ALU.subtract), u)
        ps_tok = A(lambda e: e.activation(p_self[:, :, :], z3, ACT.Exp), u)
        w_am = pr.dma("sp", s_tab, t_am.rearrange("(t p) h -> p t h", p=P), am[:, :, :], t)

        xt_mem = xT[:, :, :].rearrange("p k n -> p (k n)")
        hot_T = xt_mem[:, 0:UNROLL * P].rearrange("p (k n) -> p k n", n=P)
        dst_row = xt_mem[:, UNROLL * P:2 * UNROLL * P].bitcast(I32)
        node_at = src_hi
        c3 = control_dst[:, :].rearrange("p (t c) -> p t c", c=CONTROL)
        t = V(lambda e: e.tensor_copy(node_at[:, :].rearrange("p (t k) -> p t k", k=UNROLL), c3[:, :, 0:UNROLL]))
        node_ok = V(lambda e: e.tensor_scalar(node_at[:, :], node_at[:, :], part[:, 0:1], None, ALU.add), t)
        s_dst_row = pr.sem("dst_row_landed")
        s_hot_T = pr.sem("transposed_onehot_built")
        s_window = [pr.sem(f"window_landed{k}") for k in range(UNROLL)]
        s_expanded = pr.sem("window_multiplied")
        s_step = pr.sem("exponent_step")
        s_z = pr.sem("exponents_made")
        s_p = pr.sem("edge_weights_made")
        bank_exp = psum[4]
        pr.queue["pe"].append(lambda e, read=reader[4]: e.wait_ge(*read))
        seen = bank_exp[:, 0:UNROLL * 2 * HEADS].rearrange("p (t h) -> p t h", h=2 * HEADS)

        class Attention:

            def expand(self, e, j):
                e.wait_ge(s_dst_row, j * 16 + 16)
                if not (isinstance(j, int) and j == 0):
                    e.wait_ge(s_expanded, j * UNROLL)
                e.tensor_tensor(hot_T, dst_row.rearrange("p (k n) -> p k n", n=P),
                                node_at[:, bass.ds(j * UNROLL, UNROLL)].unsqueeze(2).broadcast_to([P, UNROLL, P]),
                                ALU.is_equal).then_inc(s_hot_T, 1)

            def multiply(self, e, j):
                e.wait_ge(s_hot_T, j + 1)
                if not (isinstance(j, int) and j == 0):
                    e.wait_ge(s_z, j)
                for k in range(UNROLL):
                    e.wait_ge(s_window[k], j * 16 + 16)
                    e.matmul(bank_exp[:, k * 2 * HEADS:(k + 1) * 2 * HEADS], hot_T[:, k, :], window[:, k, :],
                             start=True, stop=True).then_inc(s_expanded, 1)

            def exponents(self, e, j):
                z = p_all[:, bass.ds(j * (UNROLL * HEADS), UNROLL * HEADS)].rearrange("p (t h) -> p t h", h=HEADS)
                e.wait_ge(s_expanded, j * UNROLL + UNROLL)
                e.tensor_tensor(z, z, seen[:, :, 0:HEADS], ALU.add).then_inc(s_step, 1)
                e.wait_ge(s_step, j * 3 + 1)
                e.scalar_tensor_tensor(out=z, in0=z, scalar=0.2, in1=z, op0=ALU.mult, op1=ALU.max).then_inc(s_step, 1)
                e.wait_ge(s_step, j * 3 + 2)
                e.tensor_tensor(z, z, seen[:, :, HEADS:2 * HEADS], ALU.subtract).then_inc(s_step, 1)
                e.wait_ge(s_step, j * 3 + 3)
                e.tensor_scalar(z, z, 0.0, None, ALU.min).then_inc(s_z, 1)

            def weigh(self, e, i, g, place):
                e.wait_ge(s_p, i + 1)
                n = GROUP * HEADS
                rows3 = place.rearrange("p k (h c) -> p (k h) c", c=HEAD_ROW)
                p = p_all[:, bass.ds(i * (UNROLL * HEADS) + g * n, n)]
                return e.tensor_tensor(rows3, rows3, p.unsqueeze(2).broadcast_to([P, n, HEAD_ROW]), ALU.mult)

        def attention_sp(e):
            regs = [e.alloc_register(f"window_row{k}") for k in range(UNROLL)]
            e.wait_ge(*w_am)

            def windows(j):
                e.load(regs, control_dst[0:1, bass.ds(j * CONTROL, UNROLL)])
                at = [e.snap(r, min_val=0, max_val=PADDED_NODES) for r in regs]
                for k in range(UNROLL):
                    if not (isinstance(j, int) and j == 0):
                        e.wait_ge(s_expanded, j * UNROLL + (k + 1 - UNROLL))
                    e.dma_start(window[:, k, :], t_am[bass.ds(at[k], P), :]).then_inc(s_window[k], 16)

            windows(0)
            with e.Fori(1, TURNS) as j:
                windows(j)

        def attention_act(e):
            def load(j):
                e.dma_start(dst_row, a["dst_run"][0:1, bass.ds(j * (UNROLL * P) + 1, UNROLL * P)]
                            .broadcast_to([P, UNROLL * P])).then_inc(s_dst_row, 16)

            def exp(j):
                e.wait_ge(s_z, j + 1)
                z = p_all[:, bass.ds(j * (UNROLL * HEADS), UNROLL * HEADS)]
                e.activation(z, z, ACT.Exp).then_inc(s_p, 1)

            e.wait_ge(*xt_free)
            e.wait_ge(*expanded)
            load(0)
            with e.Fori(0, TURNS - 1) as j:
                e.wait_ge(s_hot_T, j + 1)
                load(j + 1)
                exp(j)
            exp(TURNS - 1)

        pr.queue["sp"].append(attention_sp)
        pr.queue["act"].append(attention_act)
        pr.queue["pe"].append(lambda e: e.wait_ge(*node_ok))
        pr.queue["dve"].append(lambda e: (e.wait_ge(*node_ok), e.wait_ge(*w_run), e.wait_ge(*g_as)))
        t = V(lambda e: e.tensor_tensor(h_rows, h_rows, p_self.unsqueeze(3).broadcast_to([P, NODE_TILES, HEADS, HEAD_ROW]),
                                        ALU.mult), ps_tok, w_h)
        pass_done = edge_pass(t_h, w_h, by_dst, width=ATT_ROW, planes=3, attention=Attention(), other_gathers=gather_last)

        biased, stored = {}, {}

        def attended(g):
            for j in g:
                i, ps, freed = bank()
                for c, at in ((2, ATT_ROW - P), (1, P), (0, 0)):
                    m = T(lambda e, ps=ps, j=j, c=c, at=at: e.transpose(ps[:, at:at + P], agg[:, c, j * P:(j + 1) * P],
                                                                        ident[:, :]), freed, pass_done)
                reader[i] = t = V(lambda e, j=j, ps=ps: e.tensor_tensor(own[:, j, :], own[:, j, :], ps[:, 0:ATT_ROW], ALU.add), m)
            den = tiles(a_dst, g)
            t = V(lambda e: e.tensor_scalar(den, tiles(h_rows, g)[:, :, :, HEAD_DIM], 1e-16, None, ALU.add), t)
            t = V(lambda e: e.reciprocal(den, den), t)
            for j in g:
                t = V(lambda e, j=j: e.tensor_tensor(heads(spare[:, j, :]), h_rows[:, j, :, 0:HEAD_DIM],
                                                     a_dst[:, j, :].unsqueeze(2).broadcast_to([P, HEADS, HEAD_DIM]), ALU.mult), t if j == g[0] else None)
            y = tiles(spare, g)
            biased[g] = pr.op("pool", lambda e: e.tensor_tensor(
                y, y, brow[:, B_ATT:B_ATT + 1, :].broadcast_to([P, len(g), DIM]), ALU.add), t)

        def inner_stats(g):
            roots[g] = mean_and_root(lambda j: spare[:, j, :], g, biased[g])

        def inner_norm(g):
            r = V(lambda e: e.reciprocal(tiles(rstd, g), tiles(rstd, g)), roots[g])
            shift = V(lambda e: e.scalar_tensor_tensor(out=tiles(sq, g), in0=tiles(mv, g)[:, :, 0], scalar=-1.0,
                                                       in1=tiles(rstd, g), op0=ALU.mult, op1=ALU.mult), r)
            for j in g:
                t = A(lambda e, j=j: e.activation(spare[:, j, :], spare[:, j, :], ACT.Identity, bias=sq[:, j:j + 1],
                                                  scale=rstd[:, j:j + 1]), shift)
            y = tiles(spare, g)
            biased[g] = pr.op("pool", lambda e: e.tensor_tensor(
                y, y, brow[:, B_GAMMA:B_GAMMA + 1, :].broadcast_to([P, len(g), DIM]), ALU.mult), t)

        def inner_add(g):
            t = V(lambda e: e.tensor_tensor(tiles(x, g), tiles(x, g), tiles(spare, g), ALU.add), biased[g])
            roots[g] = mean_and_root(lambda j: x[:, j, :], g, t)

        def store(g):
            r = V(lambda e: e.reciprocal(tiles(rstd, g), tiles(rstd, g)), roots[g])
            shift = V(lambda e: e.scalar_tensor_tensor(out=tiles(sq, g), in0=tiles(mv, g)[:, :, 0], scalar=-1.0,
                                                       in1=tiles(rstd, g), op0=ALU.mult, op1=ALU.mult), r)
            for j in g:
                t = A(lambda e, j=j: e.activation(x[:, j, :], x[:, j, :], ACT.Identity, bias=sq[:, j:j + 1],
                                                  scale=rstd[:, j:j + 1]), shift)
            full = [j for j in g if tile_rows(j) == P]
            if full:
                pr.dma("sp", s_out, out[full[0] * P:(full[-1] + 1) * P, :].rearrange("(t p) d -> p t d", p=P),
                       tiles(x, full), t)
                stores[0] += 1
            if len(full) < len(g):
                pr.dma("sp", s_out, out[g[-1] * P:NODES, :], x[0:LAST_ROWS, g[-1], :], t)
                stores[0] += 1

        stores = [0]
        in_groups(attended, inner_stats, inner_norm, inner_add, store)
        pr.queue["sp"].append(lambda g: g.wait_ge(s_out, 16 * stores[0]))
        pr.queue["sp"].append(lambda g: g.wait_ge(s_tab, pr.count[s_tab.name]))

        block = stack.enter_context(nc.Block())
        pr.run(block)


def all_staged(pr, staged):
    toks = list(staged.values())
    done = pr.done["sp"]
    pr.count[done.name] = pr.count.get(done.name, 0) + 1

    def emit(eng):
        for s, v in toks:
            eng.wait_ge(s, v)
        eng.sem_inc(done, 1)

    pr.queue["sp"].append(emit)
    return done, pr.count[done.name]


def kernel(**inputs):
    import concourse.bacc as bacc
    from concourse.bass_utils import run_bass_kernel_spmd as run

    arr = {n: np.asarray(v) for n, v in inputs.items()}

    def tiled(v, fill):
        flat = np.full((PADDED_EDGES,), fill, v.dtype)
        flat[:EDGES] = v
        return np.ascontiguousarray(flat.reshape(EDGE_TILES, P).T)

    def t(v):
        return np.ascontiguousarray(np.swapaxes(v, -1, -2))

    x_rows = np.zeros((PADDED_NODES, DIM), arr["x"].dtype)
    x_rows[:NODES] = arr["x"]
    src_run, dst_run = (np.full((1, PADDED_EDGES + 1), PAD_NODE, arr[n].dtype) for n in ("src", "dst"))
    for run_of, n in ((src_run, "src"), (dst_run, "dst")):
        run_of[0, 0] = -1
        run_of[0, 1:EDGES + 1] = arr[n]
    data = {
        "x": x_rows,
        "src_t": tiled(arr["src"], PAD_NODE),
        "dst_t": tiled(arr["dst"], PAD_NODE),
        "w_t": tiled(arr["edge_weight"], 0),
        "src_run": src_run, "dst_run": dst_run,
        "w1l": t(arr["L0_gnn_W1l"]), "w1r": t(arr["L0_gnn_W1r"]),
        "w2l": t(arr["L0_gnn_W2l"]), "w2r": t(arr["L0_gnn_W2r"]),
        "b1": t(arr["L0_gnn_b1l"].reshape(K_HID, P)),
        "b2": arr["L0_gnn_b2l"].reshape(1, DIM),
        "wn": t(arr["L1_gnn_Wn"]), "ws": t(arr["L1_gnn_Ws"]),
        "bn": arr["L1_gnn_bn"], "bs": arr["L1_gnn_bs"],
        "l2w1": arr["L2_gnn_W1"], "l2w2": arr["L2_gnn_W2"], "l2b": arr["L2_gnn_b"].reshape(1, DIM),
        "l3w": arr["L3_gnn_W"],
        "att_src": t(arr["L3_gnn_att_src"].reshape(K_IN, P)), "att_dst": t(arr["L3_gnn_att_dst"].reshape(K_IN, P)),
        "l3bias": arr["L3_gnn_bias"].reshape(1, DIM),
        "gamma": arr["L3_gnn_ln_gamma"].reshape(1, DIM), "beta": arr["L3_gnn_ln_beta"].reshape(1, DIM),
    }
    nc = bacc.Bacc("TRN2", target_bir_lowering=False, num_devices=1)
    aps = {n: nc.dram_tensor(n, v.shape, mybir.dt.from_np(v.dtype), kind="ExternalInput").ap()
           for n, v in data.items()}
    out = nc.dram_tensor("out", (NODES, DIM), F32, kind="ExternalOutput").ap()
    residual_gnn(nc, aps, out)
    r = run(nc, [data], core_ids=[0])
    return r.results[0]["out"]
```
